# Optimizing a Trainium2 kernel written in Bass

```python
import numpy as np
import jax
import jax.numpy as jnp

def _softmax(x, axis=-1):
    return jax.nn.softmax(x, axis=axis)

def _gelu(x):
    return jax.nn.gelu(x, approximate=True)

def _silu(x):
    return jax.nn.silu(x)

def _sigmoid(x):
    return jax.nn.sigmoid(x)

def _layernorm(x, axis=-1, eps=1e-05):
    m = jnp.mean(x, axis=axis, keepdims=True)
    v = jnp.var(x, axis=axis, keepdims=True)
    return (x - m) / jnp.sqrt(v + eps)

def _scatter_add(tgt, idx, src, axis=0):
    return tgt.at[idx].add(src)

def _segment_sum(src, seg, n):
    return jax.ops.segment_sum(src, seg, n)
kernel_name = 'mk_seq_postln_d2_jaxref_r8_6ba805'

def setup_inputs(seed: int=0):
    np.random.seed(seed)
    _w = jnp.asarray

    def _L0_attn_setup():
        import jax, jax.numpy as jnp
        import numpy as np
        B, T, E, H = (8, 256, 128, 128)
        _LN_EPS = 0.001

        def _ln(x, g, b):
            mu = jnp.mean(x, axis=-1, keepdims=True)
            var = jnp.var(x, axis=-1, keepdims=True)
            return (x - mu) * jax.lax.rsqrt(var + _LN_EPS) * g + b

        def _time_shift(x):
            return jnp.pad(x[:, :-1], ((0, 0), (1, 0), (0, 0)))

        def _wkv(k, v, w, u):
            Bk, Tk, Hk = k.shape

            def step(carry, kv_t):
                aa, bb, pp = carry
                kt, vt = kv_t
                ww = u + kt
                q = jnp.maximum(pp, ww)
                e1 = jnp.exp(pp - q)
                e2 = jnp.exp(ww - q)
                out = (e1 * aa + e2 * vt) / (e1 * bb + e2)
                ww2 = pp + w
                q2 = jnp.maximum(ww2, kt)
                e1b = jnp.exp(ww2 - q2)
                e2b = jnp.exp(kt - q2)
                return ((e1b * aa + e2b * vt, e1b * bb + e2b, q2), out)
            init = (jnp.zeros((Bk, Hk), k.dtype), jnp.zeros((Bk, Hk), k.dtype), jnp.full((Bk, Hk), -1e+38, k.dtype))
            kT = jnp.swapaxes(k, 0, 1)
            vT = jnp.swapaxes(v, 0, 1)
            _, outs = jax.lax.scan(step, init, (kT, vT))
            return jnp.swapaxes(outs, 0, 1)
        key = jax.random.key(seed)
        ks = jax.random.split(key, 20)

        def glorot(k, shape):
            lim = np.sqrt(6.0 / (shape[0] + shape[1]))
            return jax.random.uniform(k, shape, jnp.float32, -lim, lim)
        return {'inputs': jax.random.normal(ks[0], (B, T, E), jnp.float32), 'ln1_g': jnp.ones((E,), jnp.float32), 'ln1_b': jnp.zeros((E,), jnp.float32), 'ln2_g': jnp.ones((E,), jnp.float32), 'ln2_b': jnp.zeros((E,), jnp.float32), 'tm_mix_k': jax.random.uniform(ks[1], (E,), jnp.float32, 0.0, 2.0 / E), 'tm_mix_v': jax.random.uniform(ks[2], (E,), jnp.float32, 0.0, 2.0 / E), 'tm_mix_r': jax.random.uniform(ks[3], (E,), jnp.float32, 0.0, (2.0 / E) ** 0.5), 'tm_Wk': glorot(ks[4], (E, H)), 'tm_Wv': glorot(ks[5], (E, H)), 'tm_Wr': glorot(ks[6], (E, H)), 'time_decay': jax.random.uniform(ks[7], (H,), jnp.float32, 0.0, 0.5), 'time_first': jax.random.uniform(ks[8], (H,), jnp.float32, 0.0, 0.05), 'Wo': glorot(ks[9], (H, E)), 'cm_mix_k': jax.random.uniform(ks[10], (E,), jnp.float32, 0.0, 2.0 / E), 'cm_mix_r': jax.random.uniform(ks[11], (E,), jnp.float32, 0.0, 2.0 / E), 'cm_Wk': glorot(ks[12], (E, 4 * H)), 'cm_Wv': glorot(ks[13], (4 * H, E)), 'cm_Wr': glorot(ks[14], (E, E))}
    _L0_attn_in = _L0_attn_setup()

    def _L0_ffn_setup():
        import jax, jax.numpy as jnp
        import numpy as np
        DIM = 128
        HIDDEN = 512
        E = 8
        B, S = (2, 512)
        key = jax.random.key(seed)
        ks = jax.random.split(key, 8)
        sd = 1.0 / np.sqrt(DIM)
        sh = 1.0 / np.sqrt(HIDDEN)
        return {'x': jax.random.normal(ks[0], (B, S, DIM), dtype=jnp.float32), 'router_w': jax.random.uniform(ks[1], (DIM, E), jnp.float32, -sd, sd), 'router_b': jax.random.uniform(ks[2], (E,), jnp.float32, -sd, sd), 'w1': jax.random.uniform(ks[3], (E, DIM, 2 * HIDDEN), jnp.float32, -sd, sd), 'b1': jax.random.uniform(ks[4], (E, 2 * HIDDEN), jnp.float32, -sd, sd), 'w2': jax.random.uniform(ks[5], (E, HIDDEN, DIM), jnp.float32, -sh, sh), 'b2': jax.random.uniform(ks[6], (E, DIM), jnp.float32, -sh, sh)}
    _L0_ffn_in = _L0_ffn_setup()

    def _L1_attn_setup():
        import jax, jax.numpy as jnp
        import numpy as np
        DIM = 128
        HEADS = 16
        DHEAD = DIM // HEADS
        EPS_NORM = 1e-06
        EPS_DEN = 1e-06

        def rmsnorm(x, w):
            xf = x.astype(jnp.float32)
            return (w * xf * jax.lax.rsqrt(jnp.mean(xf * xf, axis=-1, keepdims=True) + EPS_NORM)).astype(x.dtype)
        key = jax.random.key(seed)
        ks = jax.random.split(key, 6)
        b, n = (4, 512)
        x = jax.random.normal(ks[0], (b, n, DIM), dtype=jnp.float32)
        W_qkv = jax.random.normal(ks[1], (DIM, 3 * DIM), dtype=jnp.float32) * DIM ** (-0.5)
        qn_w = jnp.ones((DIM,), dtype=jnp.float32)
        kn_w = jnp.ones((DIM,), dtype=jnp.float32)
        W_out = jax.random.normal(ks[2], (DIM, DIM), dtype=jnp.float32) * DIM ** (-0.5)
        b_out = jnp.zeros((DIM,), dtype=jnp.float32)
        return {'x': x, 'W_qkv': W_qkv, 'qn_w': qn_w, 'kn_w': kn_w, 'W_out': W_out, 'b_out': b_out}
    _L1_attn_in = _L1_attn_setup()

    def _L1_ffn_setup():
        import jax, jax.numpy as jnp
        import numpy as np
        EPS = 1e-12

        def rms_norm(t, gamma):
            n = jnp.maximum(jnp.linalg.norm(t, axis=-1, keepdims=True), EPS)
            scale = jnp.sqrt(jnp.asarray(t.shape[-1], t.dtype))
            return t / n * scale * gamma
        key = jax.random.key(seed)
        ks = jax.random.split(key, 4)
        b, s, d = (4, 512, 128)
        e, t = (8, 64)
        hidden = 4 * d
        return {'x': jax.random.normal(ks[0], (b, s, d), dtype=jnp.float32), 'gamma_x': jnp.ones((d,), dtype=jnp.float32), 'gamma_slot': jnp.ones((d,), dtype=jnp.float32), 'slot_embeds': jax.random.normal(ks[1], (e, t, d), dtype=jnp.float32), 'w1': jax.random.normal(ks[2], (d, hidden), dtype=jnp.float32) * (1.0 / np.sqrt(d)), 'w2': jax.random.normal(ks[3], (hidden, d), dtype=jnp.float32) * (1.0 / np.sqrt(hidden))}
    _L1_ffn_in = _L1_ffn_setup()
    _d = {'L0_attn_inputs': _L0_attn_in['inputs'], 'L0_attn_ln1_g': _L0_attn_in['ln1_g'], 'L0_attn_ln1_b': _L0_attn_in['ln1_b'], 'L0_attn_ln2_g': _L0_attn_in['ln2_g'], 'L0_attn_ln2_b': _L0_attn_in['ln2_b'], 'L0_attn_tm_mix_k': _L0_attn_in['tm_mix_k'], 'L0_attn_tm_mix_v': _L0_attn_in['tm_mix_v'], 'L0_attn_tm_mix_r': _L0_attn_in['tm_mix_r'], 'L0_attn_tm_Wk': _L0_attn_in['tm_Wk'], 'L0_attn_tm_Wv': _L0_attn_in['tm_Wv'], 'L0_attn_tm_Wr': _L0_attn_in['tm_Wr'], 'L0_attn_time_decay': _L0_attn_in['time_decay'], 'L0_attn_time_first': _L0_attn_in['time_first'], 'L0_attn_Wo': _L0_attn_in['Wo'], 'L0_attn_cm_mix_k': _L0_attn_in['cm_mix_k'], 'L0_attn_cm_mix_r': _L0_attn_in['cm_mix_r'], 'L0_attn_cm_Wk': _L0_attn_in['cm_Wk'], 'L0_attn_cm_Wv': _L0_attn_in['cm_Wv'], 'L0_attn_cm_Wr': _L0_attn_in['cm_Wr'], 'L0_ffn_router_w': _L0_ffn_in['router_w'], 'L0_ffn_router_b': _L0_ffn_in['router_b'], 'L0_ffn_w1': _L0_ffn_in['w1'], 'L0_ffn_b1': _L0_ffn_in['b1'], 'L0_ffn_w2': _L0_ffn_in['w2'], 'L0_ffn_b2': _L0_ffn_in['b2'], 'L1_attn_W_qkv': _L1_attn_in['W_qkv'], 'L1_attn_qn_w': _L1_attn_in['qn_w'], 'L1_attn_kn_w': _L1_attn_in['kn_w'], 'L1_attn_W_out': _L1_attn_in['W_out'], 'L1_attn_b_out': _L1_attn_in['b_out'], 'L1_ffn_gamma_x': _L1_ffn_in['gamma_x'], 'L1_ffn_gamma_slot': _L1_ffn_in['gamma_slot'], 'L1_ffn_slot_embeds': _L1_ffn_in['slot_embeds'], 'L1_ffn_w1': _L1_ffn_in['w1'], 'L1_ffn_w2': _L1_ffn_in['w2']}
    _x0 = _d['L0_attn_inputs']
    _d['L0_attn_inputs'] = jax.random.normal(jax.random.fold_in(jax.random.key(seed), 1), (16, 256, 128), dtype=_x0.dtype)
    del _x0
    return _d

def reference(L0_attn_inputs, L0_attn_ln1_g, L0_attn_ln1_b, L0_attn_ln2_g, L0_attn_ln2_b, L0_attn_tm_mix_k, L0_attn_tm_mix_v, L0_attn_tm_mix_r, L0_attn_tm_Wk, L0_attn_tm_Wv, L0_attn_tm_Wr, L0_attn_time_decay, L0_attn_time_first, L0_attn_Wo, L0_attn_cm_mix_k, L0_attn_cm_mix_r, L0_attn_cm_Wk, L0_attn_cm_Wv, L0_attn_cm_Wr, L0_ffn_router_w, L0_ffn_router_b, L0_ffn_w1, L0_ffn_b1, L0_ffn_w2, L0_ffn_b2, L1_attn_W_qkv, L1_attn_qn_w, L1_attn_kn_w, L1_attn_W_out, L1_attn_b_out, L1_ffn_gamma_x, L1_ffn_gamma_slot, L1_ffn_slot_embeds, L1_ffn_w1, L1_ffn_w2):

    def _L0_attn_ref(inputs, ln1_g, ln1_b, ln2_g, ln2_b, tm_mix_k, tm_mix_v, tm_mix_r, tm_Wk, tm_Wv, tm_Wr, time_decay, time_first, Wo, cm_mix_k, cm_mix_r, cm_Wk, cm_Wv, cm_Wr):
        import jax, jax.numpy as jnp
        import numpy as np
        B, T, E, H = (8, 256, 128, 128)
        _LN_EPS = 0.001

        def _ln(x, g, b):
            mu = jnp.mean(x, axis=-1, keepdims=True)
            var = jnp.var(x, axis=-1, keepdims=True)
            return (x - mu) * jax.lax.rsqrt(var + _LN_EPS) * g + b

        def _time_shift(x):
            return jnp.pad(x[:, :-1], ((0, 0), (1, 0), (0, 0)))

        def _wkv(k, v, w, u):
            Bk, Tk, Hk = k.shape

            def step(carry, kv_t):
                aa, bb, pp = carry
                kt, vt = kv_t
                ww = u + kt
                q = jnp.maximum(pp, ww)
                e1 = jnp.exp(pp - q)
                e2 = jnp.exp(ww - q)
                out = (e1 * aa + e2 * vt) / (e1 * bb + e2)
                ww2 = pp + w
                q2 = jnp.maximum(ww2, kt)
                e1b = jnp.exp(ww2 - q2)
                e2b = jnp.exp(kt - q2)
                return ((e1b * aa + e2b * vt, e1b * bb + e2b, q2), out)
            init = (jnp.zeros((Bk, Hk), k.dtype), jnp.zeros((Bk, Hk), k.dtype), jnp.full((Bk, Hk), -1e+38, k.dtype))
            kT = jnp.swapaxes(k, 0, 1)
            vT = jnp.swapaxes(v, 0, 1)
            _, outs = jax.lax.scan(step, init, (kT, vT))
            return jnp.swapaxes(outs, 0, 1)
        x = inputs
        h = _ln(x, ln1_g, ln1_b)
        h1 = _time_shift(h)
        xk = h * tm_mix_k + h1 * (1.0 - tm_mix_k)
        xv = h * tm_mix_v + h1 * (1.0 - tm_mix_v)
        xr = h * tm_mix_r + h1 * (1.0 - tm_mix_r)
        k = xk @ tm_Wk
        v = xv @ tm_Wv
        r = xr @ tm_Wr
        wkv = _wkv(k, v, -jnp.exp(time_decay), time_first)
        x = x + jax.nn.sigmoid(r) * wkv @ Wo
        h = _ln(x, ln2_g, ln2_b)
        h1 = _time_shift(h)
        xk = h * cm_mix_k + h1 * (1.0 - cm_mix_k)
        xr = h * cm_mix_r + h1 * (1.0 - cm_mix_r)
        kc = jnp.square(jax.nn.relu(xk @ cm_Wk))
        rc = jax.nn.sigmoid(xr @ cm_Wr)
        x = x + rc * (kc @ cm_Wv)
        return x

    def _L0_ffn_ref(x, router_w, router_b, w1, b1, w2, b2):
        import jax, jax.numpy as jnp
        import numpy as np
        DIM = 128
        HIDDEN = 512
        E = 8
        B, S = (2, 512)
        logits = jnp.einsum('bsd,de->bse', x, router_w) + router_b
        probs = jax.nn.softmax(logits, axis=-1)
        top1 = jnp.argmax(probs, axis=-1)
        out = jnp.zeros_like(x)
        for i in range(E):
            h = jnp.einsum('bsd,df->bsf', x, w1[i]) + b1[i]
            a, g = jnp.split(h, 2, axis=-1)
            y = jnp.einsum('bsh,hd->bsd', a * jax.nn.sigmoid(g), w2[i]) + b2[i]
            out = out + jnp.where((top1 == i)[..., None], y, 0.0)
        return out

    def _L1_attn_ref(x, W_qkv, qn_w, kn_w, W_out, b_out):
        import jax, jax.numpy as jnp
        import numpy as np
        DIM = 128
        HEADS = 16
        DHEAD = DIM // HEADS
        EPS_NORM = 1e-06
        EPS_DEN = 1e-06

        def rmsnorm(x, w):
            xf = x.astype(jnp.float32)
            return (w * xf * jax.lax.rsqrt(jnp.mean(xf * xf, axis=-1, keepdims=True) + EPS_NORM)).astype(x.dtype)
        b, n, _ = x.shape
        qkv = x @ W_qkv
        q, k, v = jnp.split(qkv, 3, axis=-1)
        q = rmsnorm(q, qn_w)
        k = rmsnorm(k, kn_w)

        def split_heads(t):
            return t.reshape(b, n, HEADS, DHEAD).transpose(0, 2, 1, 3)
        q, k, v = map(split_heads, (q, k, v))
        q = jax.nn.relu(q).astype(jnp.float32)
        k = jax.nn.relu(k).astype(jnp.float32)
        v = v.astype(jnp.float32)
        kv = jnp.einsum('bhnd,bhne->bhde', k, v)
        out = jnp.einsum('bhnd,bhde->bhne', q, kv)
        k_sum = k.sum(axis=2)
        normalizer = jnp.einsum('bhnd,bhd->bhn', q, k_sum) + EPS_DEN
        out = out / normalizer[..., None]
        out = out.transpose(0, 2, 1, 3).reshape(b, n, DIM)
        return out @ W_out + b_out

    def _L1_ffn_ref(x, gamma_x, gamma_slot, slot_embeds, w1, w2):
        import jax, jax.numpy as jnp
        import numpy as np
        EPS = 1e-12

        def rms_norm(t, gamma):
            n = jnp.maximum(jnp.linalg.norm(t, axis=-1, keepdims=True), EPS)
            scale = jnp.sqrt(jnp.asarray(t.shape[-1], t.dtype))
            return t / n * scale * gamma
        b, s, d = x.shape
        e, t, _ = slot_embeds.shape
        xn = rms_norm(x, gamma_x)
        se = rms_norm(slot_embeds, gamma_slot)
        logits = jnp.einsum('bsd,etd->bset', xn, se)
        dispatch = jax.nn.softmax(logits, axis=1)
        slots = jnp.einsum('bsd,bset->betd', xn, dispatch)
        h = jax.nn.gelu(slots @ w1, approximate=False)
        processed = h @ w2
        combine = jax.nn.softmax(logits.reshape(b, s, e * t), axis=-1)
        out = jnp.einsum('bnd,bsn->bsd', processed.reshape(b, e * t, d), combine)
        return out
    x = L0_attn_inputs
    x = _layernorm(x + _L0_attn_ref(x, L0_attn_ln1_g, L0_attn_ln1_b, L0_attn_ln2_g, L0_attn_ln2_b, L0_attn_tm_mix_k, L0_attn_tm_mix_v, L0_attn_tm_mix_r, L0_attn_tm_Wk, L0_attn_tm_Wv, L0_attn_tm_Wr, L0_attn_time_decay, L0_attn_time_first, L0_attn_Wo, L0_attn_cm_mix_k, L0_attn_cm_mix_r, L0_attn_cm_Wk, L0_attn_cm_Wv, L0_attn_cm_Wr), axis=-1)
    x = _layernorm(x + _L0_ffn_ref(x, L0_ffn_router_w, L0_ffn_router_b, L0_ffn_w1, L0_ffn_b1, L0_ffn_w2, L0_ffn_b2), axis=-1)
    x = _layernorm(x + _L1_attn_ref(x, L1_attn_W_qkv, L1_attn_qn_w, L1_attn_kn_w, L1_attn_W_out, L1_attn_b_out), axis=-1)
    x = _layernorm(x + _L1_ffn_ref(x, L1_ffn_gamma_x, L1_ffn_gamma_slot, L1_ffn_slot_embeds, L1_ffn_w1, L1_ffn_w2), axis=-1)
    return x

_drawn_inputs = setup_inputs


def setup_inputs(seed=0):
    import zlib

    import numpy as np

    out = dict(_drawn_inputs(seed))
    spreads = {'L0_attn_ln1_g': (1.0, 0.2),
     'L0_attn_ln1_b': (0.0, 0.1),
     'L0_attn_ln2_g': (1.0, 0.2),
     'L0_attn_ln2_b': (0.0, 0.1),
     'L1_attn_qn_w': (1.0, 0.6),
     'L1_attn_kn_w': (1.0, 0.6),
     'L1_attn_b_out': (0.0, 0.1),
     'L1_ffn_gamma_x': (1.0, 0.2),
     'L1_ffn_gamma_slot': (1.0, 0.2)}
    factors = {'L0_attn_tm_mix_k': 6.481,
     'L0_attn_tm_mix_v': 4.555,
     'L0_attn_time_first': 6.465,
     'L0_attn_cm_mix_k': 4.897,
     'L0_attn_cm_mix_r': 6.474}
    for name, (base, spread) in spreads.items():
        noise = np.random.default_rng([zlib.crc32(name.encode()), seed]).standard_normal(out[name].shape)
        drawn = base * np.exp(spread * noise) if base else spread * noise
        out[name] = jnp.asarray(drawn.astype(out[name].dtype))
    for name, factor in factors.items():
        out[name] = (out[name] * factor).astype(out[name].dtype)
    return out
```

```python
from contextlib import ExitStack

import concourse.bass as bass
from concourse import mybir

ALU = mybir.AluOpType
ACT = mybir.ActivationFunctionType
F32 = mybir.dt.float32
BF16 = mybir.dt.bfloat16
I32 = mybir.dt.int32
AX = mybir.AxisListType.X

P = 128
U = 2

C_IDENT, C_UPPER, C_BLOCK, C_HEADS = 0, 128, 256, 384
C_FIRST, C_TILE, C_COUNT, C_RESET, C_DIAG, C_END = 400, 408, 448, 480, 736, 752
(V_G1, V_B1, V_G2, V_B2, V_MK, V_MV, V_MR, V_CK, V_CR, V_DECAY, V_FIRST, V_QN, V_N) = range(13)
R_KN, R_BOUT, R_GX, R_GS, R_N = range(5)


class Chain:

    def __init__(self, eng, sem, turn=0, per_turn=0):
        self.eng, self.sem, self.turn, self.per_turn, self.n = eng, sem, turn, per_turn, 0

    def step(self, ins):
        ins.then_inc(self.sem, 1)
        self.n += 1
        return self.n

    def wait(self, n=None):
        n = self.n if n is None else n
        self.eng.wait_ge(self.sem, self.turn * self.per_turn + n if self.per_turn else n)

    def close(self):
        assert self.n == self.per_turn, f"per_turn should be {self.n}"


def settle(eng, sem, value, passed):
    eng.wait_ge(sem, value)
    eng.sem_inc(passed, 1)


def two_layer_kernel(nc, x_in, vecs_in, rows_in, consts_in, w, out):
    SEQ, T, D = x_in.shape
    NT = T // P
    TILES = SEQ * NT
    TURNS = SEQ // U
    HID = w["cm_Wk"].shape[1]
    HC = HID // P
    E, _, GLU = w["w1"].shape
    XH = GLU // 2
    XC = XH // P
    XTILES = U * -(-(TILES + E - 1) // U)
    HEADS = C_FIRST - C_HEADS
    DH = D // HEADS
    SLOTS = w["slots"].shape[0]
    SC = SLOTS // P
    N129 = D + 1

    x_rows = x_in.rearrange("s (j p) d -> s p j d", p=P)
    out_rows = out.rearrange("s (j p) d -> s p j d", p=P)
    sorted_x = nc.dram_tensor("sorted_x", [XTILES * P, D], F32, kind="Internal").ap()
    sorted_y = nc.dram_tensor("sorted_y", [XTILES * P, D], F32, kind="Internal").ap()
    bias_parts = nc.dram_tensor("bias_parts", [3, E, GLU + D], BF16, kind="Internal").ap()

    ctx = ExitStack()
    with ctx:
        rwkv_sems = ExitStack()
        used_semaphores = []

        def sem(name, scope=ctx):
            made = scope.enter_context(nc.semaphore(name))
            if scope is rwkv_sems:
                used_semaphores.append(made)
            return made

        def pair(name, scope=ctx):
            return [sem(f"{name}{u}", scope) for u in range(U)]

        def sb(name, shape, dt=F32, scope=ctx):
            return scope.enter_context(nc.sbuf_tensor(name, shape, dt))

        banks = ctx.enter_context(nc.psum_tensor("banks", [P, 8, 512], F32))

        def bank(u, k, lo=0, hi=512):
            return banks[:, 4 * u + k, lo:hi]

        consts = sb("consts", [P, C_END])
        vecs = sb("vecs", [P, V_N])
        rows = sb("rows", [P, R_N, D])
        router_b = sb("router_b", [P, E])
        ident = consts[:, C_IDENT:C_IDENT + P]
        ones_bf = sb("ones_bf", [P, P], BF16)
        eps = sb("eps", [P, 3, NT])
        EPS_LN, EPS_TM, EPS_RMS = 0, 1, 2
        neg_half = sb("neg_half", [P, 4])
        zeros = sb("zeros", [P, D])
        w1 = sb("w1", [P, E, GLU])
        w2 = sb("w2", [P, E, XC, D])
        biases = sb("biases", [3, E, GLU + D], BF16)
        xa = sb("xa", [P, TILES, D])
        logits = sb("logits", [P, TILES, E])
        slot_of = sb("slot_of", [P, TILES], I32)
        tile_expert = sb("tile_expert", [P, XTILES], I32)

        consts_in_sem = sem("consts_loaded")
        rows_in_sem = sem("rows_loaded")
        rwkv_w_sem = sem("rwkv_weights_loaded")
        expert_w_sem = sem("expert_weights_loaded")
        layer1_w_sem = sem("layer1_weights_loaded")
        zeroed_sem = sem("sorted_x_zeroed")
        vec_passed = sem("vec_passed")
        pool_passed = sem("pool_passed")
        parts_sem = sem("bias_parts_stored")
        biases_sem = sem("biases_loaded")
        scattered = sem("rows_scattered")
        y_stored = pair("expert_rows_stored")

        layer0 = ExitStack()
        prep = ExitStack()

        def vec(k):
            return vecs[:, k:k + 1]

        mixed = {n: (sb(f"{n}_now", [P, c], scope=layer0), sb(f"{n}_before", [P, c], scope=layer0))
                 for n, c in (("tm_Wk", D), ("tm_Wv", D), ("tm_Wr", D), ("cm_Wk", HID), ("cm_Wr", D))}
        mix_of = {"tm_Wk": V_MK, "tm_Wv": V_MV, "tm_Wr": V_MR, "cm_Wk": V_CK, "cm_Wr": V_CR}
        wo = sb("wo", [P, D], scope=layer0)
        cm_wv = sb("cm_wv", [P, HC, D], scope=layer0)
        router_w = sb("router_w", [P, E], scope=layer0)
        decay = sb("decay", [P, 2], scope=layer0)
        NEG_W, U_PLUS_W = decay[:, 0:1], decay[:, 1:2]

        raw_b = sb("raw_b", [E, GLU + D], scope=prep)
        rest_b = sb("rest_b", [E, GLU + D], scope=prep)
        part_b = sb("part_b", [E, 3, GLU + D], BF16, scope=prep)
        exp_decay = sb("exp_decay", [P, 1], scope=prep)

        zero_made = sem("zero_made", rwkv_sems)
        ones_made = sem("ones_made", rwkv_sems)
        vec_prep = sem("vec_prep", rwkv_sems)
        decay_exp = sem("decay_exp", rwkv_sems)
        parts_made = sem("bias_parts_made", rwkv_sems)

        with nc.Block() as block:

            @block.sync
            def _(sp):
                sp.dma_start(consts[:, :], consts_in).then_inc(consts_in_sem, 16)
                sp.dma_start(vecs[:, :], vecs_in).then_inc(consts_in_sem, 16)
                for n in mixed:
                    sp.dma_start(mixed[n][1][:, :], w[n]).then_inc(rwkv_w_sem, 16)
                sp.dma_start(wo[:, :], w["Wo"]).then_inc(rwkv_w_sem, 16)
                sp.dma_start(cm_wv[:, :, :], w["cm_Wv"].rearrange("(c p) d -> p c d", p=P)).then_inc(rwkv_w_sem, 16)
                sp.dma_start(router_w[:, :], w["router_w"]).then_inc(rwkv_w_sem, 16)
                sp.dma_start(raw_b[:, 0:GLU], w["b1"]).then_inc(consts_in_sem, 16)
                sp.dma_start(raw_b[:, GLU:GLU + D], w["b2"]).then_inc(consts_in_sem, 16)

            @block.scalar
            def _(act):
                act.wait_ge(consts_in_sem, 64)
                act.activation(exp_decay[:, :], vec(V_DECAY), ACT.Exp).then_inc(decay_exp, 1)
                act.dma_start(rows[:, :, :], rows_in.partition_broadcast(P)).then_inc(rows_in_sem, 16)
                act.dma_start(router_b[:, :], w["router_b"].partition_broadcast(P)).then_inc(rows_in_sem, 16)
                act.wait_ge(zero_made, 1)
                act.dma_start(sorted_x.rearrange("(t p) d -> p t d", p=P),
                              zeros[:, :].unsqueeze(1).to_broadcast([P, XTILES, D])).then_inc(zeroed_sem, 16)
                act.dma_start(w1[:, :, :], w["w1"].rearrange("e p f -> p e f")).then_inc(expert_w_sem, 16)
                act.dma_start(w2[:, :, :, :], w["w2"].rearrange("e (c p) d -> p e c d", p=P)).then_inc(expert_w_sem, 16)
                act.wait_ge(parts_made, 3)
                for k in range(3):
                    act.dma_start(bias_parts[k], part_b[:, k, :]).then_inc(parts_sem, 16)
                act.wait_ge(parts_sem, 48)
                act.dma_start(biases[:, :, :], bias_parts).then_inc(biases_sem, 16)

            @block.gpsimd
            def _(pool):
                pool.memset(zeros[:, :], 0.0).then_inc(zero_made, 1)
                pool.memset(ones_bf[:, :], 1.0).then_inc(ones_made, 1)
                pool.memset(eps[:, EPS_LN, :], 1e-5).then_inc(ones_made, 1)
                pool.memset(eps[:, EPS_TM, :], 1e-3).then_inc(ones_made, 1)
                pool.memset(eps[:, EPS_RMS, :], 1e-6).then_inc(ones_made, 1)
                pool.memset(neg_half[:, :], -0.5).then_inc(ones_made, 1)

            @block.vector
            def _(dve):
                c = Chain(dve, vec_prep)
                dve.wait_ge(consts_in_sem, 64)
                dve.wait_ge(decay_exp, 1)
                c.step(dve.tensor_scalar(NEG_W, exp_decay[:, :], -1.0, None, ALU.mult))
                c.wait()
                c.step(dve.tensor_tensor(U_PLUS_W, NEG_W, vec(V_FIRST), ALU.add))
                dve.wait_ge(rwkv_w_sem, 16 * 8)
                for n, (now, before) in mixed.items():
                    k = c.step(dve.tensor_scalar(now[:, :], before[:, :], vec(mix_of[n]), None, ALU.mult))
                    c.wait(k)
                    c.step(dve.tensor_tensor(before[:, :], before[:, :], now[:, :], ALU.subtract))
                source = raw_b
                for k in range(3):
                    dve.tensor_copy(part_b[:, k, :], source[:, :]).then_inc(parts_made, 1)
                    if k < 2:
                        dve.wait_ge(parts_made, k + 1)
                        c.step(dve.tensor_tensor(rest_b[:, :], source[:, :], part_b[:, k, :], ALU.subtract))
                        c.wait()
                        source = rest_b

        prep.close()

        rw = ExitStack()

        def bufs(name, shape, dt=F32, scope=rw):
            return [sb(f"{name}{u}", shape, dt, scope) for u in range(U)]

        x0 = bufs("x0", [P, NT, D])
        moments = bufs("moments", [P, NT, 6])
        mean_var = bufs("mean_var", [P, NT, 2])
        rstd = bufs("rstd", [P, NT])
        normed = bufs("normed", [P, NT, D])
        h_cols = bufs("h_cols", [P, T + 1])
        peak = bufs("peak", [P, T + 1])
        delta = bufs("delta", [P, T])
        above = bufs("above", [P, 2, T])
        below = bufs("below", [P, 2, T])
        keep = bufs("keep", [P, 2, T])
        take = bufs("take", [P, 2, T])
        state = bufs("state", [P, 2, T + 1])
        value = bufs("value", [P, T])
        taken = bufs("taken", [P, T])
        frac = bufs("frac", [P, 2, T])
        recip = bufs("recip", [P, T])
        r_tanh = bufs("r_tanh", [P, T])
        y_cols = bufs("y_cols", [P, T])
        x1 = bufs("x1", [P, NT, D])
        x01 = bufs("x01", [P, NT, D])
        k_relu = bufs("k_relu", [P, HC, T])
        k_sq = bufs("k_sq", [P, HC, T])
        rc_tanh = bufs("rc_tanh", [P, NT, D])
        gated = bufs("gated", [P, NT, D])
        xa_cols = bufs("xa_cols", [P, T])

        x_loaded = pair("x_loaded", rwkv_sems)
        x_free = pair("x_free", rwkv_sems)
        var_ready = pair("var_ready", rwkv_sems)
        rstd_ready = pair("rstd_ready", rwkv_sems)
        normed_ready = pair("normed_ready", rwkv_sems)
        turned = pair("turned", rwkv_sems)
        h_ready = pair("h_ready", rwkv_sems)
        kv_ready = pair("kv_ready", rwkv_sems)
        r_ready = pair("r_ready", rwkv_sems)
        r_done = pair("r_done", rwkv_sems)
        args_ready = pair("args_ready", rwkv_sems)
        exps_ready = pair("exps_ready", rwkv_sems)
        y_ready = pair("y_ready", rwkv_sems)
        wo_ready = pair("wo_ready", rwkv_sems)
        x1_ready = pair("x1_ready", rwkv_sems)
        x01_ready = pair("x01_ready", rwkv_sems)
        kc_ready = pair("kc_ready", rwkv_sems)
        relu_ready = pair("relu_ready", rwkv_sems)
        sq_ready = pair("sq_ready", rwkv_sems)
        rc_ready = pair("rc_ready", rwkv_sems)
        rc_done = pair("rc_done", rwkv_sems)
        cv_ready = pair("cv_ready", rwkv_sems)
        xa_ready = pair("xa_ready", rwkv_sems)
        xa_turned = pair("xa_turned", rwkv_sems)
        xa_cols_ready = pair("xa_cols_ready", rwkv_sems)
        logits_ready = pair("logits_ready", rwkv_sems)
        logits_saved = pair("logits_saved", rwkv_sems)
        borders_set = sem("borders_set", rwkv_sems)
        vec_rwkv = sem("vec_rwkv", rwkv_sems)
        pool_rwkv = sem("pool_rwkv", rwkv_sems)

        def keys(u, c):
            return bank(u, 1 + c // 2, (c % 2) * T, (c % 2 + 1) * T)

        def stats(dve, c, i, src, u):
            for j in range(NT):
                c.step(dve.bn_stats(moments[u][:, j, :], src[j]))
            settle(dve, c.sem, i * c.per_turn + c.n, vec_passed)
            for j in range(NT):
                dve.bn_aggr(mean_var[u][:, j, :], moments[u][:, j, :]).then_inc(var_ready[u], 1)

        with nc.Block() as block:

            @block.sync
            def _(sp):
                with sp.Fori(0, TURNS) as i:
                    for u in range(U):
                        sp.wait_ge(x_free[u], i + 1)
                        sp.dma_start(x0[u][:, :, :], x_rows[bass.ds(i * U + u, 1)].squeeze(0)
                                     ).then_inc(x_loaded[u], 16)

            @block.tensor
            def _(pe):
                def turn(u, src, done):
                    for j in range(NT):
                        last = pe.transpose(bank(u, 0, j * P, (j + 1) * P), src[:, j, :], ident)
                    last.then_inc(done[u], 1)

                def mixed_columns(u, dst, name, lo, hi):
                    now, before = mixed[name]
                    pe.matmul(dst, now[:, lo:hi], h_cols[u][:, 1:T + 1], start=True, stop=False)
                    return pe.matmul(dst, before[:, lo:hi], h_cols[u][:, 0:T], start=False, stop=True)

                with pe.Fori(0, TURNS) as i:
                    for u in range(U):
                        pe.wait_ge(normed_ready[u], i * 4 + 2)
                        turn(u, normed[u], turned)
                    for u in range(U):
                        pe.wait_ge(h_ready[u], i * 2 + 1)
                        mixed_columns(u, bank(u, 1, 0, T), "tm_Wk", 0, D)
                        mixed_columns(u, bank(u, 1, T, 2 * T), "tm_Wv", 0, D).then_inc(kv_ready[u], 1)
                        mixed_columns(u, bank(u, 2, 0, T), "tm_Wr", 0, D).then_inc(r_ready[u], 1)
                    for u in range(U):
                        pe.wait_ge(y_ready[u], i + 1)
                        for j in range(NT):
                            last = pe.matmul(bank(u, 3, j * D, (j + 1) * D), y_cols[u][:, j * P:(j + 1) * P],
                                             wo[:, :], start=True, stop=True)
                        last.then_inc(wo_ready[u], 1)
                    for u in range(U):
                        pe.wait_ge(normed_ready[u], i * 4 + 4)
                        turn(u, normed[u], turned)
                    for u in range(U):
                        pe.wait_ge(h_ready[u], i * 2 + 2)
                        for c in range(HC):
                            mixed_columns(u, keys(u, c), "cm_Wk", c * P, (c + 1) * P).then_inc(kc_ready[u], 1)
                        now, before = mixed["cm_Wr"]
                        for j in range(NT):
                            dst = bank(u, 3, T + j * D, T + (j + 1) * D)
                            pe.matmul(dst, h_cols[u][:, 1 + j * P:1 + (j + 1) * P], now[:, :],
                                      start=True, stop=False)
                            last = pe.matmul(dst, h_cols[u][:, j * P:(j + 1) * P], before[:, :],
                                             start=False, stop=True)
                        last.then_inc(rc_ready[u], 1)
                    for u in range(U):
                        pe.wait_ge(sq_ready[u], i * 2 + 2)
                        pe.wait_ge(rc_done[u], i + 1)
                        for j in range(NT):
                            for c in range(HC):
                                last = pe.matmul(bank(u, 3, j * D, (j + 1) * D),
                                                 k_sq[u][:, c, j * P:(j + 1) * P], cm_wv[:, c, :],
                                                 start=(c == 0), stop=(c == HC - 1))
                        last.then_inc(cv_ready[u], 1)
                    for u in range(U):
                        pe.wait_ge(xa_ready[u], i * 2 + 2)
                        turn(u, normed[u], xa_turned)
                    for u in range(U):
                        pe.wait_ge(xa_cols_ready[u], i + 1)
                        pe.wait_ge(logits_saved[u], i + 1)
                        for j in range(NT):
                            last = pe.matmul(bank(u, 0, T + j * E, T + (j + 1) * E),
                                             xa_cols[u][:, j * P:(j + 1) * P], router_w[:, :],
                                             start=True, stop=True)
                        last.then_inc(logits_ready[u], 1)

            @block.scalar
            def _(act):
                with act.Fori(0, TURNS) as i:
                    for u in range(U):
                        act.wait_ge(turned[u], i * 2 + 1)
                        act.activation(h_cols[u][:, 1:T + 1], bank(u, 0, 0, T), ACT.Identity,
                                       bias=vec(V_B1), scale=vec(V_G1)).then_inc(h_ready[u], 1)
                    for u in range(U):
                        act.wait_ge(r_ready[u], i + 1)
                        act.activation(r_tanh[u][:, :], bank(u, 2, 0, T), ACT.Tanh, scale=0.5).then_inc(r_done[u], 1)
                    for u in range(U):
                        act.wait_ge(args_ready[u], i * 4 + 4)
                        act.activation(keep[u][:, :, :], above[u][:, :, :], ACT.Exp, scale=-1.0
                                       ).then_inc(exps_ready[u], 1)
                        act.activation(take[u][:, :, :], below[u][:, :, :], ACT.Exp).then_inc(exps_ready[u], 1)
                    for u in range(U):
                        act.wait_ge(turned[u], i * 2 + 2)
                        act.activation(h_cols[u][:, 1:T + 1], bank(u, 0, 0, T), ACT.Identity,
                                       bias=vec(V_B2), scale=vec(V_G2)).then_inc(h_ready[u], 1)
                    for u in range(U):
                        for half in range(2):
                            act.wait_ge(kc_ready[u], i * HC + (half + 1) * HC // 2)
                            act.activation(k_relu[u][:, 2 * half:2 * half + 2, :],
                                           bank(u, 1 + half).rearrange("p (c t) -> p c t", t=T),
                                           ACT.Relu).then_inc(relu_ready[u], 1)
                        act.wait_ge(rc_ready[u], i + 1)
                        act.activation(rc_tanh[u][:, :, :],
                                       bank(u, 3, T, 2 * T).rearrange("p (j d) -> p j d", d=D),
                                       ACT.Tanh, scale=0.5).then_inc(rc_done[u], 1)
                    for u in range(U):
                        act.wait_ge(xa_turned[u], i + 1)
                        act.activation(xa_cols[u][:, :], bank(u, 0, 0, T), ACT.Copy).then_inc(xa_cols_ready[u], 1)

            @block.gpsimd
            def _(pool):
                for u in range(U):
                    pool.memset(h_cols[u][:, 0:1], 0.0).then_inc(borders_set, 1)
                    pool.memset(peak[u][:, 0:1], -1e38).then_inc(borders_set, 1)
                    pool.memset(state[u][:, :, 0:1], 0.0).then_inc(borders_set, 1)

                with pool.Fori(0, TURNS) as i:
                    c = Chain(pool, pool_rwkv, i, 6)

                    def rstds(u, k, e):
                        pool.wait_ge(var_ready[u], i * 6 + 2 * k)
                        c.step(pool.tensor_tensor(rstd[u][:, :], mean_var[u][:, :, 1], eps[:, e, :], ALU.add))
                        c.wait()
                        pool.tensor_tensor(rstd[u][:, :], rstd[u][:, :], neg_half[:, 0:NT], ALU.pow
                                           ).then_inc(rstd_ready[u], 1)

                    for u in range(U):
                        rstds(u, 1, EPS_TM)
                    for u in range(U):
                        rstds(u, 2, EPS_TM)
                        pool.wait_ge(x1_ready[u], i + 1)
                        pool.tensor_tensor(x01[u][:, :, :], x0[u][:, :, :], x1[u][:, :, :], ALU.add
                                           ).then_inc(x01_ready[u], 1)
                    for u in range(U):
                        for half in range(2):
                            pool.wait_ge(relu_ready[u], i * 2 + half + 1)
                            k = k_relu[u][:, 2 * half:2 * half + 2, :]
                            pool.tensor_tensor(k_sq[u][:, 2 * half:2 * half + 2, :], k, k, ALU.mult
                                               ).then_inc(sq_ready[u], 1)
                    for u in range(U):
                        rstds(u, 3, EPS_LN)
                    c.close()

            @block.vector
            def _(dve):
                dve.wait_ge(borders_set, 3 * U)
                dve.wait_ge(rows_in_sem, 32)
                for u in range(U):
                    dve.sem_inc(x_free[u], 1)
                    dve.sem_inc(logits_saved[u], 1)
                with dve.Fori(0, TURNS) as i:
                    c = Chain(dve, vec_rwkv, i, 40)

                    def normalise(u, k, src, dst, done):
                        dve.wait_ge(rstd_ready[u], i * 3 + k)
                        for j in range(NT):
                            dve.tensor_scalar(dst[j], src[j], mean_var[u][:, j, 0:1], rstd[u][:, j:j + 1],
                                              ALU.subtract, ALU.mult).then_inc(done[u], 1)

                    for u in range(U):
                        dve.wait_ge(x_loaded[u], i * 16 + 16)
                        stats(dve, c, i, [x0[u][:, j, :] for j in range(NT)], u)
                    for u in range(U):
                        normalise(u, 1, [x0[u][:, j, :] for j in range(NT)],
                                  [normed[u][:, j, :] for j in range(NT)], normed_ready)

                    for u in range(U):
                        key = bank(u, 1, 0, T)
                        before = peak[u][:, 0:T]
                        dve.wait_ge(kv_ready[u], i + 1)
                        c.step(dve.tensor_tensor_scan(peak[u][:, 1:T + 1], NEG_W.to_broadcast([P, T]), key,
                                                      -1e38, ALU.add, ALU.max))
                        c.wait()
                        k = c.step(dve.scalar_tensor_tensor(delta[u][:, :], key, vec(V_FIRST), before,
                                                            ALU.add, ALU.subtract))
                        c.wait(k)
                        for dst, op in ((above, ALU.max), (below, ALU.min)):
                            dve.tensor_scalar(dst[u][:, 0, :], delta[u][:, :], 0.0, None, op
                                              ).then_inc(args_ready[u], 1)
                            dve.tensor_scalar(dst[u][:, 1, :], delta[u][:, :], U_PLUS_W, 0.0,
                                              ALU.subtract, op).then_inc(args_ready[u], 1)
                    for u in range(U):
                        v = bank(u, 1, T, 2 * T)
                        dve.wait_ge(exps_ready[u], i * 2 + 2)
                        k = c.step(dve.tensor_tensor(taken[u][:, :], take[u][:, 1, :], v, ALU.mult))
                        bb = c.step(dve.tensor_tensor_scan(state[u][:, 1, 1:T + 1], keep[u][:, 1, :],
                                                           take[u][:, 1, :], 0.0, ALU.mult, ALU.add))
                        c.wait(k)
                        aa = c.step(dve.tensor_tensor_scan(state[u][:, 0, 1:T + 1], keep[u][:, 1, :],
                                                           taken[u][:, :], 0.0, ALU.mult, ALU.add))
                        vv = c.step(dve.tensor_tensor(value[u][:, :], take[u][:, 0, :], v, ALU.mult))
                        c.wait(bb)
                        den = c.step(dve.tensor_tensor(frac[u][:, 1, :], keep[u][:, 0, :],
                                                       state[u][:, 1, 0:T], ALU.mult))
                        c.wait(aa)
                        num = c.step(dve.tensor_tensor(frac[u][:, 0, :], keep[u][:, 0, :],
                                                       state[u][:, 0, 0:T], ALU.mult))
                        c.wait(den)
                        den = c.step(dve.tensor_tensor(frac[u][:, 1, :], frac[u][:, 1, :],
                                                       take[u][:, 0, :], ALU.add))
                        c.wait(num)
                        num = c.step(dve.tensor_tensor(frac[u][:, 0, :], frac[u][:, 0, :],
                                                       value[u][:, :], ALU.add))
                        c.wait(den)
                        rec = c.step(dve.reciprocal(recip[u][:, :], frac[u][:, 1, :]))
                        dve.wait_ge(r_done[u], i + 1)
                        c.wait(num)
                        num = c.step(dve.scalar_tensor_tensor(frac[u][:, 0, :], r_tanh[u][:, :], 1.0,
                                                              frac[u][:, 0, :], ALU.add, ALU.mult))
                        c.wait(num)
                        dve.scalar_tensor_tensor(y_cols[u][:, :], frac[u][:, 0, :], 0.5, recip[u][:, :],
                                                 ALU.mult, ALU.mult).then_inc(y_ready[u], 1)
                    for u in range(U):
                        dve.wait_ge(wo_ready[u], i + 1)
                        dve.tensor_tensor(x1[u][:, :, :], x0[u][:, :, :],
                                          bank(u, 3, 0, T).rearrange("p (j d) -> p j d", d=D),
                                          ALU.add).then_inc(x1_ready[u], 1)
                        dve.wait_ge(x1_ready[u], i + 1)
                        stats(dve, c, i, [x1[u][:, j, :] for j in range(NT)], u)
                    for u in range(U):
                        normalise(u, 2, [x1[u][:, j, :] for j in range(NT)],
                                  [normed[u][:, j, :] for j in range(NT)], normed_ready)
                    for u in range(U):
                        dve.wait_ge(rc_done[u], i + 1)
                        dve.wait_ge(cv_ready[u], i + 1)
                        c.step(dve.scalar_tensor_tensor(
                            gated[u][:, :, :], rc_tanh[u][:, :, :], 1.0,
                            bank(u, 3, 0, T).rearrange("p (j d) -> p j d", d=D), ALU.add, ALU.mult))
                        dve.wait_ge(x01_ready[u], i + 1)
                        c.wait()
                        c.step(dve.scalar_tensor_tensor(gated[u][:, :, :], gated[u][:, :, :], 0.5,
                                                        x01[u][:, :, :], ALU.mult, ALU.add))
                        c.wait()
                        stats(dve, c, i, [gated[u][:, j, :] for j in range(NT)], u)
                    for u in range(U):
                        normalise(u, 3, [gated[u][:, j, :] for j in range(NT)],
                                  [normed[u][:, j, :] for j in range(NT)], xa_ready)
                        dve.wait_ge(xa_ready[u], i * 2 + 2)
                        dve.tensor_copy(xa[:, bass.ds((i * U + u) * NT, NT), :], normed[u][:, :, :]
                                        ).then_inc(x_free[u], 1)
                    for u in range(U):
                        dve.wait_ge(logits_ready[u], i + 1)
                        dve.tensor_tensor(logits[:, bass.ds((i * U + u) * NT, NT), :],
                                          bank(u, 0, T, T + NT * E).rearrange("p (j e) -> p j e", e=E),
                                          router_b[:, :].unsqueeze(1).to_broadcast([P, NT, E]),
                                          ALU.add).then_inc(logits_saved[u], 1)
                    c.close()

        rw.close()
        layer0.close()

        route = ExitStack()

        best = sb("best", [P, TILES], scope=route)
        candidate = sb("candidate", [P, TILES, E], scope=route)
        chosen = sb("chosen", [P, TILES, E], scope=route)
        chosen_bf = sb("chosen_bf", [P, TILES, E], BF16, scope=route)
        upper_bf = sb("upper_bf", [P, P], BF16, scope=route)
        in_tile = sb("in_tile", [P, E, TILES], scope=route)
        so_far = sb("so_far", [P, E, TILES], scope=route)
        more_than = sb("more_than", [P, E, TILES], scope=route)
        tiles_of = sb("tiles_of", [P, E], scope=route)
        tiles_end = sb("tiles_end", [P, E], scope=route)
        first_row = sb("first_row", [P, E], scope=route)
        place = sb("place", [P, TILES, E], scope=route)
        place_sum = sb("place_sum", [P, TILES], scope=route)
        ended = sb("ended", [P, XTILES, E], scope=route)
        expert_f = sb("expert_f", [P, XTILES], scope=route)

        vec_route = sem("vec_route", rwkv_sems)
        chosen_ready = sem("chosen_ready", rwkv_sems)
        counts_ready = sem("counts_ready", rwkv_sems)
        places_ready = sem("places_ready", rwkv_sems)

        rank = banks[:, 0, 0:TILES * E].rearrange("p (t e) -> p t e", e=E)
        count = banks[:, 1, 0:TILES * E].rearrange("p (t e) -> p t e", e=E)
        preference = consts[:, C_FIRST:C_FIRST + E]
        tile_number = consts[:, C_TILE:C_TILE + XTILES]
        full_tiles = consts[:, C_COUNT:C_COUNT + TILES]
        restart = consts[:, C_RESET:C_RESET + E * TILES]

        with nc.Block() as block:

            @block.vector
            def _(dve):
                c = Chain(dve, vec_route)

                def then(ins):
                    c.wait(c.step(ins))

                wide = [P, TILES, E]
                then(dve.tensor_copy(upper_bf[:, :], consts[:, C_UPPER:C_UPPER + P]))
                then(dve.tensor_reduce(best[:, :], logits[:, :, :], AX, ALU.max))
                then(dve.tensor_tensor(candidate[:, :, :], logits[:, :, :],
                                       best[:, :].unsqueeze(2).to_broadcast(wide), ALU.is_ge))
                then(dve.tensor_tensor(candidate[:, :, :], candidate[:, :, :],
                                       preference.unsqueeze(1).to_broadcast(wide), ALU.mult))
                then(dve.tensor_reduce(best[:, :], candidate[:, :, :], AX, ALU.max))
                then(dve.tensor_tensor(chosen[:, :, :], best[:, :].unsqueeze(2).to_broadcast(wide),
                                       preference.unsqueeze(1).to_broadcast(wide), ALU.is_equal))
                dve.tensor_copy(chosen_bf[:, :, :], chosen[:, :, :]).then_inc(chosen_ready, 1)
                dve.wait_ge(counts_ready, 1)
                then(dve.tensor_copy(in_tile[:, :, :], count.rearrange("p t e -> p e t")))
                then(dve.tensor_tensor_scan(so_far[:, :, :].rearrange("p e t -> p (e t)"), restart,
                                            in_tile[:, :, :].rearrange("p e t -> p (e t)"),
                                            0.0, ALU.mult, ALU.add))
                then(dve.tensor_tensor(more_than[:, :, :],
                                       so_far[:, :, TILES - 1:TILES].to_broadcast([P, E, TILES]),
                                       full_tiles.unsqueeze(1).to_broadcast([P, E, TILES]), ALU.is_gt))
                then(dve.tensor_reduce(tiles_of[:, :], more_than[:, :, :], AX, ALU.add))
                then(dve.tensor_tensor_scan(tiles_end[:, :], restart[:, 1:1 + E], tiles_of[:, :],
                                            0.0, ALU.mult, ALU.add))
                then(dve.tensor_tensor(first_row[:, :], tiles_end[:, :], tiles_of[:, :], ALU.subtract))
                then(dve.tensor_scalar(first_row[:, :], first_row[:, :], float(P), None, ALU.mult))
                then(dve.tensor_tensor(so_far[:, :, :], so_far[:, :, :], in_tile[:, :, :], ALU.subtract))
                then(dve.tensor_tensor(place[:, :, :], rank, so_far[:, :, :].rearrange("p e t -> p t e"), ALU.add))
                then(dve.tensor_tensor(place[:, :, :], place[:, :, :],
                                       first_row[:, :].unsqueeze(1).to_broadcast(wide), ALU.add))
                then(dve.tensor_tensor(place[:, :, :], place[:, :, :], chosen[:, :, :], ALU.mult))
                then(dve.tensor_reduce(place_sum[:, :], place[:, :, :], AX, ALU.add))
                dve.tensor_copy(slot_of[:, :], place_sum[:, :]).then_inc(places_ready, 1)
                then(dve.tensor_tensor(ended[:, :, :], tiles_end[:, :].unsqueeze(1).to_broadcast([P, XTILES, E]),
                                       tile_number.unsqueeze(2).to_broadcast([P, XTILES, E]), ALU.is_le))
                then(dve.tensor_reduce(expert_f[:, :], ended[:, :, :], AX, ALU.add))
                then(dve.tensor_scalar(expert_f[:, :], expert_f[:, :], float(E - 1), None, ALU.min))
                then(dve.tensor_copy(tile_expert[:, :], expert_f[:, :]))

            @block.tensor
            def _(pe):
                flat = chosen_bf[:, :, :].rearrange("p t e -> p (t e)")
                pe.wait_ge(chosen_ready, 1)
                pe.matmul(banks[:, 0, 0:TILES * E], upper_bf[:, :], flat, start=True, stop=True)
                pe.matmul(banks[:, 1, 0:TILES * E], ones_bf[:, :], flat, start=True, stop=True
                          ).then_inc(counts_ready, 1)

            @block.gpsimd
            def _(pool):
                pool.wait_ge(places_ready, 1)
                pool.wait_ge(zeroed_sem, 16)
                for t in range(TILES):
                    pool.indirect_dma_start(sorted_x, bass.IndirectOffsetOnAxis(ap=slot_of[:, t:t + 1], axis=0),
                                            xa[:, t, :], None).then_inc(scattered, 16)

        route.close()

        ex = ExitStack()

        def bufs(name, shape, dt=F32, scope=ex):
            return [sb(f"{name}{u}", shape, dt, scope) for u in range(U)]

        xg = bufs("xg", [P, D])
        xg_cols = bufs("xg_cols", [P, P])
        gate = bufs("gate", [P, XH])
        hidden = bufs("hidden", [P, XH])
        hidden_cols = bufs("hidden_cols", [P, XC, P])
        y_rows = bufs("y_rows", [P, D])

        xg_loaded = pair("xg_loaded")
        xg_turned = pair("xg_turned")
        xg_cols_ready = pair("xg_cols_ready")
        lin_ready = pair("lin_ready")
        gate_in_ready = pair("gate_in_ready")
        gate_ready = pair("gate_ready")
        hidden_ready = pair("hidden_ready")
        hidden_turned = pair("hidden_turned")
        hidden_cols_ready = pair("hidden_cols_ready")
        down_ready = pair("down_ready")
        y_rows_ready = pair("y_rows_ready")

        with nc.Block() as block:

            @block.gpsimd
            def _(pool):
                for used in used_semaphores:
                    pool.sem_clear(used)

            @block.sync
            def _(sp):
                sp.wait_ge(scattered, 16 * TILES)
                with sp.Fori(0, XTILES // U) as i:
                    for u in range(U):
                        sp.wait_ge(xg_turned[u], i + 1)
                        sp.dma_start(xg[u][:, :], sorted_x[bass.ds((i * U + u) * P, P), :]
                                     ).then_inc(xg_loaded[u], 16)

            @block.tensor
            def _(pe):
                pe.wait_ge(expert_w_sem, 32)
                pe.wait_ge(biases_sem, 16)
                ones = ones_bf[0:3, :]
                for u in range(U):
                    pe.sem_inc(xg_turned[u], 1)
                with pe.Fori(0, XTILES // U) as i:
                    e = [pe.value_load(tile_expert[0:1, bass.ds(i * U + u, 1)], min_val=0, max_val=E - 1)
                         for u in range(U)]
                    for u in range(U):
                        pe.wait_ge(xg_loaded[u], i * 16 + 16)
                        pe.wait_ge(y_rows_ready[u], i + 1)
                        pe.transpose(bank(u, 0, 0, P), xg[u][:, :], ident).then_inc(xg_turned[u], 1)
                    for u in range(U):
                        pe.wait_ge(xg_cols_ready[u], i + 1)
                        for k, lo, done in ((2, XH, gate_in_ready), (1, 0, lin_ready)):
                            pe.matmul(bank(u, k), ones, biases[:, bass.ds(e[u], 1), lo:lo + XH].squeeze(1),
                                      start=True, stop=False)
                            pe.matmul(bank(u, k), xg_cols[u][:, :], w1[:, bass.ds(e[u], 1), lo:lo + XH].squeeze(1),
                                      start=False, stop=True).then_inc(done[u], 1)
                    for u in range(U):
                        pe.wait_ge(hidden_ready[u], i + 1)
                        for c in range(XC):
                            last = pe.transpose(bank(u, 3, c * P, (c + 1) * P),
                                                hidden[u][:, c * P:(c + 1) * P], ident)
                        last.then_inc(hidden_turned[u], 1)
                    for u in range(U):
                        pe.wait_ge(hidden_cols_ready[u], i + 1)
                        dst = bank(u, 0, P, P + D)
                        pe.matmul(dst, ones, biases[:, bass.ds(e[u], 1), GLU:GLU + D].squeeze(1),
                                  start=True, stop=False)
                        for c in range(XC):
                            last = pe.matmul(dst, hidden_cols[u][:, c, :],
                                             w2[:, bass.ds(e[u], 1), c, :].squeeze(1),
                                             start=False, stop=(c == XC - 1))
                        last.then_inc(down_ready[u], 1)

            @block.scalar
            def _(act):
                with act.Fori(0, XTILES // U) as i:
                    for u in range(U):
                        act.wait_ge(xg_turned[u], i + 2)
                        act.activation(xg_cols[u][:, :], bank(u, 0, 0, P), ACT.Copy).then_inc(xg_cols_ready[u], 1)
                    for u in range(U):
                        act.wait_ge(gate_in_ready[u], i + 1)
                        act.activation(gate[u][:, :], bank(u, 2), ACT.Sigmoid).then_inc(gate_ready[u], 1)
                    for u in range(U):
                        act.wait_ge(hidden_turned[u], i + 1)
                        act.activation(hidden_cols[u][:, :, :].rearrange("p c t -> p (c t)"), bank(u, 3), ACT.Copy
                                       ).then_inc(hidden_cols_ready[u], 1)
                    for u in range(U):
                        act.wait_ge(y_rows_ready[u], i + 2)
                        act.dma_start(sorted_y[bass.ds((i * U + u) * P, P), :], y_rows[u][:, :]
                                      ).then_inc(y_stored[u], 16)

            @block.vector
            def _(dve):
                for u in range(U):
                    dve.sem_inc(y_rows_ready[u], 1)
                    dve.sem_inc(y_stored[u], 16)
                with dve.Fori(0, XTILES // U) as i:
                    for u in range(U):
                        dve.wait_ge(gate_ready[u], i + 1)
                        dve.wait_ge(lin_ready[u], i + 1)
                        dve.tensor_tensor(hidden[u][:, :], gate[u][:, :], bank(u, 1), ALU.mult
                                          ).then_inc(hidden_ready[u], 1)
                    for u in range(U):
                        dve.wait_ge(down_ready[u], i + 1)
                        dve.wait_ge(y_stored[u], i * 16 + 16)
                        dve.tensor_copy(y_rows[u][:, :], bank(u, 0, P, P + D)).then_inc(y_rows_ready[u], 1)

        ex.close()
        rwkv_sems.close()

        l1 = ExitStack()

        def bufs(name, shape, dt=F32, scope=l1):
            return [sb(f"{name}{u}", shape, dt, scope) for u in range(U)]

        w_qkv = sb("w_qkv", [P, 3 * D], scope=l1)
        w_out = sb("w_out", [P, D], scope=l1)
        ffn_w1 = sb("ffn_w1", [P, HID], scope=l1)
        ffn_w2 = sb("ffn_w2", [P, HC, D], scope=l1)
        slot_rows = sb("slot_rows", [P, SC, D], scope=l1)
        slot_sq = sb("slot_sq", [P, SC, 2], scope=l1)
        slot_cols = sb("slot_cols", [P, SLOTS], scope=l1)
        square_junk = sb("square_junk", [P, D], scope=l1)

        y_idx = bufs("y_idx", [P, NT], I32)
        y_got = bufs("y_got", [P, NT, D])
        summed = bufs("summed", [P, NT, D])
        moments = bufs("moments_b", [P, NT, 6])
        mean_var = bufs("mean_var_b", [P, NT, 2])
        rstd = bufs("rstd_b", [P, NT])
        xb = bufs("xb", [P, NT, D])
        xb_bias = bufs("xb_bias", [P, NT, D])
        cols = bufs("cols", [P, T])
        junk = bufs("junk", [P, D])
        qk_sq = bufs("qk_sq", [P, 2 * NT])
        qk_rms = bufs("qk_rms", [P, 2 * NT])
        q_rows = bufs("q_rows", [P, NT, D])
        q_cols = bufs("q_cols", [P, T])
        k_rows = bufs("k_rows", [P, NT, D])
        v_rows = bufs("v_rows", [P, NT, N129])
        kv_heads = bufs("kv_heads", [P, D + HEADS])
        norm_inv = bufs("norm_inv", [P, NT, HEADS])
        att = bufs("att", [P, NT, D])
        att_cols = bufs("att_cols", [P, T])
        xc = bufs("xc", [P, NT, D])
        xc_sq = bufs("xc_sq", [P, NT])
        xc_rms = bufs("xc_rms", [P, NT])
        xn = bufs("xn", [P, NT, N129])
        xn_cols = bufs("xn_cols", [P, T])
        slot_peak = bufs("slot_peak", [P, SC], BF16)
        token_peak = bufs("token_peak", [P, NT], BF16)
        slot_shift = bufs("slot_shift", [SC, SC, P], BF16)
        token_shift = bufs("token_shift", [NT, NT, P], BF16)
        dispatch = bufs("dispatch", [P, NT, SLOTS])
        combine = bufs("combine", [P, SC, T])
        slot_inv = bufs("slot_inv", [P, SC])
        slots_n = bufs("slots_n", [P, SC, D])
        slots_cols = bufs("slots_cols", [P, SLOTS])
        act_cols = bufs("act_cols", [P, HC, SLOTS])
        processed = bufs("processed", [P, SC, N129])
        out_inv = bufs("out_inv", [P, NT])
        final = bufs("final", [P, NT, D])
        ident_bf = sb("ident_bf", [P, P], BF16, scope=l1)

        slot_sq_ready = sem("slot_sq_ready", l1)
        slot_rms_ready = sem("slot_rms_ready", l1)
        slot_rows_ready = sem("slot_rows_ready", l1)
        slot_turned = sem("slot_turned", l1)
        slot_cols_ready = sem("slot_cols_ready", l1)
        ones_set = sem("ones_set", l1)
        vec_l1 = sem("vec_l1", l1)
        vec_slots = sem("vec_slots", l1)
        pool_slots = sem("pool_slots", l1)
        pool_l1 = sem("pool_l1", l1)
        names = """idx_ready y_gathered var_l1 rstd_l1 xb_ready xb_bias_ready xb_turned xb_cols_ready
            qk_ready qk_sq_ready qk_rms_ready q_rows_ready k_rows_ready v_rows_ready
            q_turned q_cols_ready kv_sum_ready kv_heads_ready att_ready att_rows_ready att_turned
            att_cols_ready wout_ready xc_ready xc_sq_ready xc_rms_ready xn_ready xn_turned
            xn_cols_ready by_slot_ready slot_peak_ready slot_peak_turned slot_shift_ready
            by_token_ready token_peak_ready by_token_shifted dispatch_ready token_peak_turned
            token_shift_ready by_slot_shifted combine_ready slots_ready slots_n_ready slots_turned
            slots_cols_ready hid_ready gelu_ready proc_ready processed_ready mix_ready
            final_ready final_stored""".split()
        S = {n: pair(n, l1) for n in names}

        def by_slot(u, c):
            return bank(u, c // 2, (c % 2) * T, (c % 2 + 1) * T)

        with nc.Block() as block:

            @block.sync
            def _(sp):
                sp.dma_start(w_qkv[:, :], w["W_qkv"]).then_inc(layer1_w_sem, 16)
                sp.dma_start(w_out[:, :], w["W_out"]).then_inc(layer1_w_sem, 16)
                sp.dma_start(ffn_w1[:, :], w["ffn_w1"]).then_inc(layer1_w_sem, 16)
                sp.dma_start(ffn_w2[:, :, :], w["ffn_w2"].rearrange("(c p) d -> p c d", p=P)).then_inc(layer1_w_sem, 16)
                sp.dma_start(slot_rows[:, :, :], w["slots"].rearrange("(c p) d -> p c d", p=P)).then_inc(layer1_w_sem, 16)
                with sp.Fori(0, TURNS) as i:
                    for u in range(U):
                        sp.wait_ge(S["final_ready"][u], i * NT + NT)
                        sp.dma_start(out_rows[bass.ds(i * U + u, 1)].squeeze(0), final[u][:, :, :]
                                     ).then_inc(S["final_stored"][u], 16)
                for u in range(U):
                    sp.wait_ge(S["final_stored"][u], 16 + 16 * TURNS)

            @block.tensor
            def _(pe):
                def turn(u, src, done, lo=0):
                    for j in range(NT):
                        last = pe.transpose(bank(u, 0, j * P, (j + 1) * P), src[:, j, 0:D], ident)
                    last.then_inc(S[done][u], 1)

                pe.wait_ge(slot_rows_ready, SC)
                for s in range(SC):
                    last = pe.transpose(bank(0, 0, s * P, (s + 1) * P), slot_rows[:, s, :], ident)
                last.then_inc(slot_turned, 1)
                pe.wait_ge(slot_cols_ready, 1)
                pe.wait_ge(layer1_w_sem, 16 * 5)
                with pe.Fori(0, TURNS) as i:
                    for u in range(U):
                        pe.wait_ge(S["xb_ready"][u], i * NT + NT)
                        turn(u, xb[u], "xb_turned")
                    for u in range(U):
                        pe.wait_ge(S["xb_cols_ready"][u], i + 1)
                        for j in range(NT):
                            last = pe.matmul(bank(u, 2 + j, 0, 3 * D), cols[u][:, j * P:(j + 1) * P], w_qkv[:, :],
                                             start=True, stop=True)
                        last.then_inc(S["qk_ready"][u], 1)
                    for u in range(U):
                        pe.wait_ge(S["q_rows_ready"][u], i * NT + NT)
                        turn(u, q_rows[u], "q_turned")
                        pe.wait_ge(S["k_rows_ready"][u], i + 1)
                        pe.wait_ge(S["v_rows_ready"][u], i + 1)
                        for j in range(NT):
                            last = pe.matmul(bank(u, 1, 0, N129), k_rows[u][:, j, :], v_rows[u][:, j, :],
                                             start=(j == 0), stop=(j == NT - 1))
                        last.then_inc(S["kv_sum_ready"][u], 1)
                    for u in range(U):
                        pe.wait_ge(S["q_cols_ready"][u], i + 1)
                        pe.wait_ge(S["kv_heads_ready"][u], i * 2 + 2)
                        for j in range(NT):
                            last = pe.matmul(bank(u, 1, 144 + j * (D + HEADS), 144 + (j + 1) * (D + HEADS)),
                                             q_cols[u][:, j * P:(j + 1) * P], kv_heads[u][:, :],
                                             start=True, stop=True)
                        last.then_inc(S["att_ready"][u], 1)
                    for u in range(U):
                        pe.wait_ge(S["att_rows_ready"][u], i + 1)
                        turn(u, att[u], "att_turned")
                    for u in range(U):
                        pe.wait_ge(S["att_cols_ready"][u], i + 1)
                        for j in range(NT):
                            last = pe.matmul(bank(u, 0, T + j * D, T + (j + 1) * D),
                                             att_cols[u][:, j * P:(j + 1) * P], w_out[:, :],
                                             start=True, stop=True)
                        last.then_inc(S["wout_ready"][u], 1)
                    for u in range(U):
                        pe.wait_ge(S["xn_ready"][u], i * NT + NT)
                        turn(u, xn[u], "xn_turned")
                    for u in range(U):
                        pe.wait_ge(S["xn_cols_ready"][u], i + 1)
                        for s in range(SC):
                            last = pe.matmul(by_slot(u, s), slot_cols[:, s * P:(s + 1) * P], xn_cols[u][:, :],
                                             start=(s % 2 == 0), stop=False, skip_group_check=True)
                        last.then_inc(S["by_slot_ready"][u], 1)
                    for u in range(U):
                        pe.wait_ge(S["slot_peak_ready"][u], i + 1)
                        pe.transpose(bank(u, 2, 0, P // 2).bitcast(BF16)[0:SC, :], slot_peak[u][:, :], ident_bf[:, :]
                                     ).then_inc(S["slot_peak_turned"][u], 1)
                    for u in range(U):
                        pe.wait_ge(S["slot_shift_ready"][u], i + 1)
                        for j in range(NT):
                            last = pe.matmul(bank(u, 2 + j), xn_cols[u][:, j * P:(j + 1) * P], slot_cols[:, :],
                                             start=True, stop=False, skip_group_check=True)
                        last.then_inc(S["by_token_ready"][u], 1)
                        pe.wait_ge(S["token_peak_ready"][u], i + 1)
                        for j in range(NT):
                            last = pe.matmul(bank(u, 2 + j), ones_bf[0:SC, :],
                                             slot_shift[u][:, :, :].rearrange("c s p -> c (s p)"),
                                             start=False, stop=True, skip_group_check=True)
                        last.then_inc(S["by_token_shifted"][u], 1)
                    for u in range(U):
                        pe.wait_ge(S["dispatch_ready"][u], i * NT + NT)
                        pe.transpose(bank(u, 2, 0, P // 2).bitcast(BF16)[0:NT, :], token_peak[u][:, :], ident_bf[:, :]
                                     ).then_inc(S["token_peak_turned"][u], 1)
                    for u in range(U):
                        pe.wait_ge(S["token_shift_ready"][u], i + 1)
                        for s in range(SC):
                            dst = bank(u, 2 + s // 2, P + (s % 2) * N129, P + (s % 2 + 1) * N129)
                            for j in range(NT):
                                last = pe.matmul(dst, dispatch[u][:, j, s * P:(s + 1) * P], xn[u][:, j, :],
                                                 start=(j == 0), stop=(j == NT - 1))
                        last.then_inc(S["slots_ready"][u], 1)
                    for u in range(U):
                        shift = token_shift[u][:, :, :].rearrange("c j p -> c (j p)")
                        for s in range(SC):
                            last = pe.matmul(by_slot(u, s), ones_bf[0:NT, :], shift,
                                             start=False, stop=True, skip_group_check=True)
                        last.then_inc(S["by_slot_shifted"][u], 1)
                    for u in range(U):
                        pe.wait_ge(S["slots_n_ready"][u], i + 1)
                        pe.wait_ge(S["combine_ready"][u], i + 1)
                        for s in range(SC):
                            last = pe.transpose(bank(u, 0, s * P, (s + 1) * P), slots_n[u][:, s, :], ident)
                        last.then_inc(S["slots_turned"][u], 1)
                    for u in range(U):
                        pe.wait_ge(S["slots_cols_ready"][u], i + 1)
                        for c in (1, 2, 3, 0):
                            pe.matmul(bank(u, c), ffn_w1[:, c * P:(c + 1) * P], slots_cols[u][:, :],
                                      start=True, stop=True).then_inc(S["hid_ready"][u], 1)
                    for u in range(U):
                        pe.wait_ge(S["gelu_ready"][u], i * HC + HC)
                        for s in range(SC):
                            for c in range(HC):
                                last = pe.matmul(bank(u, 0, s * D, (s + 1) * D), act_cols[u][:, c, s * P:(s + 1) * P],
                                                 ffn_w2[:, c, :], start=(c == 0), stop=(c == HC - 1))
                        last.then_inc(S["proc_ready"][u], 1)
                    for u in range(U):
                        pe.wait_ge(S["processed_ready"][u], i + 1)
                        for j in range(NT):
                            for s in range(SC):
                                last = pe.matmul(bank(u, 1, j * N129, (j + 1) * N129),
                                                 combine[u][:, s, j * P:(j + 1) * P], processed[u][:, s, :],
                                                 start=(s == 0), stop=(s == SC - 1))
                        last.then_inc(S["mix_ready"][u], 1)

            @block.scalar
            def _(act):
                act.wait_ge(layer1_w_sem, 16 * 5)
                for s in range(SC):
                    act.activation(square_junk[:, :], slot_rows[:, s, :], ACT.Square,
                                   accum_out=slot_sq[:, s, 0:1]).then_inc(slot_sq_ready, 1)
                    act.wait_ge(slot_sq_ready, s + 1)
                act.wait_ge(slot_turned, 1)
                act.activation(slot_cols[:, :], bank(0, 0), ACT.Copy).then_inc(slot_cols_ready, 1)

                def take(u, i, wait, dst, done, **how):
                    act.wait_ge(S[wait][u], i + 1)
                    act.activation(dst[u][:, :], bank(u, 0, 0, T), how.pop("func", ACT.Copy), **how
                                   ).then_inc(S[done][u], 1)

                with act.Fori(0, TURNS) as i:
                    for u in range(U):
                        take(u, i, "xb_turned", cols, "xb_cols_ready")
                    for u in range(U):
                        act.wait_ge(S["qk_ready"][u], i + 1)
                        act.activation(v_rows[u][:, :, 0:D], banks[:, 4 * u + 2:4 * u + 4, 2 * D:3 * D], ACT.Copy
                                       ).then_inc(S["v_rows_ready"][u], 1)
                        for j in range(NT):
                            for m in range(2):
                                n = m * NT + j
                                act.activation(junk[u][:, :], bank(u, 2 + j, m * D, (m + 1) * D), ACT.Square,
                                               accum_out=qk_sq[u][:, n:n + 1]).then_inc(S["qk_sq_ready"][u], 1)
                                act.wait_ge(S["qk_sq_ready"][u], i * 2 * NT + j * 2 + m + 1)
                    for u in range(U):
                        take(u, i, "q_turned", q_cols, "q_cols_ready", func=ACT.Relu, scale=vec(V_QN))
                    for u in range(U):
                        take(u, i, "att_turned", att_cols, "att_cols_ready")
                    for u in range(U):
                        act.wait_ge(S["xc_ready"][u], i * NT + NT)
                        for j in range(NT):
                            act.activation(junk[u][:, :], xc[u][:, j, :], ACT.Square,
                                           accum_out=xc_sq[u][:, j:j + 1]).then_inc(S["xc_sq_ready"][u], 1)
                            act.wait_ge(S["xc_sq_ready"][u], i * NT + j + 1)
                    for u in range(U):
                        take(u, i, "xn_turned", xn_cols, "xn_cols_ready")
                    for u in range(U):
                        act.wait_ge(S["by_token_shifted"][u], i + 1)
                        for j in range(NT):
                            act.activation(dispatch[u][:, j, :], bank(u, 2 + j), ACT.Exp
                                           ).then_inc(S["dispatch_ready"][u], 1)
                    for u in range(U):
                        act.wait_ge(S["by_slot_shifted"][u], i + 1)
                        act.activation(combine[u][:, :, :].rearrange("p (b c) t -> p b (c t)", b=2),
                                       banks[:, 4 * u:4 * u + 2, :], ACT.Exp).then_inc(S["combine_ready"][u], 1)
                    for u in range(U):
                        act.wait_ge(S["slots_turned"][u], i + 1)
                        act.activation(slots_cols[u][:, :], bank(u, 0), ACT.Copy
                                       ).then_inc(S["slots_cols_ready"][u], 1)
                    for u in range(U):
                        for n, c in enumerate((1, 2, 3, 0)):
                            act.wait_ge(S["hid_ready"][u], i * HC + n + 1)
                            act.activation(act_cols[u][:, c, :], bank(u, c), ACT.Gelu).then_inc(S["gelu_ready"][u], 1)

            @block.gpsimd
            def _(pool):
                for u in range(U):
                    pool.memset(v_rows[u][:, :, D:D + 1], 1.0).then_inc(ones_set, 1)
                    pool.memset(xn[u][:, :, D:D + 1], 1.0).then_inc(ones_set, 1)
                    pool.memset(processed[u][:, :, D:D + 1], 1.0).then_inc(ones_set, 1)

                c = Chain(pool, pool_slots)
                pool.wait_ge(slot_sq_ready, SC)
                c.step(pool.tensor_scalar(slot_sq[:, :, 1], slot_sq[:, :, 0], 1e-24, 1.0 / D, ALU.max, ALU.mult))
                c.wait()
                pool.tensor_tensor(slot_sq[:, :, 0], slot_sq[:, :, 1], neg_half[:, 0:SC], ALU.pow
                                   ).then_inc(slot_rms_ready, 1)

                for u in range(U):
                    pool.wait_ge(y_stored[u], 16 + 16 * (XTILES // U))
                with pool.Fori(0, TURNS) as i:
                    c = Chain(pool, pool_l1, i, 6 + 2 * 2)

                    def rstds(u, k):
                        pool.wait_ge(S["var_l1"][u], i * 3 * NT + NT * k)
                        c.step(pool.tensor_tensor(rstd[u][:, :], mean_var[u][:, :, 1], eps[:, EPS_LN, :], ALU.add))
                        c.wait()
                        pool.tensor_tensor(rstd[u][:, :], rstd[u][:, :], neg_half[:, 0:NT], ALU.pow
                                           ).then_inc(S["rstd_l1"][u], 1)

                    for u in range(U):
                        settle(pool, S["idx_ready"][u], i + 1, pool_passed)
                        for j in range(NT):
                            pool.indirect_dma_start(y_got[u][:, j, :], None, sorted_y,
                                                    bass.IndirectOffsetOnAxis(ap=y_idx[u][:, j:j + 1], axis=0)
                                                    ).then_inc(S["y_gathered"][u], 16)
                    for u in range(U):
                        rstds(u, 1)
                    for u in range(U):
                        pool.wait_ge(S["xb_ready"][u], i * NT + NT)
                        pool.tensor_tensor(xb_bias[u][:, :, :], xb[u][:, :, :],
                                           rows[:, R_BOUT, :].unsqueeze(1).to_broadcast([P, NT, D]), ALU.add
                                           ).then_inc(S["xb_bias_ready"][u], 1)
                    for u in range(U):
                        settle(pool, S["qk_sq_ready"][u], i * 2 * NT + 2 * NT, pool_passed)
                        k = c.step(pool.tensor_scalar(qk_rms[u][:, :], qk_sq[u][:, :], 1.0 / D, 1e-6,
                                                      ALU.mult, ALU.add))
                        c.wait(k)
                        pool.tensor_tensor(qk_rms[u][:, :], qk_rms[u][:, :], neg_half[:, 0:2 * NT], ALU.pow
                                           ).then_inc(S["qk_rms_ready"][u], 1)
                    for u in range(U):
                        rstds(u, 2)
                    for u in range(U):
                        settle(pool, S["xc_sq_ready"][u], i * NT + NT, pool_passed)
                        k = c.step(pool.tensor_scalar(xc_rms[u][:, :], xc_sq[u][:, :], 1e-24, 1.0 / D,
                                                      ALU.max, ALU.mult))
                        c.wait(k)
                        pool.tensor_tensor(xc_rms[u][:, :], xc_rms[u][:, :], neg_half[:, 0:NT], ALU.pow
                                           ).then_inc(S["xc_rms_ready"][u], 1)
                    for u in range(U):
                        rstds(u, 3)
                    c.close()

            @block.vector
            def _(dve):
                p = Chain(dve, vec_slots)
                p.step(dve.tensor_copy(ident_bf[:, :], ident))
                dve.wait_ge(slot_rms_ready, 1)
                for s in range(SC):
                    dve.scalar_tensor_tensor(slot_rows[:, s, :], slot_rows[:, s, :], slot_sq[:, s, 0:1],
                                             rows[:, R_GS, :], ALU.mult, ALU.mult).then_inc(slot_rows_ready, 1)
                dve.wait_ge(ones_set, 3 * U)
                p.wait()
                for u in range(U):
                    dve.sem_inc(S["final_stored"][u], 16)
                with dve.Fori(0, TURNS) as i:
                    c = Chain(dve, vec_l1, i, 32)

                    def stats_l1(u, src):
                        for j in range(NT):
                            c.step(dve.bn_stats(moments[u][:, j, :], src[u][:, j, :]))
                        settle(dve, c.sem, i * c.per_turn + c.n, vec_passed)
                        for j in range(NT):
                            dve.bn_aggr(mean_var[u][:, j, :], moments[u][:, j, :]).then_inc(S["var_l1"][u], 1)

                    def normalise(u, k, src, dst, done):
                        dve.wait_ge(S["rstd_l1"][u], i * 3 + k)
                        for j in range(NT):
                            dve.tensor_scalar(dst[u][:, j, :], src[u][:, j, :], mean_var[u][:, j, 0:1],
                                              rstd[u][:, j:j + 1], ALU.subtract, ALU.mult).then_inc(S[done][u], 1)

                    for u in range(U):
                        dve.tensor_copy(y_idx[u][:, :], slot_of[:, bass.ds((i * U + u) * NT, NT)]
                                        ).then_inc(S["idx_ready"][u], 1)
                    for u in range(U):
                        dve.wait_ge(S["y_gathered"][u], i * 16 * NT + 16 * NT)
                        c.step(dve.tensor_tensor(summed[u][:, :, :], xa[:, bass.ds((i * U + u) * NT, NT), :],
                                                 y_got[u][:, :, :], ALU.add))
                        c.wait()
                        stats_l1(u, summed)
                    for u in range(U):
                        normalise(u, 1, summed, xb, "xb_ready")
                    for u in range(U):
                        dve.wait_ge(S["qk_rms_ready"][u], i + 1)
                        for j in range(NT):
                            dve.tensor_scalar(q_rows[u][:, j, :], bank(u, 2 + j, 0, D), qk_rms[u][:, j:j + 1],
                                              None, ALU.mult).then_inc(S["q_rows_ready"][u], 1)
                        for j in range(NT):
                            c.step(dve.scalar_tensor_tensor(k_rows[u][:, j, :], bank(u, 2 + j, D, 2 * D),
                                                            qk_rms[u][:, NT + j:NT + j + 1], rows[:, R_KN, :],
                                                            ALU.mult, ALU.mult))
                        c.wait()
                        dve.tensor_scalar(k_rows[u][:, :, :], k_rows[u][:, :, :], 0.0, None, ALU.max
                                          ).then_inc(S["k_rows_ready"][u], 1)
                    for u in range(U):
                        dve.wait_ge(S["kv_sum_ready"][u], i + 1)
                        dve.tensor_tensor(kv_heads[u][:, 0:D], consts[:, C_BLOCK:C_BLOCK + D], bank(u, 1, 0, D),
                                          ALU.mult).then_inc(S["kv_heads_ready"][u], 1)
                        dve.tensor_scalar(kv_heads[u][:, D:D + HEADS], consts[:, C_HEADS:C_HEADS + HEADS],
                                          bank(u, 1, D, D + 1), None, ALU.mult).then_inc(S["kv_heads_ready"][u], 1)
                    for u in range(U):
                        o = bank(u, 1, 144, 144 + NT * (D + HEADS)).rearrange("p (j n) -> p j n", j=NT)
                        dve.wait_ge(S["att_ready"][u], i + 1)
                        c.step(dve.tensor_scalar(norm_inv[u][:, :, :], o[:, :, D:D + HEADS], 1e-6, None, ALU.add))
                        c.wait()
                        c.step(dve.reciprocal(norm_inv[u][:, :, :], norm_inv[u][:, :, :]))
                        c.wait()
                        dve.tensor_tensor(att[u][:, :, :].rearrange("p j (h d) -> p j h d", d=DH),
                                          o[:, :, 0:D].rearrange("p j (h d) -> p j h d", d=DH),
                                          norm_inv[u][:, :, :].unsqueeze(3).to_broadcast([P, NT, HEADS, DH]),
                                          ALU.mult).then_inc(S["att_rows_ready"][u], 1)
                    for u in range(U):
                        dve.wait_ge(S["wout_ready"][u], i + 1)
                        dve.wait_ge(S["xb_bias_ready"][u], i + 1)
                        c.step(dve.tensor_tensor(summed[u][:, :, :], xb_bias[u][:, :, :],
                                                 bank(u, 0, T, 2 * T).rearrange("p (j d) -> p j d", d=D), ALU.add))
                        c.wait()
                        stats_l1(u, summed)
                    for u in range(U):
                        normalise(u, 2, summed, xc, "xc_ready")
                    for u in range(U):
                        dve.wait_ge(S["xc_rms_ready"][u], i + 1)
                        for j in range(NT):
                            dve.scalar_tensor_tensor(xn[u][:, j, 0:D], xc[u][:, j, :], xc_rms[u][:, j:j + 1],
                                                     rows[:, R_GX, :], ALU.mult, ALU.mult
                                                     ).then_inc(S["xn_ready"][u], 1)
                    for u in range(U):
                        dve.wait_ge(S["by_slot_ready"][u], i + 1)
                        dve.tensor_reduce(slot_peak[u][:, :],
                                          banks[:, 4 * u:4 * u + 2, :].rearrange("p b (c t) -> p (b c) t", t=T),
                                          AX, ALU.max, negate=True).then_inc(S["slot_peak_ready"][u], 1)
                    for u in range(U):
                        dve.wait_ge(S["slot_peak_turned"][u], i + 1)
                        dve.tensor_tensor(slot_shift[u][:, :, :],
                                          consts[0:SC, C_DIAG:C_DIAG + SC].unsqueeze(2).to_broadcast([SC, SC, P]),
                                          bank(u, 2, 0, P // 2).bitcast(BF16)[0:SC, :].unsqueeze(1).to_broadcast([SC, SC, P]),
                                          ALU.mult).then_inc(S["slot_shift_ready"][u], 1)
                    for u in range(U):
                        dve.wait_ge(S["by_token_ready"][u], i + 1)
                        dve.tensor_reduce(token_peak[u][:, :], banks[:, 4 * u + 2:4 * u + 4, :], AX, ALU.max,
                                          negate=True).then_inc(S["token_peak_ready"][u], 1)
                    for u in range(U):
                        dve.wait_ge(S["token_peak_turned"][u], i + 1)
                        dve.tensor_tensor(token_shift[u][:, :, :],
                                          consts[0:NT, C_DIAG:C_DIAG + NT].unsqueeze(2).to_broadcast([NT, NT, P]),
                                          bank(u, 2, 0, P // 2).bitcast(BF16)[0:NT, :].unsqueeze(1).to_broadcast([NT, NT, P]),
                                          ALU.mult).then_inc(S["token_shift_ready"][u], 1)
                    for u in range(U):
                        s = banks[:, 4 * u + 2:4 * u + 4, P:P + 2 * N129].rearrange("p b (c n) -> p b c n", n=N129)
                        inv = slot_inv[u][:, :].rearrange("p (b c) -> p b c", b=2)
                        dve.wait_ge(S["slots_ready"][u], i + 1)
                        c.step(dve.reciprocal(inv, s[:, :, :, D]))
                        c.wait()
                        dve.tensor_tensor(slots_n[u][:, :, :].rearrange("p (b c) d -> p b c d", b=2),
                                          s[:, :, :, 0:D], inv.unsqueeze(3).to_broadcast([P, 2, 2, D]), ALU.mult
                                          ).then_inc(S["slots_n_ready"][u], 1)
                    for u in range(U):
                        dve.wait_ge(S["proc_ready"][u], i + 1)
                        dve.tensor_copy(processed[u][:, :, 0:D], bank(u, 0).rearrange("p (s d) -> p s d", d=D)
                                        ).then_inc(S["processed_ready"][u], 1)
                    for u in range(U):
                        o = bank(u, 1, 0, NT * N129).rearrange("p (j n) -> p j n", n=N129)
                        dve.wait_ge(S["mix_ready"][u], i + 1)
                        c.step(dve.reciprocal(out_inv[u][:, :], o[:, :, D]))
                        c.wait()
                        for j in range(NT):
                            c.step(dve.scalar_tensor_tensor(summed[u][:, j, :], o[:, j, 0:D], out_inv[u][:, j:j + 1],
                                                            xc[u][:, j, :], ALU.mult, ALU.add))
                        c.wait()
                        stats_l1(u, summed)
                    for u in range(U):
                        dve.wait_ge(S["final_stored"][u], i * 16 + 16)
                        normalise(u, 3, summed, final, "final_ready")
                    c.close()

        l1.close()


_COLUMNS = ["L0_attn_ln1_g", "L0_attn_ln1_b", "L0_attn_ln2_g", "L0_attn_ln2_b", "L0_attn_tm_mix_k",
            "L0_attn_tm_mix_v", "L0_attn_tm_mix_r", "L0_attn_cm_mix_k", "L0_attn_cm_mix_r",
            "L0_attn_time_decay", "L0_attn_time_first", "L1_attn_qn_w"]
_ROWS = ["L1_attn_kn_w", "L1_attn_b_out", "L1_ffn_gamma_x", "L1_ffn_gamma_slot"]
_WEIGHTS = {"tm_Wk": "L0_attn_tm_Wk", "tm_Wv": "L0_attn_tm_Wv", "tm_Wr": "L0_attn_tm_Wr", "Wo": "L0_attn_Wo",
            "cm_Wk": "L0_attn_cm_Wk", "cm_Wv": "L0_attn_cm_Wv", "cm_Wr": "L0_attn_cm_Wr",
            "router_w": "L0_ffn_router_w", "router_b": "L0_ffn_router_b", "w1": "L0_ffn_w1", "b1": "L0_ffn_b1",
            "w2": "L0_ffn_w2", "b2": "L0_ffn_b2", "W_qkv": "L1_attn_W_qkv", "W_out": "L1_attn_W_out",
            "slots": "L1_ffn_slot_embeds", "ffn_w1": "L1_ffn_w1", "ffn_w2": "L1_ffn_w2"}


def _constants(np, heads=16, experts=8, tiles=32):
    c = np.zeros((P, C_END), np.float32)
    p = np.arange(P)
    c[:, C_IDENT:C_IDENT + P] = np.eye(P)
    c[:, C_UPPER:C_UPPER + P] = p[:, None] < p[None, :]
    c[:, C_BLOCK:C_BLOCK + P] = p[:, None] // (P // heads) == p[None, :] // (P // heads)
    c[:, C_HEADS:C_HEADS + heads] = p[:, None] // (P // heads) == np.arange(heads)
    c[:, C_FIRST:C_FIRST + experts] = experts - np.arange(experts)
    c[:, C_TILE:C_TILE + 40] = np.arange(40)
    c[:, C_COUNT:C_COUNT + tiles] = P * np.arange(tiles)
    c[:, C_RESET:C_RESET + experts * tiles] = np.arange(experts * tiles) % tiles != 0
    c[0:16, C_DIAG:C_DIAG + 16] = np.eye(16)
    return c


def kernel(**inputs):
    import numpy as _np
    import concourse.bacc as _bacc
    from concourse import mybir as _mybir
    from concourse.bass_utils import run_bass_kernel_spmd as _run

    nc = _bacc.Bacc("TRN2", target_bir_lowering=False, num_devices=1)
    arrays = {}

    def give(name, a):
        a = _np.ascontiguousarray(a)
        arrays[name] = a
        return nc.dram_tensor(name, a.shape, _mybir.dt.from_np(a.dtype), kind="ExternalInput").ap()

    x = give("x_dram", inputs["L0_attn_inputs"])
    vecs = give("vecs_dram", _np.stack([_np.asarray(inputs[n]) for n in _COLUMNS], axis=1))
    rows = give("rows_dram", _np.stack([_np.asarray(inputs[n]) for n in _ROWS], axis=0))
    consts = give("consts_dram", _constants(_np))
    w = {}
    for short, name in _WEIGHTS.items():
        a = _np.asarray(inputs[name])
        w[short] = give(short + "_dram", a.reshape(-1, a.shape[-1]) if short == "slots" else a)
    out = nc.dram_tensor("out_dram", inputs["L0_attn_inputs"].shape, F32, kind="ExternalOutput").ap()
    two_layer_kernel(nc, x, vecs, rows, consts, w, out)
    r = _run(nc, [arrays], core_ids=[0])
    return r.results[0]["out_dram"]
```

```python
from contextlib import ExitStack

import concourse.bass as bass
from concourse import mybir

ALU = mybir.AluOpType
ACT = mybir.ActivationFunctionType
F32 = mybir.dt.float32
BF16 = mybir.dt.bfloat16
I32 = mybir.dt.int32
AX = mybir.AxisListType.X

P = 128
U = 2

C_IDENT, C_UPPER, C_BLOCK, C_HEADS = 0, 128, 256, 384
C_FIRST, C_TILE, C_COUNT, C_RESET, C_DIAG, C_END = 400, 408, 448, 480, 736, 752
(V_G1, V_B1, V_G2, V_B2, V_MK, V_MV, V_MR, V_CK, V_CR, V_DECAY, V_FIRST, V_QN, V_N) = range(13)
R_KN, R_BOUT, R_GX, R_GS, R_N = range(5)


class Chain:

    def __init__(self, eng, sem, turn=0, per_turn=0):
        self.eng, self.sem, self.turn, self.per_turn, self.n = eng, sem, turn, per_turn, 0

    def step(self, ins):
        ins.then_inc(self.sem, 1)
        self.n += 1
        return self.n

    def wait(self, n=None):
        n = self.n if n is None else n
        self.eng.wait_ge(self.sem, self.turn * self.per_turn + n if self.per_turn else n)

    def close(self):
        assert self.n == self.per_turn, f"per_turn should be {self.n}"


def settle(eng, sem, value, passed):
    eng.wait_ge(sem, value)
    eng.sem_inc(passed, 1)


def two_layer_kernel(nc, x_in, vecs_in, rows_in, consts_in, w, out):
    SEQ, T, D = x_in.shape
    NT = T // P
    TILES = SEQ * NT
    TURNS = SEQ // U
    HID = w["cm_Wk"].shape[1]
    HC = HID // P
    E, _, GLU = w["w1"].shape
    XH = GLU // 2
    XC = XH // P
    XTILES = U * -(-(TILES + E - 1) // U)
    HEADS = C_FIRST - C_HEADS
    DH = D // HEADS
    SLOTS = w["slots"].shape[0]
    SC = SLOTS // P
    N129 = D + 1

    x_rows = x_in.rearrange("s (j p) d -> s p j d", p=P)
    out_rows = out.rearrange("s (j p) d -> s p j d", p=P)
    sorted_x = nc.dram_tensor("sorted_x", [XTILES * P, D], F32, kind="Internal").ap()
    sorted_y = nc.dram_tensor("sorted_y", [XTILES * P, D], F32, kind="Internal").ap()
    bias_parts = nc.dram_tensor("bias_parts", [3, E, GLU + D], BF16, kind="Internal").ap()

    ctx = ExitStack()
    with ctx:
        rwkv_sems = ExitStack()
        used_semaphores = []
        expert_sems = ExitStack()
        expert_semaphores = []

        def sem(name, scope=ctx):
            made = scope.enter_context(nc.semaphore(name))
            if scope is rwkv_sems:
                used_semaphores.append(made)
            if scope is expert_sems:
                expert_semaphores.append(made)
            return made

        def pair(name, scope=ctx):
            return [sem(f"{name}{u}", scope) for u in range(U)]

        def sb(name, shape, dt=F32, scope=ctx):
            return scope.enter_context(nc.sbuf_tensor(name, shape, dt))

        banks = ctx.enter_context(nc.psum_tensor("banks", [P, 8, 512], F32))

        def bank(u, k, lo=0, hi=512):
            return banks[:, 4 * u + k, lo:hi]

        consts = sb("consts", [P, C_END])
        vecs = sb("vecs", [P, V_N])
        rows = sb("rows", [P, R_N, D])
        router_b = sb("router_b", [P, E])
        ident = consts[:, C_IDENT:C_IDENT + P]
        ones_bf = sb("ones_bf", [P, P], BF16)
        eps = sb("eps", [P, 3, NT])
        EPS_LN, EPS_TM, EPS_RMS = 0, 1, 2
        neg_half = sb("neg_half", [P, 4])
        zeros = sb("zeros", [P, D])
        w1 = sb("w1", [P, E, GLU])
        w2 = sb("w2", [P, E, XC, D])
        biases = sb("biases", [3, E, GLU + D], BF16)
        xa = sb("xa", [P, TILES, D])
        logits = sb("logits", [P, TILES, E])
        slot_of = sb("slot_of", [P, TILES], I32)
        tile_expert = sb("tile_expert", [P, XTILES], I32)

        consts_in_sem = sem("consts_loaded")
        rows_in_sem = sem("rows_loaded")
        rwkv_w_sem = sem("rwkv_weights_loaded")
        expert_w_sem = sem("expert_weights_loaded")
        layer1_w_sem = sem("layer1_weights_loaded")
        zeroed_sem = sem("sorted_x_zeroed")
        vec_passed = sem("vec_passed")
        pool_passed = sem("pool_passed")
        parts_sem = sem("bias_parts_stored")
        biases_sem = sem("biases_loaded")
        scattered = sem("rows_scattered")
        y_stored = pair("expert_rows_stored")

        layer0 = ExitStack()
        prep = ExitStack()

        def vec(k):
            return vecs[:, k:k + 1]

        mixed = {n: (sb(f"{n}_now", [P, c], scope=layer0), sb(f"{n}_before", [P, c], scope=layer0))
                 for n, c in (("tm_Wk", D), ("tm_Wv", D), ("tm_Wr", D), ("cm_Wk", HID), ("cm_Wr", D))}
        mix_of = {"tm_Wk": V_MK, "tm_Wv": V_MV, "tm_Wr": V_MR, "cm_Wk": V_CK, "cm_Wr": V_CR}
        wo = sb("wo", [P, D], scope=layer0)
        cm_wv = sb("cm_wv", [P, HC, D], scope=layer0)
        router_w = sb("router_w", [P, E], scope=layer0)
        decay = sb("decay", [P, 2], scope=layer0)
        NEG_W, U_PLUS_W = decay[:, 0:1], decay[:, 1:2]

        raw_b = sb("raw_b", [E, GLU + D], scope=prep)
        rest_b = sb("rest_b", [E, GLU + D], scope=prep)
        part_b = sb("part_b", [E, 3, GLU + D], BF16, scope=prep)
        exp_decay = sb("exp_decay", [P, 1], scope=prep)

        zero_made = sem("zero_made", rwkv_sems)
        ones_made = sem("ones_made", rwkv_sems)
        vec_prep = sem("vec_prep", rwkv_sems)
        decay_exp = sem("decay_exp", rwkv_sems)
        parts_made = sem("bias_parts_made", rwkv_sems)

        with nc.Block() as block:

            @block.sync
            def _(sp):
                sp.dma_start(consts[:, :], consts_in).then_inc(consts_in_sem, 16)
                sp.dma_start(vecs[:, :], vecs_in).then_inc(consts_in_sem, 16)
                for n in mixed:
                    sp.dma_start(mixed[n][1][:, :], w[n]).then_inc(rwkv_w_sem, 16)
                sp.dma_start(wo[:, :], w["Wo"]).then_inc(rwkv_w_sem, 16)
                sp.dma_start(cm_wv[:, :, :], w["cm_Wv"].rearrange("(c p) d -> p c d", p=P)).then_inc(rwkv_w_sem, 16)
                sp.dma_start(router_w[:, :], w["router_w"]).then_inc(rwkv_w_sem, 16)
                sp.dma_start(raw_b[:, 0:GLU], w["b1"]).then_inc(consts_in_sem, 16)
                sp.dma_start(raw_b[:, GLU:GLU + D], w["b2"]).then_inc(consts_in_sem, 16)

            @block.scalar
            def _(act):
                act.wait_ge(consts_in_sem, 64)
                act.activation(exp_decay[:, :], vec(V_DECAY), ACT.Exp).then_inc(decay_exp, 1)
                act.dma_start(rows[:, :, :], rows_in.partition_broadcast(P)).then_inc(rows_in_sem, 16)
                act.dma_start(router_b[:, :], w["router_b"].partition_broadcast(P)).then_inc(rows_in_sem, 16)
                act.wait_ge(zero_made, 1)
                act.dma_start(sorted_x.rearrange("(t p) d -> p t d", p=P),
                              zeros[:, :].unsqueeze(1).to_broadcast([P, XTILES, D])).then_inc(zeroed_sem, 16)
                act.dma_start(w1[:, :, :], w["w1"].rearrange("e p f -> p e f")).then_inc(expert_w_sem, 16)
                act.dma_start(w2[:, :, :, :], w["w2"].rearrange("e (c p) d -> p e c d", p=P)).then_inc(expert_w_sem, 16)
                act.wait_ge(parts_made, 3)
                for k in range(3):
                    act.dma_start(bias_parts[k], part_b[:, k, :]).then_inc(parts_sem, 16)
                act.wait_ge(parts_sem, 48)
                act.dma_start(biases[:, :, :], bias_parts).then_inc(biases_sem, 16)

            @block.gpsimd
            def _(pool):
                pool.memset(zeros[:, :], 0.0).then_inc(zero_made, 1)
                pool.memset(ones_bf[:, :], 1.0).then_inc(ones_made, 1)
                pool.memset(eps[:, EPS_LN, :], 1e-5).then_inc(ones_made, 1)
                pool.memset(eps[:, EPS_TM, :], 1e-3).then_inc(ones_made, 1)
                pool.memset(eps[:, EPS_RMS, :], 1e-6).then_inc(ones_made, 1)
                pool.memset(neg_half[:, :], -0.5).then_inc(ones_made, 1)

            @block.vector
            def _(dve):
                c = Chain(dve, vec_prep)
                dve.wait_ge(consts_in_sem, 64)
                dve.wait_ge(decay_exp, 1)
                c.step(dve.tensor_scalar(NEG_W, exp_decay[:, :], -1.0, None, ALU.mult))
                c.wait()
                c.step(dve.tensor_tensor(U_PLUS_W, NEG_W, vec(V_FIRST), ALU.add))
                dve.wait_ge(rwkv_w_sem, 16 * 8)
                for n, (now, before) in mixed.items():
                    k = c.step(dve.tensor_scalar(now[:, :], before[:, :], vec(mix_of[n]), None, ALU.mult))
                    c.wait(k)
                    c.step(dve.tensor_tensor(before[:, :], before[:, :], now[:, :], ALU.subtract))
                source = raw_b
                for k in range(3):
                    dve.tensor_copy(part_b[:, k, :], source[:, :]).then_inc(parts_made, 1)
                    if k < 2:
                        dve.wait_ge(parts_made, k + 1)
                        c.step(dve.tensor_tensor(rest_b[:, :], source[:, :], part_b[:, k, :], ALU.subtract))
                        c.wait()
                        source = rest_b

        prep.close()

        rw = ExitStack()

        def bufs(name, shape, dt=F32, scope=rw):
            return [sb(f"{name}{u}", shape, dt, scope) for u in range(U)]

        x0 = bufs("x0", [P, NT, D])
        moments = bufs("moments", [P, NT, 6])
        mean_var = bufs("mean_var", [P, NT, 2])
        rstd = bufs("rstd", [P, NT])
        normed = bufs("normed", [P, NT, D])
        h_cols = bufs("h_cols", [P, T + 1])
        peak = bufs("peak", [P, T + 1])
        delta = bufs("delta", [P, T])
        above = bufs("above", [P, 2, T])
        below = bufs("below", [P, 2, T])
        keep = bufs("keep", [P, 2, T])
        take = bufs("take", [P, 2, T])
        state = bufs("state", [P, 2, T + 1])
        value = bufs("value", [P, T])
        taken = bufs("taken", [P, T])
        frac = bufs("frac", [P, 2, T])
        recip = bufs("recip", [P, T])
        r_tanh = bufs("r_tanh", [P, T])
        y_cols = bufs("y_cols", [P, T])
        x1 = bufs("x1", [P, NT, D])
        x01 = bufs("x01", [P, NT, D])
        k_relu = bufs("k_relu", [P, HC, T])
        k_sq = bufs("k_sq", [P, HC, T])
        rc_tanh = bufs("rc_tanh", [P, NT, D])
        gated = bufs("gated", [P, NT, D])
        xa_cols = bufs("xa_cols", [P, T])

        x_loaded = pair("x_loaded", rwkv_sems)
        x_free = pair("x_free", rwkv_sems)
        var_ready = pair("var_ready", rwkv_sems)
        rstd_ready = pair("rstd_ready", rwkv_sems)
        normed_ready = pair("normed_ready", rwkv_sems)
        turned = pair("turned", rwkv_sems)
        h_ready = pair("h_ready", rwkv_sems)
        kv_ready = pair("kv_ready", rwkv_sems)
        r_ready = pair("r_ready", rwkv_sems)
        r_done = pair("r_done", rwkv_sems)
        args_ready = pair("args_ready", rwkv_sems)
        exps_ready = pair("exps_ready", rwkv_sems)
        y_ready = pair("y_ready", rwkv_sems)
        wo_ready = pair("wo_ready", rwkv_sems)
        x1_ready = pair("x1_ready", rwkv_sems)
        x01_ready = pair("x01_ready", rwkv_sems)
        kc_ready = pair("kc_ready", rwkv_sems)
        relu_ready = pair("relu_ready", rwkv_sems)
        sq_ready = pair("sq_ready", rwkv_sems)
        rc_ready = pair("rc_ready", rwkv_sems)
        rc_done = pair("rc_done", rwkv_sems)
        cv_ready = pair("cv_ready", rwkv_sems)
        xa_ready = pair("xa_ready", rwkv_sems)
        xa_turned = pair("xa_turned", rwkv_sems)
        xa_cols_ready = pair("xa_cols_ready", rwkv_sems)
        logits_ready = pair("logits_ready", rwkv_sems)
        logits_saved = pair("logits_saved", rwkv_sems)
        borders_set = sem("borders_set", rwkv_sems)
        vec_rwkv = sem("vec_rwkv", rwkv_sems)
        pool_rwkv = sem("pool_rwkv", rwkv_sems)

        def keys(u, c):
            return bank(u, 1 + c // 2, (c % 2) * T, (c % 2 + 1) * T)

        def stats(dve, c, i, src, u):
            for j in range(NT):
                c.step(dve.bn_stats(moments[u][:, j, :], src[j]))
            settle(dve, c.sem, i * c.per_turn + c.n, vec_passed)
            for j in range(NT):
                dve.bn_aggr(mean_var[u][:, j, :], moments[u][:, j, :]).then_inc(var_ready[u], 1)

        with nc.Block() as block:

            @block.sync
            def _(sp):
                with sp.Fori(0, TURNS) as i:
                    for u in range(U):
                        sp.wait_ge(x_free[u], i + 1)
                        sp.dma_start(x0[u][:, :, :], x_rows[bass.ds(i * U + u, 1)].squeeze(0)
                                     ).then_inc(x_loaded[u], 16)

            @block.tensor
            def _(pe):
                def turn(u, src, done):
                    for j in range(NT):
                        last = pe.transpose(bank(u, 0, j * P, (j + 1) * P), src[:, j, :], ident)
                    last.then_inc(done[u], 1)

                def mixed_columns(u, dst, name, lo, hi):
                    now, before = mixed[name]
                    pe.matmul(dst, now[:, lo:hi], h_cols[u][:, 1:T + 1], start=True, stop=False)
                    return pe.matmul(dst, before[:, lo:hi], h_cols[u][:, 0:T], start=False, stop=True)

                with pe.Fori(0, TURNS) as i:
                    for u in range(U):
                        pe.wait_ge(normed_ready[u], i * 4 + 2)
                        turn(u, normed[u], turned)
                    for u in range(U):
                        pe.wait_ge(h_ready[u], i * 2 + 1)
                        mixed_columns(u, bank(u, 1, 0, T), "tm_Wk", 0, D)
                        mixed_columns(u, bank(u, 1, T, 2 * T), "tm_Wv", 0, D).then_inc(kv_ready[u], 1)
                        mixed_columns(u, bank(u, 2, 0, T), "tm_Wr", 0, D).then_inc(r_ready[u], 1)
                    for u in range(U):
                        pe.wait_ge(y_ready[u], i + 1)
                        for j in range(NT):
                            last = pe.matmul(bank(u, 3, j * D, (j + 1) * D), y_cols[u][:, j * P:(j + 1) * P],
                                             wo[:, :], start=True, stop=True)
                        last.then_inc(wo_ready[u], 1)
                    for u in range(U):
                        pe.wait_ge(normed_ready[u], i * 4 + 4)
                        turn(u, normed[u], turned)
                    for u in range(U):
                        pe.wait_ge(h_ready[u], i * 2 + 2)
                        for c in range(HC):
                            mixed_columns(u, keys(u, c), "cm_Wk", c * P, (c + 1) * P).then_inc(kc_ready[u], 1)
                        now, before = mixed["cm_Wr"]
                        for j in range(NT):
                            dst = bank(u, 3, T + j * D, T + (j + 1) * D)
                            pe.matmul(dst, h_cols[u][:, 1 + j * P:1 + (j + 1) * P], now[:, :],
                                      start=True, stop=False)
                            last = pe.matmul(dst, h_cols[u][:, j * P:(j + 1) * P], before[:, :],
                                             start=False, stop=True)
                        last.then_inc(rc_ready[u], 1)
                    for u in range(U):
                        pe.wait_ge(sq_ready[u], i * 2 + 2)
                        pe.wait_ge(rc_done[u], i + 1)
                        for j in range(NT):
                            for c in range(HC):
                                last = pe.matmul(bank(u, 3, j * D, (j + 1) * D),
                                                 k_sq[u][:, c, j * P:(j + 1) * P], cm_wv[:, c, :],
                                                 start=(c == 0), stop=(c == HC - 1))
                        last.then_inc(cv_ready[u], 1)
                    for u in range(U):
                        pe.wait_ge(xa_ready[u], i * 2 + 2)
                        turn(u, normed[u], xa_turned)
                    for u in range(U):
                        pe.wait_ge(xa_cols_ready[u], i + 1)
                        pe.wait_ge(logits_saved[u], i + 1)
                        for j in range(NT):
                            last = pe.matmul(bank(u, 0, T + j * E, T + (j + 1) * E),
                                             xa_cols[u][:, j * P:(j + 1) * P], router_w[:, :],
                                             start=True, stop=True)
                        last.then_inc(logits_ready[u], 1)

            @block.scalar
            def _(act):
                with act.Fori(0, TURNS) as i:
                    for u in range(U):
                        act.wait_ge(turned[u], i * 2 + 1)
                        act.activation(h_cols[u][:, 1:T + 1], bank(u, 0, 0, T), ACT.Identity,
                                       bias=vec(V_B1), scale=vec(V_G1)).then_inc(h_ready[u], 1)
                    for u in range(U):
                        act.wait_ge(r_ready[u], i + 1)
                        act.activation(r_tanh[u][:, :], bank(u, 2, 0, T), ACT.Tanh, scale=0.5).then_inc(r_done[u], 1)
                    for u in range(U):
                        act.wait_ge(args_ready[u], i * 4 + 4)
                        act.activation(keep[u][:, :, :], above[u][:, :, :], ACT.Exp, scale=-1.0
                                       ).then_inc(exps_ready[u], 1)
                        act.activation(take[u][:, :, :], below[u][:, :, :], ACT.Exp).then_inc(exps_ready[u], 1)
                    for u in range(U):
                        act.wait_ge(turned[u], i * 2 + 2)
                        act.activation(h_cols[u][:, 1:T + 1], bank(u, 0, 0, T), ACT.Identity,
                                       bias=vec(V_B2), scale=vec(V_G2)).then_inc(h_ready[u], 1)
                    for u in range(U):
                        for half in range(2):
                            act.wait_ge(kc_ready[u], i * HC + (half + 1) * HC // 2)
                            act.activation(k_relu[u][:, 2 * half:2 * half + 2, :],
                                           bank(u, 1 + half).rearrange("p (c t) -> p c t", t=T),
                                           ACT.Relu).then_inc(relu_ready[u], 1)
                        act.wait_ge(rc_ready[u], i + 1)
                        act.activation(rc_tanh[u][:, :, :],
                                       bank(u, 3, T, 2 * T).rearrange("p (j d) -> p j d", d=D),
                                       ACT.Tanh, scale=0.5).then_inc(rc_done[u], 1)
                    for u in range(U):
                        act.wait_ge(xa_turned[u], i + 1)
                        act.activation(xa_cols[u][:, :], bank(u, 0, 0, T), ACT.Copy).then_inc(xa_cols_ready[u], 1)

            @block.gpsimd
            def _(pool):
                for u in range(U):
                    pool.memset(h_cols[u][:, 0:1], 0.0).then_inc(borders_set, 1)
                    pool.memset(peak[u][:, 0:1], -1e38).then_inc(borders_set, 1)
                    pool.memset(state[u][:, :, 0:1], 0.0).then_inc(borders_set, 1)

                with pool.Fori(0, TURNS) as i:
                    c = Chain(pool, pool_rwkv, i, 6)

                    def rstds(u, k, e):
                        pool.wait_ge(var_ready[u], i * 6 + 2 * k)
                        c.step(pool.tensor_tensor(rstd[u][:, :], mean_var[u][:, :, 1], eps[:, e, :], ALU.add))
                        c.wait()
                        pool.tensor_tensor(rstd[u][:, :], rstd[u][:, :], neg_half[:, 0:NT], ALU.pow
                                           ).then_inc(rstd_ready[u], 1)

                    for u in range(U):
                        rstds(u, 1, EPS_TM)
                    for u in range(U):
                        rstds(u, 2, EPS_TM)
                        pool.wait_ge(x1_ready[u], i + 1)
                        pool.tensor_tensor(x01[u][:, :, :], x0[u][:, :, :], x1[u][:, :, :], ALU.add
                                           ).then_inc(x01_ready[u], 1)
                    for u in range(U):
                        for half in range(2):
                            pool.wait_ge(relu_ready[u], i * 2 + half + 1)
                            k = k_relu[u][:, 2 * half:2 * half + 2, :]
                            pool.tensor_tensor(k_sq[u][:, 2 * half:2 * half + 2, :], k, k, ALU.mult
                                               ).then_inc(sq_ready[u], 1)
                    for u in range(U):
                        rstds(u, 3, EPS_LN)
                    c.close()

            @block.vector
            def _(dve):
                dve.wait_ge(borders_set, 3 * U)
                dve.wait_ge(rows_in_sem, 32)
                for u in range(U):
                    dve.sem_inc(x_free[u], 1)
                    dve.sem_inc(logits_saved[u], 1)
                with dve.Fori(0, TURNS) as i:
                    c = Chain(dve, vec_rwkv, i, 40)

                    def normalise(u, k, src, dst, done):
                        dve.wait_ge(rstd_ready[u], i * 3 + k)
                        for j in range(NT):
                            dve.tensor_scalar(dst[j], src[j], mean_var[u][:, j, 0:1], rstd[u][:, j:j + 1],
                                              ALU.subtract, ALU.mult).then_inc(done[u], 1)

                    for u in range(U):
                        dve.wait_ge(x_loaded[u], i * 16 + 16)
                        stats(dve, c, i, [x0[u][:, j, :] for j in range(NT)], u)
                    for u in range(U):
                        normalise(u, 1, [x0[u][:, j, :] for j in range(NT)],
                                  [normed[u][:, j, :] for j in range(NT)], normed_ready)

                    for u in range(U):
                        key = bank(u, 1, 0, T)
                        before = peak[u][:, 0:T]
                        dve.wait_ge(kv_ready[u], i + 1)
                        c.step(dve.tensor_tensor_scan(peak[u][:, 1:T + 1], NEG_W.to_broadcast([P, T]), key,
                                                      -1e38, ALU.add, ALU.max))
                        c.wait()
                        k = c.step(dve.scalar_tensor_tensor(delta[u][:, :], key, vec(V_FIRST), before,
                                                            ALU.add, ALU.subtract))
                        c.wait(k)
                        for dst, op in ((above, ALU.max), (below, ALU.min)):
                            dve.tensor_scalar(dst[u][:, 0, :], delta[u][:, :], 0.0, None, op
                                              ).then_inc(args_ready[u], 1)
                            dve.tensor_scalar(dst[u][:, 1, :], delta[u][:, :], U_PLUS_W, 0.0,
                                              ALU.subtract, op).then_inc(args_ready[u], 1)
                    for u in range(U):
                        v = bank(u, 1, T, 2 * T)
                        dve.wait_ge(exps_ready[u], i * 2 + 2)
                        k = c.step(dve.tensor_tensor(taken[u][:, :], take[u][:, 1, :], v, ALU.mult))
                        bb = c.step(dve.tensor_tensor_scan(state[u][:, 1, 1:T + 1], keep[u][:, 1, :],
                                                           take[u][:, 1, :], 0.0, ALU.mult, ALU.add))
                        c.wait(k)
                        aa = c.step(dve.tensor_tensor_scan(state[u][:, 0, 1:T + 1], keep[u][:, 1, :],
                                                           taken[u][:, :], 0.0, ALU.mult, ALU.add))
                        vv = c.step(dve.tensor_tensor(value[u][:, :], take[u][:, 0, :], v, ALU.mult))
                        c.wait(bb)
                        den = c.step(dve.tensor_tensor(frac[u][:, 1, :], keep[u][:, 0, :],
                                                       state[u][:, 1, 0:T], ALU.mult))
                        c.wait(aa)
                        num = c.step(dve.tensor_tensor(frac[u][:, 0, :], keep[u][:, 0, :],
                                                       state[u][:, 0, 0:T], ALU.mult))
                        c.wait(den)
                        den = c.step(dve.tensor_tensor(frac[u][:, 1, :], frac[u][:, 1, :],
                                                       take[u][:, 0, :], ALU.add))
                        c.wait(num)
                        num = c.step(dve.tensor_tensor(frac[u][:, 0, :], frac[u][:, 0, :],
                                                       value[u][:, :], ALU.add))
                        c.wait(den)
                        rec = c.step(dve.reciprocal(recip[u][:, :], frac[u][:, 1, :]))
                        dve.wait_ge(r_done[u], i + 1)
                        c.wait(num)
                        num = c.step(dve.scalar_tensor_tensor(frac[u][:, 0, :], r_tanh[u][:, :], 1.0,
                                                              frac[u][:, 0, :], ALU.add, ALU.mult))
                        c.wait(num)
                        dve.scalar_tensor_tensor(y_cols[u][:, :], frac[u][:, 0, :], 0.5, recip[u][:, :],
                                                 ALU.mult, ALU.mult).then_inc(y_ready[u], 1)
                    for u in range(U):
                        dve.wait_ge(wo_ready[u], i + 1)
                        dve.tensor_tensor(x1[u][:, :, :], x0[u][:, :, :],
                                          bank(u, 3, 0, T).rearrange("p (j d) -> p j d", d=D),
                                          ALU.add).then_inc(x1_ready[u], 1)
                        dve.wait_ge(x1_ready[u], i + 1)
                        stats(dve, c, i, [x1[u][:, j, :] for j in range(NT)], u)
                    for u in range(U):
                        normalise(u, 2, [x1[u][:, j, :] for j in range(NT)],
                                  [normed[u][:, j, :] for j in range(NT)], normed_ready)
                    for u in range(U):
                        dve.wait_ge(rc_done[u], i + 1)
                        dve.wait_ge(cv_ready[u], i + 1)
                        c.step(dve.scalar_tensor_tensor(
                            gated[u][:, :, :], rc_tanh[u][:, :, :], 1.0,
                            bank(u, 3, 0, T).rearrange("p (j d) -> p j d", d=D), ALU.add, ALU.mult))
                        dve.wait_ge(x01_ready[u], i + 1)
                        c.wait()
                        c.step(dve.scalar_tensor_tensor(gated[u][:, :, :], gated[u][:, :, :], 0.5,
                                                        x01[u][:, :, :], ALU.mult, ALU.add))
                        c.wait()
                        stats(dve, c, i, [gated[u][:, j, :] for j in range(NT)], u)
                    for u in range(U):
                        normalise(u, 3, [gated[u][:, j, :] for j in range(NT)],
                                  [normed[u][:, j, :] for j in range(NT)], xa_ready)
                        dve.wait_ge(xa_ready[u], i * 2 + 2)
                        dve.tensor_copy(xa[:, bass.ds((i * U + u) * NT, NT), :], normed[u][:, :, :]
                                        ).then_inc(x_free[u], 1)
                    for u in range(U):
                        dve.wait_ge(logits_ready[u], i + 1)
                        dve.tensor_tensor(logits[:, bass.ds((i * U + u) * NT, NT), :],
                                          bank(u, 0, T, T + NT * E).rearrange("p (j e) -> p j e", e=E),
                                          router_b[:, :].unsqueeze(1).to_broadcast([P, NT, E]),
                                          ALU.add).then_inc(logits_saved[u], 1)
                    c.close()

        rw.close()
        layer0.close()

        route = ExitStack()

        best = sb("best", [P, TILES], scope=route)
        candidate = sb("candidate", [P, TILES, E], scope=route)
        chosen = sb("chosen", [P, TILES, E], scope=route)
        chosen_bf = sb("chosen_bf", [P, TILES, E], BF16, scope=route)
        upper_bf = sb("upper_bf", [P, P], BF16, scope=route)
        in_tile = sb("in_tile", [P, E, TILES], scope=route)
        so_far = sb("so_far", [P, E, TILES], scope=route)
        more_than = sb("more_than", [P, E, TILES], scope=route)
        tiles_of = sb("tiles_of", [P, E], scope=route)
        tiles_end = sb("tiles_end", [P, E], scope=route)
        first_row = sb("first_row", [P, E], scope=route)
        place = sb("place", [P, TILES, E], scope=route)
        place_sum = sb("place_sum", [P, TILES], scope=route)
        ended = sb("ended", [P, XTILES, E], scope=route)
        expert_f = sb("expert_f", [P, XTILES], scope=route)

        vec_route = sem("vec_route", rwkv_sems)
        chosen_ready = sem("chosen_ready", rwkv_sems)
        counts_ready = sem("counts_ready", rwkv_sems)
        places_ready = sem("places_ready", rwkv_sems)

        rank = banks[:, 0, 0:TILES * E].rearrange("p (t e) -> p t e", e=E)
        count = banks[:, 1, 0:TILES * E].rearrange("p (t e) -> p t e", e=E)
        preference = consts[:, C_FIRST:C_FIRST + E]
        tile_number = consts[:, C_TILE:C_TILE + XTILES]
        full_tiles = consts[:, C_COUNT:C_COUNT + TILES]
        restart = consts[:, C_RESET:C_RESET + E * TILES]

        with nc.Block() as block:

            @block.vector
            def _(dve):
                c = Chain(dve, vec_route)

                def then(ins):
                    c.wait(c.step(ins))

                wide = [P, TILES, E]
                then(dve.tensor_copy(upper_bf[:, :], consts[:, C_UPPER:C_UPPER + P]))
                then(dve.tensor_reduce(best[:, :], logits[:, :, :], AX, ALU.max))
                then(dve.tensor_tensor(candidate[:, :, :], logits[:, :, :],
                                       best[:, :].unsqueeze(2).to_broadcast(wide), ALU.is_ge))
                then(dve.tensor_tensor(candidate[:, :, :], candidate[:, :, :],
                                       preference.unsqueeze(1).to_broadcast(wide), ALU.mult))
                then(dve.tensor_reduce(best[:, :], candidate[:, :, :], AX, ALU.max))
                then(dve.tensor_tensor(chosen[:, :, :], best[:, :].unsqueeze(2).to_broadcast(wide),
                                       preference.unsqueeze(1).to_broadcast(wide), ALU.is_equal))
                dve.tensor_copy(chosen_bf[:, :, :], chosen[:, :, :]).then_inc(chosen_ready, 1)
                dve.wait_ge(counts_ready, 1)
                then(dve.tensor_copy(in_tile[:, :, :], count.rearrange("p t e -> p e t")))
                then(dve.tensor_tensor_scan(so_far[:, :, :].rearrange("p e t -> p (e t)"), restart,
                                            in_tile[:, :, :].rearrange("p e t -> p (e t)"),
                                            0.0, ALU.mult, ALU.add))
                then(dve.tensor_tensor(more_than[:, :, :],
                                       so_far[:, :, TILES - 1:TILES].to_broadcast([P, E, TILES]),
                                       full_tiles.unsqueeze(1).to_broadcast([P, E, TILES]), ALU.is_gt))
                then(dve.tensor_reduce(tiles_of[:, :], more_than[:, :, :], AX, ALU.add))
                then(dve.tensor_tensor_scan(tiles_end[:, :], restart[:, 1:1 + E], tiles_of[:, :],
                                            0.0, ALU.mult, ALU.add))
                then(dve.tensor_tensor(first_row[:, :], tiles_end[:, :], tiles_of[:, :], ALU.subtract))
                then(dve.tensor_scalar(first_row[:, :], first_row[:, :], float(P), None, ALU.mult))
                then(dve.tensor_tensor(so_far[:, :, :], so_far[:, :, :], in_tile[:, :, :], ALU.subtract))
                then(dve.tensor_tensor(place[:, :, :], rank, so_far[:, :, :].rearrange("p e t -> p t e"), ALU.add))
                then(dve.tensor_tensor(place[:, :, :], place[:, :, :],
                                       first_row[:, :].unsqueeze(1).to_broadcast(wide), ALU.add))
                then(dve.tensor_tensor(place[:, :, :], place[:, :, :], chosen[:, :, :], ALU.mult))
                then(dve.tensor_reduce(place_sum[:, :], place[:, :, :], AX, ALU.add))
                dve.tensor_copy(slot_of[:, :], place_sum[:, :]).then_inc(places_ready, 1)
                then(dve.tensor_tensor(ended[:, :, :], tiles_end[:, :].unsqueeze(1).to_broadcast([P, XTILES, E]),
                                       tile_number.unsqueeze(2).to_broadcast([P, XTILES, E]), ALU.is_le))
                then(dve.tensor_reduce(expert_f[:, :], ended[:, :, :], AX, ALU.add))
                then(dve.tensor_scalar(expert_f[:, :], expert_f[:, :], float(E - 1), None, ALU.min))
                then(dve.tensor_copy(tile_expert[:, :], expert_f[:, :]))

            @block.tensor
            def _(pe):
                flat = chosen_bf[:, :, :].rearrange("p t e -> p (t e)")
                pe.wait_ge(chosen_ready, 1)
                pe.matmul(banks[:, 0, 0:TILES * E], upper_bf[:, :], flat, start=True, stop=True)
                pe.matmul(banks[:, 1, 0:TILES * E], ones_bf[:, :], flat, start=True, stop=True
                          ).then_inc(counts_ready, 1)

            @block.gpsimd
            def _(pool):
                pool.wait_ge(places_ready, 1)
                pool.wait_ge(zeroed_sem, 16)
                for t in range(TILES):
                    pool.indirect_dma_start(sorted_x, bass.IndirectOffsetOnAxis(ap=slot_of[:, t:t + 1], axis=0),
                                            xa[:, t, :], None).then_inc(scattered, 16)

        route.close()

        ex = ExitStack()

        def bufs(name, shape, dt=F32, scope=ex):
            return [sb(f"{name}{u}", shape, dt, scope) for u in range(U)]

        xg = bufs("xg", [P, D])
        xg_cols = bufs("xg_cols", [P, P])
        gate = bufs("gate", [P, XH])
        hidden = bufs("hidden", [P, XH])
        hidden_cols = bufs("hidden_cols", [P, XC, P])
        y_rows = bufs("y_rows", [P, D])

        xg_loaded = pair("xg_loaded", expert_sems)
        xg_turned = pair("xg_turned", expert_sems)
        xg_cols_ready = pair("xg_cols_ready", expert_sems)
        lin_ready = pair("lin_ready", expert_sems)
        gate_in_ready = pair("gate_in_ready", expert_sems)
        gate_ready = pair("gate_ready", expert_sems)
        hidden_ready = pair("hidden_ready", expert_sems)
        hidden_turned = pair("hidden_turned", expert_sems)
        hidden_cols_ready = pair("hidden_cols_ready", expert_sems)
        down_ready = pair("down_ready", expert_sems)
        y_rows_ready = pair("y_rows_ready", expert_sems)

        with nc.Block() as block:

            @block.gpsimd
            def _(pool):
                for used in used_semaphores:
                    pool.sem_clear(used)

            @block.sync
            def _(sp):
                sp.wait_ge(scattered, 16 * TILES)
                with sp.Fori(0, XTILES // U) as i:
                    for u in range(U):
                        sp.wait_ge(xg_turned[u], i + 1)
                        sp.dma_start(xg[u][:, :], sorted_x[bass.ds((i * U + u) * P, P), :]
                                     ).then_inc(xg_loaded[u], 16)

            @block.tensor
            def _(pe):
                pe.wait_ge(expert_w_sem, 32)
                pe.wait_ge(biases_sem, 16)
                ones = ones_bf[0:3, :]
                for u in range(U):
                    pe.sem_inc(xg_turned[u], 1)
                with pe.Fori(0, XTILES // U) as i:
                    e = [pe.value_load(tile_expert[0:1, bass.ds(i * U + u, 1)], min_val=0, max_val=E - 1)
                         for u in range(U)]
                    for u in range(U):
                        pe.wait_ge(xg_loaded[u], i * 16 + 16)
                        pe.wait_ge(y_rows_ready[u], i + 1)
                        pe.transpose(bank(u, 0, 0, P), xg[u][:, :], ident).then_inc(xg_turned[u], 1)
                    for u in range(U):
                        pe.wait_ge(xg_cols_ready[u], i + 1)
                        for k, lo, done in ((2, XH, gate_in_ready), (1, 0, lin_ready)):
                            pe.matmul(bank(u, k), ones, biases[:, bass.ds(e[u], 1), lo:lo + XH].squeeze(1),
                                      start=True, stop=False)
                            pe.matmul(bank(u, k), xg_cols[u][:, :], w1[:, bass.ds(e[u], 1), lo:lo + XH].squeeze(1),
                                      start=False, stop=True).then_inc(done[u], 1)
                    for u in range(U):
                        pe.wait_ge(hidden_ready[u], i + 1)
                        for c in range(XC):
                            last = pe.transpose(bank(u, 3, c * P, (c + 1) * P),
                                                hidden[u][:, c * P:(c + 1) * P], ident)
                        last.then_inc(hidden_turned[u], 1)
                    for u in range(U):
                        pe.wait_ge(hidden_cols_ready[u], i + 1)
                        dst = bank(u, 0, P, P + D)
                        pe.matmul(dst, ones, biases[:, bass.ds(e[u], 1), GLU:GLU + D].squeeze(1),
                                  start=True, stop=False)
                        for c in range(XC):
                            last = pe.matmul(dst, hidden_cols[u][:, c, :],
                                             w2[:, bass.ds(e[u], 1), c, :].squeeze(1),
                                             start=False, stop=(c == XC - 1))
                        last.then_inc(down_ready[u], 1)

            @block.scalar
            def _(act):
                with act.Fori(0, XTILES // U) as i:
                    for u in range(U):
                        act.wait_ge(xg_turned[u], i + 2)
                        act.activation(xg_cols[u][:, :], bank(u, 0, 0, P), ACT.Copy).then_inc(xg_cols_ready[u], 1)
                    for u in range(U):
                        act.wait_ge(gate_in_ready[u], i + 1)
                        act.activation(gate[u][:, :], bank(u, 2), ACT.Sigmoid).then_inc(gate_ready[u], 1)
                    for u in range(U):
                        act.wait_ge(hidden_turned[u], i + 1)
                        act.activation(hidden_cols[u][:, :, :].rearrange("p c t -> p (c t)"), bank(u, 3), ACT.Copy
                                       ).then_inc(hidden_cols_ready[u], 1)
                    for u in range(U):
                        act.wait_ge(y_rows_ready[u], i + 2)
                        act.dma_start(sorted_y[bass.ds((i * U + u) * P, P), :], y_rows[u][:, :]
                                      ).then_inc(y_stored[u], 16)

            @block.vector
            def _(dve):
                for u in range(U):
                    dve.sem_inc(y_rows_ready[u], 1)
                    dve.sem_inc(y_stored[u], 16)
                with dve.Fori(0, XTILES // U) as i:
                    for u in range(U):
                        dve.wait_ge(gate_ready[u], i + 1)
                        dve.wait_ge(lin_ready[u], i + 1)
                        dve.tensor_tensor(hidden[u][:, :], gate[u][:, :], bank(u, 1), ALU.mult
                                          ).then_inc(hidden_ready[u], 1)
                    for u in range(U):
                        dve.wait_ge(down_ready[u], i + 1)
                        dve.wait_ge(y_stored[u], i * 16 + 16)
                        dve.tensor_copy(y_rows[u][:, :], bank(u, 0, P, P + D)).then_inc(y_rows_ready[u], 1)

        ex.close()
        rwkv_sems.close()

        with nc.Block() as block:

            @block.gpsimd
            def _(pool):
                for used in expert_semaphores[0::2]:
                    pool.sem_clear(used)

            @block.vector
            def _(dve):
                for used in expert_semaphores[1::2]:
                    dve.sem_clear(used)

        expert_sems.close()

        l1 = ExitStack()

        def bufs(name, shape, dt=F32, scope=l1):
            return [sb(f"{name}{u}", shape, dt, scope) for u in range(U)]

        w_qkv = sb("w_qkv", [P, 3 * D], scope=l1)
        w_out = sb("w_out", [P, D], scope=l1)
        ffn_w1 = sb("ffn_w1", [P, HID], scope=l1)
        ffn_w2 = sb("ffn_w2", [P, HC, D], scope=l1)
        slot_rows = sb("slot_rows", [P, SC, D], scope=l1)
        slot_sq = sb("slot_sq", [P, SC, 2], scope=l1)
        slot_cols = sb("slot_cols", [P, SLOTS], scope=l1)
        square_junk = sb("square_junk", [P, D], scope=l1)

        y_idx = bufs("y_idx", [P, NT], I32)
        y_got = bufs("y_got", [P, NT, D])
        summed = bufs("summed", [P, NT, D])
        moments = bufs("moments_a", [P, NT, 6])
        mean_var = bufs("mean_var_a", [P, NT, 2])
        rstd = bufs("rstd_a", [P, NT])
        summed_e = bufs("summed_e", [P, NT, D])
        moments_e = bufs("moments_e", [P, NT, 6])
        mean_var_e = bufs("mean_var_e", [P, NT, 2])
        rstd_e = bufs("rstd_e", [P, NT])
        x_kept = bufs("x_kept", [P, NT, D])
        summed_b = bufs("summed_b", [P, NT, D])
        moments_b = bufs("moments_b", [P, NT, 6])
        mean_var_b = bufs("mean_var_b", [P, NT, 2])
        rstd_b = bufs("rstd_b", [P, NT])
        xb = bufs("xb", [P, NT, D])
        xb_bias = bufs("xb_bias", [P, NT, D])
        cols = bufs("cols", [P, T])
        junk = bufs("junk", [P, D])
        qk_sq = bufs("qk_sq", [P, 2 * NT])
        qk_rms = bufs("qk_rms", [P, 2 * NT])
        q_rows = bufs("q_rows", [P, NT, D])
        q_cols = bufs("q_cols", [P, T])
        k_rows = bufs("k_rows", [P, NT, D])
        v_rows = bufs("v_rows", [P, NT, N129])
        kv_heads = bufs("kv_heads", [P, D + HEADS])
        norm_inv = bufs("norm_inv", [P, NT, HEADS])
        att = bufs("att", [P, NT, D])
        att_cols = bufs("att_cols", [P, T])
        xc = bufs("xc", [P, NT, D])
        xc_sq = bufs("xc_sq", [P, NT])
        xc_rms = bufs("xc_rms", [P, NT])
        xn = bufs("xn", [P, NT, N129])
        xn_cols = bufs("xn_cols", [P, T])
        slot_peak = bufs("slot_peak", [P, SC], BF16)
        token_peak = bufs("token_peak", [P, NT], BF16)
        slot_shift = bufs("slot_shift", [SC, SC, P], BF16)
        token_shift = bufs("token_shift", [NT, NT, P], BF16)
        dispatch = bufs("dispatch", [P, NT, SLOTS])
        combine = bufs("combine", [P, SC, T])
        slot_inv = bufs("slot_inv", [P, SC])
        slots_n = bufs("slots_n", [P, SC, D])
        slots_cols = bufs("slots_cols", [P, SLOTS])
        act_cols = bufs("act_cols", [P, HC, SLOTS])
        processed = bufs("processed", [P, SC, N129])
        out_inv = bufs("out_inv", [P, NT])
        final = bufs("final", [P, NT, D])
        ident_bf = sb("ident_bf", [P, P], BF16, scope=l1)

        slot_sq_ready = sem("slot_sq_ready", l1)
        slot_rms_ready = sem("slot_rms_ready", l1)
        slot_rows_ready = sem("slot_rows_ready", l1)
        slot_turned = sem("slot_turned", l1)
        slot_cols_ready = sem("slot_cols_ready", l1)
        ones_set = sem("ones_set", l1)
        mix_read = sem("mix_read", l1)
        vec_slots = sem("vec_slots", l1)
        pool_slots = sem("pool_slots", l1)
        vec_a, vec_f, vec_b = pair("vec_a", l1), pair("vec_f", l1), pair("vec_b", l1)
        pool_a, pool_b, pool_e = pair("pool_a", l1), pair("pool_b", l1), pair("pool_e", l1)
        vec_e = pair("vec_e", l1)
        names = """idx_ready y_gathered var_a rstd_a var_b rstd_b var_e rstd_e kept mix_added xb_ready xb_bias_ready xb_turned xb_cols_ready
            qk_ready qk_sq_ready qk_rms_ready q_rows_ready k_rows_ready v_rows_ready
            q_turned q_cols_ready kv_sum_ready kv_heads_ready att_ready att_rows_ready att_turned
            att_cols_ready wout_ready xc_ready xc_sq_ready xc_rms_ready xn_ready xn_turned
            xn_cols_ready by_slot_ready slot_peak_ready slot_peak_turned slot_shift_ready
            by_token_ready token_peak_ready by_token_shifted dispatch_ready token_peak_turned
            token_shift_ready by_slot_shifted combine_ready slots_ready slots_n_ready slots_turned
            slots_cols_ready hid_ready gelu_ready proc_ready processed_ready mix_ready
            final_ready final_stored""".split()
        S = {n: pair(n, l1) for n in names}

        STEPS_LOOPED = 2 * ((SEQ - 4) // 2)
        last_looped = STEPS_LOOPED

        def pipeline(eng, step):
            def place(turn, k):
                return k % 2, turn + k // 2

            for s in range(-3, 1):
                step(lambda k, s=s: place(0, s + k), live(s))
            with eng.Fori(0, STEPS_LOOPED // 2) as i:
                for s in (1, 2):
                    step(lambda k, s=s: place(i, s + k), "GEAFB")
            for s in range(last_looped + 1, SEQ + 1):
                step(lambda k, s=s: place(0, s + k), live(s))

        def live(s):
            return "".join(part for part, k in (("G", 3), ("E", 2), ("A", 1), ("F", 0), ("B", -1)) if 0 <= s + k < SEQ)

        def tile_of(u, n):
            return bass.ds((n * 2 + u) * NT, NT)

        LT, L = banks[:, 2:4, :], banks[:, 4:6, :]

        def by_slot(s):
            return banks[:, 2 + s // 2, (s % 2) * T:(s % 2 + 1) * T]

        peak_turned = banks[:, 5, 0:P // 2].bitcast(BF16)
        token_turned = banks[:, 4, 0:P // 2].bitcast(BF16)

        with nc.Block() as block:

            @block.sync
            def _(sp):
                sp.dma_start(w_qkv[:, :], w["W_qkv"]).then_inc(layer1_w_sem, 16)
                sp.dma_start(w_out[:, :], w["W_out"]).then_inc(layer1_w_sem, 16)
                sp.dma_start(ffn_w1[:, :], w["ffn_w1"]).then_inc(layer1_w_sem, 16)
                sp.dma_start(ffn_w2[:, :, :], w["ffn_w2"].rearrange("(c p) d -> p c d", p=P)).then_inc(layer1_w_sem, 16)
                sp.dma_start(slot_rows[:, :, :], w["slots"].rearrange("(c p) d -> p c d", p=P)).then_inc(layer1_w_sem, 16)

                def step(at, parts):
                    if "B" in parts:
                        u, n = at(-1)
                        sp.wait_ge(S["final_ready"][u], n * NT + NT)
                        sp.dma_start(out_rows[bass.ds(n * 2 + u, 1)].squeeze(0), final[u][:, :, :]
                                     ).then_inc(S["final_stored"][u], 16)

                pipeline(sp, step)
                for u in range(U):
                    sp.wait_ge(S["final_stored"][u], 16 + 16 * TURNS)

            @block.tensor
            def _(pe):
                def turn(dst, src, u, done):
                    for j in range(NT):
                        last = pe.transpose(dst[:, j * P:(j + 1) * P], src[u][:, j, 0:D], ident)
                    last.then_inc(S[done][u], 1)

                def step(at, parts):
                    a, f, b = "A" in parts, "F" in parts, "B" in parts
                    ua, na = at(1)
                    uf, nf = at(0)
                    ub, nb = at(-1)

                    def hidden_chunks(chunks):
                        for c in chunks:
                            if c >= 2:
                                pe.wait_ge(S["gelu_ready"][ub], nb * HC + c - 1)
                            pe.matmul(banks[:, 6 + c % 2, :], ffn_w1[:, c * P:(c + 1) * P], slots_cols[ub][:, :],
                                      start=True, stop=True).then_inc(S["hid_ready"][ub], 1)

                    def process(slots):
                        for s in slots:
                            for c in range(HC):
                                last = pe.matmul(banks[:, 6, s * D:(s + 1) * D], act_cols[ub][:, c, s * P:(s + 1) * P],
                                                 ffn_w2[:, c, :], start=(c == 0), stop=(c == HC - 1))
                        return last

                    if a:
                        pe.wait_ge(S["xb_ready"][ua], na * NT + NT)
                        turn(banks[:, 0, :], xb, ua, "xb_turned")
                    if b:
                        pe.wait_ge(S["slots_cols_ready"][ub], nb + 1)
                        pe.wait_ge(mix_read, nb * 2 + ub + 1)
                        hidden_chunks((0, 1))
                    if f:
                        pe.wait_ge(S["xn_ready"][uf], nf * NT + NT)
                        turn(banks[:, 4, :], xn, uf, "xn_turned")
                    if a:
                        pe.wait_ge(S["xb_cols_ready"][ua], na + 1)
                        for j in range(NT):
                            last = pe.matmul(banks[:, j, 0:3 * D], cols[ua][:, j * P:(j + 1) * P], w_qkv[:, :],
                                             start=True, stop=True)
                        last.then_inc(S["qk_ready"][ua], 1)
                    if f:
                        pe.wait_ge(S["xn_cols_ready"][uf], nf + 1)
                        for s in range(SC):
                            last = pe.matmul(by_slot(s), slot_cols[:, s * P:(s + 1) * P], xn_cols[uf][:, :],
                                             start=(s % 2 == 0), stop=False, skip_group_check=True)
                        last.then_inc(S["by_slot_ready"][uf], 1)
                    if b:
                        hidden_chunks((2, 3))
                    if f:
                        pe.wait_ge(S["slot_peak_ready"][uf], nf + 1)
                        pe.transpose(peak_turned[0:SC, :], slot_peak[uf][:, :], ident_bf[:, :]
                                     ).then_inc(S["slot_peak_turned"][uf], 1)
                    if a:
                        pe.wait_ge(S["q_rows_ready"][ua], na * NT + NT)
                        pe.wait_ge(S["k_rows_ready"][ua], na + 1)
                        pe.wait_ge(S["v_rows_ready"][ua], na + 1)
                        turn(banks[:, 0, :], q_rows, ua, "q_turned")
                        for j in range(NT):
                            last = pe.matmul(banks[:, 1, 0:N129], k_rows[ua][:, j, :], v_rows[ua][:, j, :],
                                             start=(j == 0), stop=(j == NT - 1))
                        last.then_inc(S["kv_sum_ready"][ua], 1)
                    if f:
                        pe.wait_ge(S["slot_shift_ready"][uf], nf + 1)
                        for j in range(NT):
                            last = pe.matmul(banks[:, 4 + j, :], xn_cols[uf][:, j * P:(j + 1) * P], slot_cols[:, :],
                                             start=True, stop=False, skip_group_check=True)
                        last.then_inc(S["by_token_ready"][uf], 1)
                    if b:
                        pe.wait_ge(S["gelu_ready"][ub], nb * HC + HC)
                        process((0, 1))
                    if f:
                        pe.wait_ge(S["token_peak_ready"][uf], nf + 1)
                        for j in range(NT):
                            last = pe.matmul(banks[:, 4 + j, :], ones_bf[0:SC, :],
                                             slot_shift[uf][:, :, :].rearrange("c s p -> c (s p)"),
                                             start=False, stop=True, skip_group_check=True)
                        last.then_inc(S["by_token_shifted"][uf], 1)
                    if a:
                        pe.wait_ge(S["q_cols_ready"][ua], na + 1)
                        pe.wait_ge(S["kv_heads_ready"][ua], na * 2 + 2)
                        for j in range(NT):
                            last = pe.matmul(banks[:, 1, j * (D + HEADS):(j + 1) * (D + HEADS)],
                                             q_cols[ua][:, j * P:(j + 1) * P], kv_heads[ua][:, :],
                                             start=True, stop=True)
                        last.then_inc(S["att_ready"][ua], 1)
                    if b:
                        process((2, 3)).then_inc(S["proc_ready"][ub], 1)
                    if f:
                        pe.wait_ge(S["dispatch_ready"][uf], nf * NT + NT)
                        pe.transpose(token_turned[0:NT, :], token_peak[uf][:, :], ident_bf[:, :]
                                     ).then_inc(S["token_peak_turned"][uf], 1)
                    if a:
                        pe.wait_ge(S["att_rows_ready"][ua], na + 1)
                        turn(banks[:, 0, :], att, ua, "att_turned")
                    if b:
                        pe.wait_ge(S["processed_ready"][ub], nb + 1)
                        for j in range(NT):
                            for s in range(SC):
                                last = pe.matmul(banks[:, 7, j * N129:(j + 1) * N129],
                                                 combine[ub][:, s, j * P:(j + 1) * P], processed[ub][:, s, :],
                                                 start=(s == 0), stop=(s == SC - 1))
                        last.then_inc(S["mix_ready"][ub], 1)
                    if f:
                        pe.wait_ge(S["token_shift_ready"][uf], nf + 1)
                        shift = token_shift[uf][:, :, :].rearrange("c j p -> c (j p)")
                        for s in range(SC):
                            last = pe.matmul(by_slot(s), ones_bf[0:NT, :], shift,
                                             start=False, stop=True, skip_group_check=True)
                        last.then_inc(S["by_slot_shifted"][uf], 1)
                    if a:
                        pe.wait_ge(S["att_cols_ready"][ua], na + 1)
                        for j in range(NT):
                            last = pe.matmul(banks[:, 1, j * D:(j + 1) * D],
                                             att_cols[ua][:, j * P:(j + 1) * P], w_out[:, :],
                                             start=True, stop=True)
                        last.then_inc(S["wout_ready"][ua], 1)
                    if f:
                        for s in range(SC):
                            dst = banks[:, 4 + s // 2, P + (s % 2) * N129:P + (s % 2 + 1) * N129]
                            for j in range(NT):
                                last = pe.matmul(dst, dispatch[uf][:, j, s * P:(s + 1) * P], xn[uf][:, j, :],
                                                 start=(j == 0), stop=(j == NT - 1))
                        last.then_inc(S["slots_ready"][uf], 1)
                    if f:
                        pe.wait_ge(S["slots_n_ready"][uf], nf + 1)
                        pe.wait_ge(S["combine_ready"][uf], nf + 1)
                        for s in range(SC):
                            last = pe.transpose(banks[:, 2, s * P:(s + 1) * P], slots_n[uf][:, s, :], ident)
                        last.then_inc(S["slots_turned"][uf], 1)


                pe.wait_ge(slot_rows_ready, SC)
                for s in range(SC):
                    last = pe.transpose(banks[:, 0, s * P:(s + 1) * P], slot_rows[:, s, :], ident)
                last.then_inc(slot_turned, 1)
                pe.wait_ge(slot_cols_ready, 1)
                pe.wait_ge(layer1_w_sem, 16 * 5)
                pipeline(pe, step)

            @block.scalar
            def _(act):
                act.wait_ge(layer1_w_sem, 16 * 5)
                for s in range(SC):
                    act.activation(square_junk[:, :], slot_rows[:, s, :], ACT.Square,
                                   accum_out=slot_sq[:, s, 0:1]).then_inc(slot_sq_ready, 1)
                    act.wait_ge(slot_sq_ready, s + 1)
                act.wait_ge(slot_turned, 1)
                act.activation(slot_cols[:, :], banks[:, 0, :], ACT.Copy).then_inc(slot_cols_ready, 1)

                def step(at, parts):
                    a, f, b = "A" in parts, "F" in parts, "B" in parts
                    ua, na = at(1)
                    uf, nf = at(0)
                    ub, nb = at(-1)

                    def gelus(chunks):
                        for c in chunks:
                            act.wait_ge(S["hid_ready"][ub], nb * HC + c + 1)
                            act.activation(act_cols[ub][:, c, :], banks[:, 6 + c % 2, :], ACT.Gelu
                                           ).then_inc(S["gelu_ready"][ub], 1)

                    if a:
                        act.wait_ge(S["xb_turned"][ua], na + 1)
                        act.activation(cols[ua][:, :], banks[:, 0, 0:T], ACT.Copy).then_inc(S["xb_cols_ready"][ua], 1)
                    if b:
                        gelus((0, 1))
                    if f:
                        act.wait_ge(S["xn_turned"][uf], nf + 1)
                        act.activation(xn_cols[uf][:, :], banks[:, 4, 0:T], ACT.Copy).then_inc(S["xn_cols_ready"][uf], 1)
                    if a:
                        act.wait_ge(S["qk_ready"][ua], na + 1)
                        act.activation(v_rows[ua][:, :, 0:D], banks[:, 0:2, 2 * D:3 * D], ACT.Copy
                                       ).then_inc(S["v_rows_ready"][ua], 1)
                        for j in range(NT):
                            for m in range(2):
                                n = m * NT + j
                                act.activation(junk[ua][:, :], banks[:, j, m * D:(m + 1) * D], ACT.Square,
                                               accum_out=qk_sq[ua][:, n:n + 1]).then_inc(S["qk_sq_ready"][ua], 1)
                                act.wait_ge(S["qk_sq_ready"][ua], na * 2 * NT + j * 2 + m + 1)
                    if b:
                        gelus((2, 3))
                    if a:
                        act.wait_ge(S["q_turned"][ua], na + 1)
                        act.activation(q_cols[ua][:, :], banks[:, 0, 0:T], ACT.Relu, scale=vec(V_QN)
                                       ).then_inc(S["q_cols_ready"][ua], 1)
                    if f:
                        act.wait_ge(S["by_token_shifted"][uf], nf + 1)
                        for j in range(NT):
                            act.activation(dispatch[uf][:, j, :], banks[:, 4 + j, :], ACT.Exp
                                           ).then_inc(S["dispatch_ready"][uf], 1)
                    if a:
                        act.wait_ge(S["att_turned"][ua], na + 1)
                        act.activation(att_cols[ua][:, :], banks[:, 0, 0:T], ACT.Copy).then_inc(S["att_cols_ready"][ua], 1)
                    if f:
                        act.wait_ge(S["by_slot_shifted"][uf], nf + 1)
                        act.activation(combine[uf][:, :, :].rearrange("p (b c) t -> p b (c t)", b=2), LT, ACT.Exp
                                       ).then_inc(S["combine_ready"][uf], 1)
                    if a:
                        act.wait_ge(S["xc_ready"][ua], na * NT + NT)
                        for j in range(NT):
                            act.activation(junk[ua][:, :], xc[ua][:, j, :], ACT.Square,
                                           accum_out=xc_sq[ua][:, j:j + 1]).then_inc(S["xc_sq_ready"][ua], 1)
                            act.wait_ge(S["xc_sq_ready"][ua], na * NT + j + 1)
                    if f:
                        act.wait_ge(S["slots_turned"][uf], nf + 1)
                        act.activation(slots_cols[uf][:, :], banks[:, 2, :], ACT.Copy
                                       ).then_inc(S["slots_cols_ready"][uf], 1)

                pipeline(act, step)

            @block.gpsimd
            def _(pool):
                for u in range(U):
                    pool.memset(v_rows[u][:, :, D:D + 1], 1.0).then_inc(ones_set, 1)
                    pool.memset(xn[u][:, :, D:D + 1], 1.0).then_inc(ones_set, 1)
                    pool.memset(processed[u][:, :, D:D + 1], 1.0).then_inc(ones_set, 1)

                c = Chain(pool, pool_slots)
                pool.wait_ge(slot_sq_ready, SC)
                c.step(pool.tensor_scalar(slot_sq[:, :, 1], slot_sq[:, :, 0], 1e-24, 1.0 / D, ALU.max, ALU.mult))
                c.wait()
                pool.tensor_tensor(slot_sq[:, :, 0], slot_sq[:, :, 1], neg_half[:, 0:SC], ALU.pow
                                   ).then_inc(slot_rms_ready, 1)

                def gather(u, n):
                    settle(pool, S["idx_ready"][u], n + 1, pool_passed)
                    for j in range(NT):
                        pool.indirect_dma_start(y_got[u][:, j, :], None, sorted_y,
                                                bass.IndirectOffsetOnAxis(ap=y_idx[u][:, j:j + 1], axis=0)
                                                ).then_inc(S["y_gathered"][u], 16)

                def step(at, parts):
                    a, b = "A" in parts, "B" in parts
                    ua, na = at(1)

                    def to_rstd(u, var_sem, value, mv, dst, done, c):
                        pool.wait_ge(var_sem, value)
                        c.step(pool.tensor_tensor(dst[u][:, :], mv[u][:, :, 1], eps[:, EPS_LN, :], ALU.add))
                        c.wait()
                        pool.tensor_tensor(dst[u][:, :], dst[u][:, :], neg_half[:, 0:NT], ALU.pow).then_inc(done, 1)

                    if "G" in parts:
                        gather(*at(3))
                    if "F" in parts:
                        u, n = at(0)
                        pool.wait_ge(S["xc_ready"][u], n * NT + NT)
                        pool.wait_ge(S["mix_added"][u], n + 1)
                        pool.tensor_tensor(x_kept[u][:, :, :], xc[u][:, :, :], zeros[:, :].unsqueeze(1).to_broadcast([P, NT, D]),
                                           ALU.add).then_inc(S["kept"][u], 1)
                    if a:
                        c = Chain(pool, pool_a[ua], na, 3)
                        pool.wait_ge(S["xb_ready"][ua], na * NT + NT)
                        pool.tensor_tensor(xb_bias[ua][:, :, :], xb[ua][:, :, :],
                                           rows[:, R_BOUT, :].unsqueeze(1).to_broadcast([P, NT, D]), ALU.add
                                           ).then_inc(S["xb_bias_ready"][ua], 1)
                        settle(pool, S["qk_sq_ready"][ua], na * 2 * NT + 2 * NT, pool_passed)
                        c.step(pool.tensor_scalar(qk_rms[ua][:, :], qk_sq[ua][:, :], 1.0 / D, 1e-6,
                                                  ALU.mult, ALU.add))
                        c.wait()
                        pool.tensor_tensor(qk_rms[ua][:, :], qk_rms[ua][:, :], neg_half[:, 0:2 * NT], ALU.pow
                                           ).then_inc(S["qk_rms_ready"][ua], 1)
                    if "E" in parts:
                        u, n = at(2)
                        to_rstd(u, S["var_e"][u], n * NT + NT, mean_var_e, rstd_e, S["rstd_e"][u],
                                Chain(pool, pool_e[u], n, 1))
                    if a:
                        to_rstd(ua, S["var_a"][ua], na * NT + NT, mean_var, rstd, S["rstd_a"][ua], c)
                        settle(pool, S["xc_sq_ready"][ua], na * NT + NT, pool_passed)
                        c.step(pool.tensor_scalar(xc_rms[ua][:, :], xc_sq[ua][:, :], 1e-24, 1.0 / D,
                                                  ALU.max, ALU.mult))
                        c.wait()
                        pool.tensor_tensor(xc_rms[ua][:, :], xc_rms[ua][:, :], neg_half[:, 0:NT], ALU.pow
                                           ).then_inc(S["xc_rms_ready"][ua], 1)
                        c.close()
                    if b:
                        u, n = at(-1)
                        to_rstd(u, S["var_b"][u], n * NT + NT, mean_var_b, rstd_b, S["rstd_b"][u],
                                Chain(pool, pool_b[u], n, 1))

                for u in range(U):
                    pool.wait_ge(y_stored[u], 16 + 16 * (XTILES // U))
                pipeline(pool, step)

            @block.vector
            def _(dve):
                p = Chain(dve, vec_slots)
                p.step(dve.tensor_copy(ident_bf[:, :], ident))
                dve.wait_ge(slot_rms_ready, 1)
                for s in range(SC):
                    dve.scalar_tensor_tensor(slot_rows[:, s, :], slot_rows[:, s, :], slot_sq[:, s, 0:1],
                                             rows[:, R_GS, :], ALU.mult, ALU.mult).then_inc(slot_rows_ready, 1)
                dve.wait_ge(ones_set, 3 * U)
                p.wait()
                dve.sem_inc(mix_read, 1)
                for u in range(U):
                    dve.sem_inc(S["final_stored"][u], 16)
                    dve.sem_inc(S["mix_added"][u], 1)

                def stats_of(c, src, moments, mean_var, done):
                    for j in range(NT):
                        c.step(dve.bn_stats(moments[:, j, :], src[:, j, :]))
                    settle(dve, c.sem, c.turn * c.per_turn + c.n, vec_passed)
                    for j in range(NT):
                        dve.bn_aggr(mean_var[:, j, :], moments[:, j, :]).then_inc(done, 1)

                def normalised(dst, src, mean_var, rstd, done):
                    for j in range(NT):
                        dve.tensor_scalar(dst[:, j, :], src[:, j, :], mean_var[:, j, 0:1],
                                          rstd[:, j:j + 1], ALU.subtract, ALU.mult).then_inc(done, 1)

                def indices(u, n):
                    dve.tensor_copy(y_idx[u][:, :], slot_of[:, tile_of(u, n)]).then_inc(S["idx_ready"][u], 1)

                def step(at, parts):
                    a, f, b = "A" in parts, "F" in parts, "B" in parts
                    ua, na = at(1)
                    uf, nf = at(0)
                    ub, nb = at(-1)
                    ca = Chain(dve, vec_a[ua], na, 7)
                    cf = Chain(dve, vec_f[uf], nf, 1)
                    cb = Chain(dve, vec_b[ub], nb, 5)
                    e = "E" in parts
                    ue, ne = at(2)
                    ce = Chain(dve, vec_e[ue], ne, 3)
                    if "G" in parts:
                        indices(*at(3))
                    if f:
                        dve.wait_ge(S["by_slot_ready"][uf], nf + 1)
                        dve.tensor_reduce(slot_peak[uf][:, :], LT.rearrange("p b (c t) -> p (b c) t", t=T),
                                          AX, ALU.max, negate=True).then_inc(S["slot_peak_ready"][uf], 1)
                        dve.wait_ge(S["slot_peak_turned"][uf], nf + 1)
                        dve.tensor_tensor(slot_shift[uf][:, :, :],
                                          consts[0:SC, C_DIAG:C_DIAG + SC].unsqueeze(2).to_broadcast([SC, SC, P]),
                                          peak_turned[0:SC, :].unsqueeze(1).to_broadcast([SC, SC, P]),
                                          ALU.mult).then_inc(S["slot_shift_ready"][uf], 1)
                    if a:
                        dve.wait_ge(S["qk_rms_ready"][ua], na + 1)
                        for j in range(NT):
                            dve.tensor_scalar(q_rows[ua][:, j, :], banks[:, j, 0:D], qk_rms[ua][:, j:j + 1],
                                              None, ALU.mult).then_inc(S["q_rows_ready"][ua], 1)
                        for j in range(NT):
                            ca.step(dve.scalar_tensor_tensor(k_rows[ua][:, j, :], banks[:, j, D:2 * D],
                                                             qk_rms[ua][:, NT + j:NT + j + 1], rows[:, R_KN, :],
                                                             ALU.mult, ALU.mult))
                        ca.wait()
                        dve.tensor_scalar(k_rows[ua][:, :, :], k_rows[ua][:, :, :], 0.0, None, ALU.max
                                          ).then_inc(S["k_rows_ready"][ua], 1)
                    if e:
                        dve.wait_ge(S["y_gathered"][ue], ne * 16 * NT + 16 * NT)
                        ce.step(dve.tensor_tensor(summed_e[ue][:, :, :], xa[:, tile_of(ue, ne), :],
                                                  y_got[ue][:, :, :], ALU.add))
                        ce.wait()
                        stats_of(ce, summed_e[ue], moments_e[ue], mean_var_e[ue], S["var_e"][ue])
                        ce.close()
                    if f:
                        dve.wait_ge(S["by_token_ready"][uf], nf + 1)
                        dve.tensor_reduce(token_peak[uf][:, :], L, AX, ALU.max, negate=True
                                          ).then_inc(S["token_peak_ready"][uf], 1)
                    if a:
                        dve.wait_ge(S["kv_sum_ready"][ua], na + 1)
                        dve.tensor_tensor(kv_heads[ua][:, 0:D], consts[:, C_BLOCK:C_BLOCK + D], banks[:, 1, 0:D],
                                          ALU.mult).then_inc(S["kv_heads_ready"][ua], 1)
                        dve.tensor_scalar(kv_heads[ua][:, D:D + HEADS], consts[:, C_HEADS:C_HEADS + HEADS],
                                          banks[:, 1, D:D + 1], None, ALU.mult).then_inc(S["kv_heads_ready"][ua], 1)
                        o = banks[:, 1, 0:NT * (D + HEADS)].rearrange("p (j n) -> p j n", j=NT)
                        dve.wait_ge(S["att_ready"][ua], na + 1)
                        ca.step(dve.tensor_scalar(norm_inv[ua][:, :, :], o[:, :, D:D + HEADS], 1e-6, None, ALU.add))
                        ca.wait()
                        ca.step(dve.reciprocal(norm_inv[ua][:, :, :], norm_inv[ua][:, :, :]))
                        ca.wait()
                        dve.tensor_tensor(att[ua][:, :, :].rearrange("p j (h d) -> p j h d", d=DH),
                                          o[:, :, 0:D].rearrange("p j (h d) -> p j h d", d=DH),
                                          norm_inv[ua][:, :, :].unsqueeze(3).to_broadcast([P, NT, HEADS, DH]),
                                          ALU.mult).then_inc(S["att_rows_ready"][ua], 1)
                    if b:
                        dve.wait_ge(S["proc_ready"][ub], nb + 1)
                        dve.tensor_copy(processed[ub][:, :, 0:D], banks[:, 6, :].rearrange("p (s d) -> p s d", d=D)
                                        ).then_inc(S["processed_ready"][ub], 1)
                    if e:
                        dve.wait_ge(S["rstd_e"][ue], ne + 1)
                        normalised(xb[ue], summed_e[ue], mean_var_e[ue], rstd_e[ue], S["xb_ready"][ue])
                    if f:
                        dve.wait_ge(S["token_peak_turned"][uf], nf + 1)
                        dve.tensor_tensor(token_shift[uf][:, :, :],
                                          consts[0:NT, C_DIAG:C_DIAG + NT].unsqueeze(2).to_broadcast([NT, NT, P]),
                                          token_turned[0:NT, :].unsqueeze(1).to_broadcast([NT, NT, P]),
                                          ALU.mult).then_inc(S["token_shift_ready"][uf], 1)
                    if b:
                        o = banks[:, 7, 0:NT * N129].rearrange("p (j n) -> p j n", n=N129)
                        dve.wait_ge(S["mix_ready"][ub], nb + 1)
                        dve.wait_ge(S["kept"][ub], nb + 1)
                        cb.step(dve.reciprocal(out_inv[ub][:, :], o[:, :, D]))
                        cb.wait()
                        for j in range(NT):
                            last = dve.scalar_tensor_tensor(summed_b[ub][:, j, :], o[:, j, 0:D], out_inv[ub][:, j:j + 1],
                                                            x_kept[ub][:, j, :], ALU.mult, ALU.add)
                            cb.step(last)
                        cb.wait()
                        dve.sem_inc(mix_read, 1)
                        dve.sem_inc(S["mix_added"][ub], 1)
                        stats_of(cb, summed_b[ub], moments_b[ub], mean_var_b[ub], S["var_b"][ub])
                        cb.close()
                    if a:
                        dve.wait_ge(S["wout_ready"][ua], na + 1)
                        dve.wait_ge(S["xb_bias_ready"][ua], na + 1)
                        ca.step(dve.tensor_tensor(summed[ua][:, :, :], xb_bias[ua][:, :, :],
                                                  banks[:, 1, 0:T].rearrange("p (j d) -> p j d", d=D), ALU.add))
                        ca.wait()
                        stats_of(ca, summed[ua], moments[ua], mean_var[ua], S["var_a"][ua])
                    if f:
                        s = banks[:, 4:6, P:P + 2 * N129].rearrange("p b (c n) -> p b c n", n=N129)
                        inv = slot_inv[uf][:, :].rearrange("p (b c) -> p b c", b=2)
                        dve.wait_ge(S["slots_ready"][uf], nf + 1)
                        cf.step(dve.reciprocal(inv, s[:, :, :, D]))
                        cf.wait()
                        dve.tensor_tensor(slots_n[uf][:, :, :].rearrange("p (b c) d -> p b c d", b=2),
                                          s[:, :, :, 0:D], inv.unsqueeze(3).to_broadcast([P, 2, 2, D]), ALU.mult
                                          ).then_inc(S["slots_n_ready"][uf], 1)
                        cf.close()
                    if a:
                        dve.wait_ge(S["rstd_a"][ua], na + 1)
                        normalised(xc[ua], summed[ua], mean_var[ua], rstd[ua], S["xc_ready"][ua])
                    if a:
                        dve.wait_ge(S["xc_rms_ready"][ua], na + 1)
                        for j in range(NT):
                            dve.scalar_tensor_tensor(xn[ua][:, j, 0:D], xc[ua][:, j, :], xc_rms[ua][:, j:j + 1],
                                                     rows[:, R_GX, :], ALU.mult, ALU.mult
                                                     ).then_inc(S["xn_ready"][ua], 1)
                        ca.close()

                    if b:
                        dve.wait_ge(S["final_stored"][ub], nb * 16 + 16)
                        dve.wait_ge(S["rstd_b"][ub], nb + 1)
                        normalised(final[ub], summed_b[ub], mean_var_b[ub], rstd_b[ub], S["final_ready"][ub])

                pipeline(dve, step)

        l1.close()


_COLUMNS = ["L0_attn_ln1_g", "L0_attn_ln1_b", "L0_attn_ln2_g", "L0_attn_ln2_b", "L0_attn_tm_mix_k",
            "L0_attn_tm_mix_v", "L0_attn_tm_mix_r", "L0_attn_cm_mix_k", "L0_attn_cm_mix_r",
            "L0_attn_time_decay", "L0_attn_time_first", "L1_attn_qn_w"]
_ROWS = ["L1_attn_kn_w", "L1_attn_b_out", "L1_ffn_gamma_x", "L1_ffn_gamma_slot"]
_WEIGHTS = {"tm_Wk": "L0_attn_tm_Wk", "tm_Wv": "L0_attn_tm_Wv", "tm_Wr": "L0_attn_tm_Wr", "Wo": "L0_attn_Wo",
            "cm_Wk": "L0_attn_cm_Wk", "cm_Wv": "L0_attn_cm_Wv", "cm_Wr": "L0_attn_cm_Wr",
            "router_w": "L0_ffn_router_w", "router_b": "L0_ffn_router_b", "w1": "L0_ffn_w1", "b1": "L0_ffn_b1",
            "w2": "L0_ffn_w2", "b2": "L0_ffn_b2", "W_qkv": "L1_attn_W_qkv", "W_out": "L1_attn_W_out",
            "slots": "L1_ffn_slot_embeds", "ffn_w1": "L1_ffn_w1", "ffn_w2": "L1_ffn_w2"}


def _constants(np, heads=16, experts=8, tiles=32):
    c = np.zeros((P, C_END), np.float32)
    p = np.arange(P)
    c[:, C_IDENT:C_IDENT + P] = np.eye(P)
    c[:, C_UPPER:C_UPPER + P] = p[:, None] < p[None, :]
    c[:, C_BLOCK:C_BLOCK + P] = p[:, None] // (P // heads) == p[None, :] // (P // heads)
    c[:, C_HEADS:C_HEADS + heads] = p[:, None] // (P // heads) == np.arange(heads)
    c[:, C_FIRST:C_FIRST + experts] = experts - np.arange(experts)
    c[:, C_TILE:C_TILE + 40] = np.arange(40)
    c[:, C_COUNT:C_COUNT + tiles] = P * np.arange(tiles)
    c[:, C_RESET:C_RESET + experts * tiles] = np.arange(experts * tiles) % tiles != 0
    c[0:16, C_DIAG:C_DIAG + 16] = np.eye(16)
    return c


def kernel(**inputs):
    import numpy as _np
    import concourse.bacc as _bacc
    from concourse import mybir as _mybir
    from concourse.bass_utils import run_bass_kernel_spmd as _run

    nc = _bacc.Bacc("TRN2", target_bir_lowering=False, num_devices=1)
    arrays = {}

    def give(name, a):
        a = _np.ascontiguousarray(a)
        arrays[name] = a
        return nc.dram_tensor(name, a.shape, _mybir.dt.from_np(a.dtype), kind="ExternalInput").ap()

    x = give("x_dram", inputs["L0_attn_inputs"])
    vecs = give("vecs_dram", _np.stack([_np.asarray(inputs[n]) for n in _COLUMNS], axis=1))
    rows = give("rows_dram", _np.stack([_np.asarray(inputs[n]) for n in _ROWS], axis=0))
    consts = give("consts_dram", _constants(_np))
    w = {}
    for short, name in _WEIGHTS.items():
        a = _np.asarray(inputs[name])
        w[short] = give(short + "_dram", a.reshape(-1, a.shape[-1]) if short == "slots" else a)
    out = nc.dram_tensor("out_dram", inputs["L0_attn_inputs"].shape, F32, kind="ExternalOutput").ap()
    two_layer_kernel(nc, x, vecs, rows, consts, w, out)
    r = _run(nc, [arrays], core_ids=[0])
    return r.results[0]["out_dram"]
```

```python
from contextlib import ExitStack

import concourse.bass as bass
from concourse import mybir

ALU = mybir.AluOpType
ACT = mybir.ActivationFunctionType
F32 = mybir.dt.float32
BF16 = mybir.dt.bfloat16
I32 = mybir.dt.int32
AX = mybir.AxisListType.X

P = 128
U = 2

C_IDENT, C_UPPER, C_BLOCK, C_HEADS = 0, 128, 256, 384
C_FIRST, C_TILE, C_COUNT, C_RESET, C_DIAG, C_END = 400, 408, 448, 480, 736, 752
(V_G1, V_B1, V_G2, V_B2, V_MK, V_MV, V_MR, V_CK, V_CR, V_DECAY, V_FIRST, V_QN, V_N) = range(13)
R_KN, R_BOUT, R_GX, R_GS, R_N = range(5)


class Chain:

    def __init__(self, eng, sem, turn=0, per_turn=0):
        self.eng, self.sem, self.turn, self.per_turn, self.n = eng, sem, turn, per_turn, 0

    def step(self, ins):
        ins.then_inc(self.sem, 1)
        self.n += 1
        return self.n

    def wait(self, n=None):
        n = self.n if n is None else n
        self.eng.wait_ge(self.sem, self.turn * self.per_turn + n if self.per_turn else n)

    def close(self):
        assert self.n == self.per_turn, f"per_turn should be {self.n}"


def settle(eng, sem, value, passed):
    eng.wait_ge(sem, value)
    eng.sem_inc(passed, 1)


def two_layer_kernel(nc, x_in, vecs_in, rows_in, consts_in, w, out):
    SEQ, T, D = x_in.shape
    NT = T // P
    TILES = SEQ * NT
    TURNS = SEQ // U
    HID = w["cm_Wk"].shape[1]
    HC = HID // P
    E, _, GLU = w["w1"].shape
    XH = GLU // 2
    XC = XH // P
    XTILES = U * -(-(TILES + E - 1) // U)
    HEADS = C_FIRST - C_HEADS
    DH = D // HEADS
    SLOTS = w["slots"].shape[0]
    SC = SLOTS // P
    N129 = D + 1

    x_rows = x_in.rearrange("s (j p) d -> s p j d", p=P)
    out_rows = out.rearrange("s (j p) d -> s p j d", p=P)
    sorted_x = nc.dram_tensor("sorted_x", [XTILES * P, D], F32, kind="Internal").ap()
    sorted_y = nc.dram_tensor("sorted_y", [XTILES * P, D], F32, kind="Internal").ap()
    bias_parts = nc.dram_tensor("bias_parts", [3, E * (GLU + D)], BF16, kind="Internal").ap()

    ctx = ExitStack()
    with ctx:
        rwkv_sems = ExitStack()
        used_semaphores = []
        expert_sems = ExitStack()
        expert_semaphores = []

        def sem(name, scope=ctx):
            made = scope.enter_context(nc.semaphore(name))
            if scope is rwkv_sems:
                used_semaphores.append(made)
            if scope is expert_sems:
                expert_semaphores.append(made)
            return made

        def pair(name, scope=ctx):
            return [sem(f"{name}{u}", scope) for u in range(U)]

        def sb(name, shape, dt=F32, scope=ctx):
            return scope.enter_context(nc.sbuf_tensor(name, shape, dt))

        banks = ctx.enter_context(nc.psum_tensor("banks", [P, 8, 512], F32))

        def bank(u, k, lo=0, hi=512):
            return banks[:, 4 * u + k, lo:hi]

        consts = sb("consts", [P, C_END])
        vecs = sb("vecs", [P, V_N])
        rows = sb("rows", [P, R_N, D])
        router_b = sb("router_b", [P, E])
        ident = consts[:, C_IDENT:C_IDENT + P]
        ones_bf = sb("ones_bf", [P, P], BF16)
        eps = sb("eps", [P, 3, NT])
        EPS_LN, EPS_TM, EPS_RMS = 0, 1, 2
        neg_half = sb("neg_half", [P, 4])
        zeros = sb("zeros", [P, D])
        w1 = sb("w1", [P, E, GLU])
        w2 = sb("w2", [P, E, XC, D])
        biases = sb("biases", [3, E * (GLU + D)], BF16)
        b1_parts = biases[:, 0:E * GLU].rearrange("k (e f) -> k e f", e=E)
        b2_parts = biases[:, E * GLU:].rearrange("k (e f) -> k e f", e=E)
        w_qkv = sb("w_qkv", [P, 3 * D])
        w_out = sb("w_out", [P, D])
        ffn_w1 = sb("ffn_w1", [P, HID])
        ffn_w2 = sb("ffn_w2", [P, HC, D])
        slot_rows = sb("slot_rows", [P, SC, D])
        xa = sb("xa", [P, TILES, D])
        logits = sb("logits", [P, TILES, E])
        slot_of = sb("slot_of", [P, TILES], I32)
        tile_expert = sb("tile_expert", [P, XTILES], I32)

        consts_in_sem = sem("consts_loaded")
        rows_in_sem = sem("rows_loaded")
        rwkv_w_sem = sem("rwkv_weights_loaded")
        expert_w_sem = sem("expert_weights_loaded")
        layer1_w_sem = sem("layer1_weights_loaded")
        zeroed_sem = sem("sorted_x_zeroed")
        vec_passed = sem("vec_passed")
        pool_passed = sem("pool_passed")
        parts_sem = sem("bias_parts_stored")
        biases_sem = sem("biases_loaded")
        scattered = sem("rows_scattered")
        y_stored = pair("expert_rows_stored")

        layer0 = ExitStack()
        prep = ExitStack()

        def vec(k):
            return vecs[:, k:k + 1]

        mixed = {n: (sb(f"{n}_now", [P, c], scope=layer0), sb(f"{n}_before", [P, c], scope=layer0))
                 for n, c in (("tm_Wk", D), ("tm_Wv", D), ("tm_Wr", D), ("cm_Wk", HID), ("cm_Wr", D))}
        mix_of = {"tm_Wk": V_MK, "tm_Wv": V_MV, "tm_Wr": V_MR, "cm_Wk": V_CK, "cm_Wr": V_CR}
        wo = sb("wo", [P, D], scope=layer0)
        cm_wv = sb("cm_wv", [P, HC, D], scope=layer0)
        router_w = sb("router_w", [P, E], scope=layer0)
        decay = sb("decay", [P, 3], scope=layer0)
        NEG_W, U_PLUS_W, MINUS_U_W = decay[:, 0:1], decay[:, 1:2], decay[:, 2:3]

        B_ROWS = E * (GLU + D) // P
        part_b = sb("part_b", [B_ROWS, 3, P], BF16, scope=layer0)
        raw_b = sb("raw_b", [B_ROWS, P], scope=prep)
        rest_b = sb("rest_b", [B_ROWS, P], scope=prep)
        exp_decay = sb("exp_decay", [P, 1], scope=prep)

        zero_made = sem("zero_made", rwkv_sems)
        ones_made = sem("ones_made", rwkv_sems)
        vec_prep = sem("vec_prep", rwkv_sems)
        decay_exp = sem("decay_exp", rwkv_sems)
        parts_made = sem("bias_parts_made", rwkv_sems)

        with nc.Block() as block:

            @block.sync
            def _(sp):
                sp.dma_start(consts[:, :], consts_in).then_inc(consts_in_sem, 16)
                sp.dma_start(vecs[:, :], vecs_in).then_inc(consts_in_sem, 16)
                for n in mixed:
                    sp.dma_start(mixed[n][1][:, :], w[n]).then_inc(rwkv_w_sem, 16)
                sp.dma_start(wo[:, :], w["Wo"]).then_inc(rwkv_w_sem, 16)
                sp.dma_start(cm_wv[:, :, :], w["cm_Wv"].rearrange("(c p) d -> p c d", p=P)).then_inc(rwkv_w_sem, 16)
                sp.dma_start(router_w[:, :], w["router_w"]).then_inc(rwkv_w_sem, 16)

            @block.scalar
            def _(act):
                act.dma_start(raw_b[0:E * GLU // P, :], w["b1"].rearrange("e (c f) -> (e c) f", f=P)
                              ).then_inc(rows_in_sem, 16)
                act.dma_start(raw_b[E * GLU // P:, :], w["b2"]).then_inc(rows_in_sem, 16)
                act.wait_ge(consts_in_sem, 32)
                act.activation(exp_decay[:, :], vec(V_DECAY), ACT.Exp).then_inc(decay_exp, 1)
                act.dma_start(rows[:, :, :], rows_in.partition_broadcast(P)).then_inc(rows_in_sem, 16)
                act.dma_start(router_b[:, :], w["router_b"].partition_broadcast(P)).then_inc(rows_in_sem, 16)
                act.wait_ge(parts_made, 3)
                act.dma_start(bias_parts.rearrange("k (r f) -> r k f", f=P), part_b[:, :, :]).then_inc(parts_sem, 16)

            @block.gpsimd
            def _(pool):
                pool.memset(zeros[:, :], 0.0).then_inc(zero_made, 1)
                pool.memset(ones_bf[:, :], 1.0).then_inc(ones_made, 1)
                pool.memset(eps[:, EPS_LN, :], 1e-5).then_inc(ones_made, 1)
                pool.memset(eps[:, EPS_TM, :], 1e-3).then_inc(ones_made, 1)
                pool.memset(eps[:, EPS_RMS, :], 1e-6).then_inc(ones_made, 1)
                pool.memset(neg_half[:, :], -0.5).then_inc(ones_made, 1)

            @block.vector
            def _(dve):
                c = Chain(dve, vec_prep)
                dve.wait_ge(consts_in_sem, 32)
                dve.wait_ge(decay_exp, 1)
                c.step(dve.tensor_scalar(NEG_W, exp_decay[:, :], -1.0, None, ALU.mult))
                c.wait()
                c.step(dve.tensor_tensor(U_PLUS_W, NEG_W, vec(V_FIRST), ALU.add))
                c.wait()
                c.step(dve.tensor_scalar(MINUS_U_W, U_PLUS_W, -1.0, None, ALU.mult))
                dve.wait_ge(rwkv_w_sem, 16 * 8)
                for n, (now, before) in mixed.items():
                    k = c.step(dve.tensor_scalar(now[:, :], before[:, :], vec(mix_of[n]), None, ALU.mult))
                    c.wait(k)
                    c.step(dve.tensor_tensor(before[:, :], before[:, :], now[:, :], ALU.subtract))
                dve.wait_ge(rows_in_sem, 64)
                source = raw_b
                for k in range(3):
                    dve.tensor_copy(part_b[:, k, :], source[:, :]).then_inc(parts_made, 1)
                    if k < 2:
                        dve.wait_ge(parts_made, k + 1)
                        c.step(dve.tensor_tensor(rest_b[:, :], source[:, :], part_b[:, k, :], ALU.subtract))
                        c.wait()
                        source = rest_b

        prep.close()

        rw = ExitStack()

        def bufs(name, shape, dt=F32, scope=rw):
            return [sb(f"{name}{u}", shape, dt, scope) for u in range(U)]

        x_in_rows = bufs("x_in_rows", [P, NT, D])
        x_res = bufs("x_res", [P, NT, D])
        norms = {k: (bufs(f"mean_var_{k}", [P, NT, 2]), bufs(f"rstd_{k}", [P, NT])) for k in (1, 2, 3)}
        moments = bufs("moments", [P, NT, 6])
        normed1 = bufs("normed1", [P, NT, D])
        normed2 = bufs("normed2", [P, NT, D])
        normed3 = bufs("normed3", [P, NT, D])
        h1_cols = bufs("h1_cols", [P, T + 1])
        h2_cols = bufs("h2_cols", [P, T + 1])
        peak = bufs("peak", [P, T + 1])
        delta = bufs("delta", [P, T])
        TAKE_V, TAKE_OUT, TAKE_STATE, KEEP_STATE, KEEP_OUT = range(5)
        below_peak = bufs("below_peak", [P, 4, T])
        share = bufs("share", [P, 5, T])
        state = bufs("state", [P, 2, T + 1])
        taken = bufs("taken", [P, T])
        frac = bufs("frac", [P, 2, T])
        recip = bufs("recip", [P, T])
        r_tanh = bufs("r_tanh", [P, T])
        y_cols = bufs("y_cols", [P, T])
        x1 = bufs("x1", [P, NT, D])
        x01 = bufs("x01", [P, NT, D])
        k_relu = bufs("k_relu", [P, HC, T])
        k_sq = bufs("k_sq", [P, HC, T])
        rc_tanh = bufs("rc_tanh", [P, NT, D])
        gated = bufs("gated", [P, NT, D])
        xa_cols = bufs("xa_cols", [P, T])

        R = {n: pair(n, rwkv_sems) for n in """x_in_loaded x_in_free x_res_loaded
            var1 var2 var3 rstd1 rstd2 rstd3 normed1_ready normed2_ready normed3_ready
            turned1 turned2 h1_ready h2_ready kv_ready r_ready r_done delta_ready args_ready exps_ready y_ready
            wo_ready x1_ready x01_ready kc_ready relu_ready sq_ready rc_ready rc_done cv_ready
            turned3 xa_cols_ready logits_ready logits_saved""".split()}
        borders_set = sem("borders_set", rwkv_sems)
        vec_n = sem("vec_n", rwkv_sems)
        vec_m = sem("vec_m", rwkv_sems)
        vec_c = sem("vec_c", rwkv_sems)
        pool_rwkv = {k: sem(f"pool_rwkv{k}", rwkv_sems) for k in (1, 2, 3)}

        def by_rows(ap):
            return ap.rearrange("p (j d) -> p j d", d=D)

        FULL = "NMCR"

        def pipeline(eng, step):
            def place(s):
                return s + 2, s + 1, s, s - 1

            def live(s):
                return "".join(part for part, t in zip(FULL, place(s)) if 0 <= t < TURNS)

            for s in range(-2, 1):
                step(live(s), *place(s))
            with eng.Fori(0, TURNS - 3) as i:
                step(FULL, i + 3, i + 2, i + 1, i)
            for s in range(TURNS - 2, TURNS + 1):
                step(live(s), *place(s))

        with nc.Block() as block:

            @block.sync
            def _(sp):
                def step(parts, n, m, c, r):
                    if "N" in parts:
                        for u in range(U):
                            sp.wait_ge(R["x_in_free"][u], n + 1)
                            sp.dma_start(x_in_rows[u][:, :, :], x_rows[bass.ds(n * U + u, 1)].squeeze(0)
                                         ).then_inc(R["x_in_loaded"][u], 16)
                    if "M" in parts:
                        for u in range(U):
                            sp.wait_ge(R["x01_ready"][u], m + 1)
                            sp.dma_start(x_res[u][:, :, :], x_rows[bass.ds(m * U + u, 1)].squeeze(0)
                                         ).then_inc(R["x_res_loaded"][u], 16)
                    if parts == "NM":
                        sp.wait_ge(zero_made, 1)
                        sp.dma_start(sorted_x.rearrange("(t p) d -> p t d", p=P),
                                     zeros[:, :].unsqueeze(1).to_broadcast([P, XTILES, D])).then_inc(zeroed_sem, 16)
                    if parts == "NMC":
                        sp.dma_start(w1[:, :, :], w["w1"].rearrange("e p f -> p e f")).then_inc(expert_w_sem, 16)
                        sp.dma_start(w2[:, :, :, :], w["w2"].rearrange("e (c p) d -> p e c d", p=P)
                                     ).then_inc(expert_w_sem, 16)
                        sp.dma_start(w_qkv[:, :], w["W_qkv"]).then_inc(layer1_w_sem, 16)
                        sp.dma_start(w_out[:, :], w["W_out"]).then_inc(layer1_w_sem, 16)
                        sp.dma_start(ffn_w1[:, :], w["ffn_w1"]).then_inc(layer1_w_sem, 16)
                        sp.dma_start(ffn_w2[:, :, :], w["ffn_w2"].rearrange("(c p) d -> p c d", p=P)).then_inc(layer1_w_sem, 16)
                        sp.dma_start(slot_rows[:, :, :], w["slots"].rearrange("(c p) d -> p c d", p=P)).then_inc(layer1_w_sem, 16)

                pipeline(sp, step)
                sp.wait_ge(parts_sem, 16)
                sp.dma_start(biases[:, :], bias_parts).then_inc(biases_sem, 16)

            @block.tensor
            def _(pe):
                def turn(dst, src, done):
                    for j in range(NT):
                        last = pe.transpose(dst[:, j * P:(j + 1) * P], src[:, j, :], ident)
                    last.then_inc(done, 1)

                def mixed_columns(dst, h, name, lo, hi):
                    now, before = mixed[name]
                    pe.matmul(dst, now[:, lo:hi], h[:, 1:T + 1], start=True, stop=False)
                    return pe.matmul(dst, before[:, lo:hi], h[:, 0:T], start=False, stop=True)

                def step(parts, n, m, c, r):
                    if "M" in parts:
                        for u in range(U):
                            pe.wait_ge(R["h1_ready"][u], m + 1)
                            mixed_columns(bank(u, 1, 0, T), h1_cols[u], "tm_Wk", 0, D)
                            mixed_columns(bank(u, 1, T, 2 * T), h1_cols[u], "tm_Wv", 0, D
                                          ).then_inc(R["kv_ready"][u], 1)
                    if "C" in parts:
                        for u in range(U):
                            pe.wait_ge(R["normed2_ready"][u], c * NT + NT)
                            turn(bank(u, 0), normed2[u], R["turned2"][u])
                    if "M" in parts:
                        for u in range(U):
                            if "C" in parts:
                                pe.wait_ge(R["h2_ready"][u], c + 1)
                            mixed_columns(bank(u, 0, 0, T), h1_cols[u], "tm_Wr", 0, D
                                          ).then_inc(R["r_ready"][u], 1)
                    if "R" in parts:
                        for u in range(U):
                            pe.wait_ge(R["normed3_ready"][u], r * NT + NT)
                            turn(bank(u, 2), normed3[u], R["turned3"][u])
                    if "R" in parts:
                        for u in range(U):
                            pe.wait_ge(R["xa_cols_ready"][u], r + 1)
                            for j in range(NT):
                                last = pe.matmul(bank(u, 2, T + j * E, T + (j + 1) * E),
                                                 xa_cols[u][:, j * P:(j + 1) * P], router_w[:, :],
                                                 start=True, stop=True)
                            last.then_inc(R["logits_ready"][u], 1)
                    for u in range(U):
                        if "C" in parts:
                            pe.wait_ge(R["h2_ready"][u], c + 1)
                            for k in (0, 1):
                                mixed_columns(bank(u, 3, k * T, (k + 1) * T), h2_cols[u], "cm_Wk", k * P, (k + 1) * P
                                              ).then_inc(R["kc_ready"][u], 1)
                    if "C" in parts:
                        for u in range(U):
                            if "R" in parts:
                                pe.wait_ge(R["logits_saved"][u], r + 1)
                            for k in (2, 3):
                                mixed_columns(bank(u, 2, (k - 2) * T, (k - 1) * T), h2_cols[u], "cm_Wk",
                                              k * P, (k + 1) * P).then_inc(R["kc_ready"][u], 1)
                            pe.wait_ge(R["relu_ready"][u], c * 2 + 1)
                            now, before = mixed["cm_Wr"]
                            for j in range(NT):
                                dst = bank(u, 3, j * D, (j + 1) * D)
                                pe.matmul(dst, h2_cols[u][:, 1 + j * P:1 + (j + 1) * P], now[:, :],
                                          start=True, stop=False)
                                last = pe.matmul(dst, h2_cols[u][:, j * P:(j + 1) * P], before[:, :],
                                                 start=False, stop=True)
                            last.then_inc(R["rc_ready"][u], 1)
                    def time_mixing_out(u):
                        pe.wait_ge(R["y_ready"][u], m + 1)
                        for j in range(NT):
                            last = pe.matmul(bank(u, 0, j * D, (j + 1) * D), y_cols[u][:, j * P:(j + 1) * P],
                                             wo[:, :], start=True, stop=True)
                        last.then_inc(R["wo_ready"][u], 1)

                    if "M" in parts:
                        time_mixing_out(0)
                    if "C" in parts:
                        for u in range(U):
                            pe.wait_ge(R["sq_ready"][u], c * 2 + 2)
                            for j in range(NT):
                                for k in range(HC):
                                    last = pe.matmul(bank(u, 2, j * D, (j + 1) * D),
                                                     k_sq[u][:, k, j * P:(j + 1) * P], cm_wv[:, k, :],
                                                     start=(k == 0), stop=(k == HC - 1))
                            last.then_inc(R["cv_ready"][u], 1)
                    if "M" in parts:
                        time_mixing_out(1)
                    if "N" in parts:
                        for u in range(U):
                            pe.wait_ge(R["normed1_ready"][u], n * NT + NT)
                            turn(bank(u, 1), normed1[u], R["turned1"][u])
                pipeline(pe, step)

            @block.scalar
            def _(act):
                def step(parts, n, m, c, r):
                    if "C" in parts:
                        for u in range(U):
                            act.wait_ge(R["turned2"][u], c + 1)
                            act.activation(h2_cols[u][:, 1:T + 1], bank(u, 0, 0, T), ACT.Identity,
                                           bias=vec(V_B2), scale=vec(V_G2)).then_inc(R["h2_ready"][u], 1)
                    if "R" in parts:
                        for u in range(U):
                            act.wait_ge(R["turned3"][u], r + 1)
                            act.activation(xa_cols[u][:, :], bank(u, 2, 0, T), ACT.Copy
                                           ).then_inc(R["xa_cols_ready"][u], 1)
                    if "M" in parts:
                        for u in range(U):
                            act.wait_ge(R["r_ready"][u], m + 1)
                            act.activation(r_tanh[u][:, :], bank(u, 0, 0, T), ACT.Tanh, scale=0.5
                                           ).then_inc(R["r_done"][u], 1)
                    for u in range(U):
                        if "M" in parts:
                            act.wait_ge(R["delta_ready"][u], m + 1)
                            for which, sign, offset in ((TAKE_OUT, -1.0, 0.0), (TAKE_STATE, -1.0, U_PLUS_W),
                                                        (KEEP_STATE, 1.0, MINUS_U_W), (KEEP_OUT, 1.0, 0.0)):
                                act.activation(below_peak[u][:, which - 1, :], delta[u][:, :], ACT.Relu,
                                               bias=offset, scale=sign).then_inc(R["args_ready"][u], 1)
                            act.wait_ge(R["args_ready"][u], m * 4 + 4)
                            act.activation(share[u][:, 1:5, :], below_peak[u][:, :, :], ACT.Exp, scale=-1.0
                                           ).then_inc(R["exps_ready"][u], 1)
                        if "C" in parts:
                            act.wait_ge(R["kc_ready"][u], c * HC + 2)
                            act.activation(k_relu[u][:, 0:2, :], bank(u, 3).rearrange("p (k t) -> p k t", t=T),
                                           ACT.Relu).then_inc(R["relu_ready"][u], 1)
                    if "C" in parts:
                        for u in range(U):
                            act.wait_ge(R["kc_ready"][u], c * HC + 4)
                            act.activation(k_relu[u][:, 2:4, :], bank(u, 2).rearrange("p (k t) -> p k t", t=T),
                                           ACT.Relu).then_inc(R["relu_ready"][u], 1)
                            act.wait_ge(R["rc_ready"][u], c + 1)
                            act.activation(rc_tanh[u][:, :, :], by_rows(bank(u, 3, 0, T)), ACT.Tanh, scale=0.5
                                           ).then_inc(R["rc_done"][u], 1)
                    if "N" in parts:
                        for u in range(U):
                            act.wait_ge(R["turned1"][u], n + 1)
                            act.activation(h1_cols[u][:, 1:T + 1], bank(u, 1, 0, T), ACT.Identity,
                                           bias=vec(V_B1), scale=vec(V_G1)).then_inc(R["h1_ready"][u], 1)
                pipeline(act, step)

            @block.gpsimd
            def _(pool):
                for u in range(U):
                    pool.memset(h1_cols[u][:, 0:1], 0.0).then_inc(borders_set, 1)
                    pool.memset(h2_cols[u][:, 0:1], 0.0).then_inc(borders_set, 1)
                    pool.memset(peak[u][:, 0:1], -1e38).then_inc(borders_set, 1)
                    pool.memset(state[u][:, :, 0:1], 0.0).then_inc(borders_set, 1)

                def to_rstd(p, k, e, t, u):
                    mean_var, rstd = norms[k]
                    pool.wait_ge(R[f"var{k}"][u], t * NT + NT)
                    p.step(pool.tensor_tensor(rstd[u][:, :], mean_var[u][:, :, 1], eps[:, e, :], ALU.add))
                    p.wait()
                    pool.tensor_tensor(rstd[u][:, :], rstd[u][:, :], neg_half[:, 0:NT], ALU.pow
                                       ).then_inc(R[f"rstd{k}"][u], 1)

                def step(parts, n, m, c, r):
                    def square(half):
                        for u in range(U):
                            pool.wait_ge(R["relu_ready"][u], c * 2 + half + 1)
                            k = k_relu[u][:, 2 * half:2 * half + 2, :]
                            pool.tensor_tensor(k_sq[u][:, 2 * half:2 * half + 2, :], k, k, ALU.mult
                                               ).then_inc(R["sq_ready"][u], 1)

                    p1 = Chain(pool, pool_rwkv[1], n, U)
                    p2 = Chain(pool, pool_rwkv[2], m, U)
                    p3 = Chain(pool, pool_rwkv[3], c, U)
                    if "N" in parts:
                        for u in range(U):
                            to_rstd(p1, 1, EPS_TM, n, u)
                    if "C" in parts:
                        square(0)
                        square(1)
                    for u in range(U):
                        if "M" in parts:
                            to_rstd(p2, 2, EPS_TM, m, u)
                        if "C" in parts:
                            to_rstd(p3, 3, EPS_LN, c, u)
                    if "M" in parts:
                        for u in range(U):
                            pool.wait_ge(R["x1_ready"][u], m + 1)
                            pool.tensor_tensor(x01[u][:, :, :], x_res[u][:, :, :], x1[u][:, :, :], ALU.add
                                               ).then_inc(R["x01_ready"][u], 1)

                pipeline(pool, step)

            @block.vector
            def _(dve):
                dve.wait_ge(borders_set, 4 * U)
                for u in range(U):
                    dve.sem_inc(R["x_in_free"][u], 1)
                    dve.sem_inc(R["x01_ready"][u], 1)

                def stats(q, k, src, u):
                    for j in range(NT):
                        q.step(dve.bn_stats(moments[u][:, j, :], src[u][:, j, :]))
                    settle(dve, q.sem, q.turn * q.per_turn + q.n, vec_passed)
                    for j in range(NT):
                        dve.bn_aggr(norms[k][0][u][:, j, :], moments[u][:, j, :]).then_inc(R[f"var{k}"][u], 1)

                def normalise(k, t, u, src, dst):
                    mean_var, rstd = norms[k]
                    dve.wait_ge(R[f"rstd{k}"][u], t + 1)
                    for j in range(NT):
                        dve.tensor_scalar(dst[u][:, j, :], src[u][:, j, :], mean_var[u][:, j, 0:1], rstd[u][:, j:j + 1],
                                          ALU.subtract, ALU.mult).then_inc(R[f"normed{k}_ready"][u], 1)

                def exponents(q, m, u):
                    key = bank(u, 1, 0, T)
                    dve.wait_ge(R["kv_ready"][u], m + 1)
                    q.step(dve.tensor_tensor_scan(peak[u][:, 1:T + 1], NEG_W.to_broadcast([P, T]), key,
                                                  -1e38, ALU.add, ALU.max))
                    q.wait()
                    dve.scalar_tensor_tensor(delta[u][:, :], key, vec(V_FIRST), peak[u][:, 0:T],
                                             ALU.add, ALU.subtract).then_inc(R["delta_ready"][u], 1)

                def weighted_values(q, m, u):
                    v = bank(u, 1, T, 2 * T)

                    def e(which):
                        return share[u][:, which, :]

                    dve.wait_ge(R["exps_ready"][u], m + 1)
                    k = q.step(dve.tensor_tensor(taken[u][:, :], e(TAKE_STATE), v, ALU.mult))
                    bb = q.step(dve.tensor_tensor_scan(state[u][:, 1, 1:T + 1], e(KEEP_STATE), e(TAKE_STATE),
                                                       0.0, ALU.mult, ALU.add))
                    q.step(dve.tensor_tensor(e(TAKE_V), e(TAKE_OUT), v, ALU.mult))
                    q.wait(k)
                    q.step(dve.tensor_tensor_scan(state[u][:, 0, 1:T + 1], e(KEEP_STATE), taken[u][:, :],
                                                  0.0, ALU.mult, ALU.add))
                    q.wait()
                    q.step(dve.tensor_tensor(frac[u][:, :, :], state[u][:, :, 0:T],
                                             share[u][:, KEEP_OUT:KEEP_OUT + 1, :].to_broadcast([P, 2, T]),
                                             ALU.mult))
                    q.wait()
                    q.step(dve.tensor_tensor(frac[u][:, :, :], frac[u][:, :, :], share[u][:, TAKE_V:TAKE_OUT + 1, :],
                                             ALU.add))
                    q.wait()
                    q.step(dve.reciprocal(recip[u][:, :], frac[u][:, 1, :]))
                    dve.wait_ge(R["r_done"][u], m + 1)
                    num = q.step(dve.scalar_tensor_tensor(frac[u][:, 0, :], r_tanh[u][:, :], 1.0,
                                                          frac[u][:, 0, :], ALU.add, ALU.mult))
                    q.wait(num)
                    dve.scalar_tensor_tensor(y_cols[u][:, :], frac[u][:, 0, :], 0.5, recip[u][:, :],
                                             ALU.mult, ALU.mult).then_inc(R["y_ready"][u], 1)

                def first_sum(q, m, u):
                    dve.wait_ge(R["wo_ready"][u], m + 1)
                    dve.wait_ge(R["x_res_loaded"][u], m * 16 + 16)
                    dve.wait_ge(R["x01_ready"][u], m + 1)
                    dve.tensor_tensor(x1[u][:, :, :], x_res[u][:, :, :], by_rows(bank(u, 0, 0, T)),
                                      ALU.add).then_inc(R["x1_ready"][u], 1)
                    dve.wait_ge(R["x1_ready"][u], m + 1)
                    stats(q, 2, x1, u)

                def second_sum(q, c, u):
                    dve.wait_ge(R["rc_done"][u], c + 1)
                    dve.wait_ge(R["cv_ready"][u], c + 1)
                    q.step(dve.scalar_tensor_tensor(gated[u][:, :, :], rc_tanh[u][:, :, :], 1.0,
                                                    by_rows(bank(u, 2, 0, T)), ALU.add, ALU.mult))
                    dve.wait_ge(R["x01_ready"][u], c + 2)
                    q.wait()
                    q.step(dve.scalar_tensor_tensor(gated[u][:, :, :], gated[u][:, :, :], 0.5,
                                                    x01[u][:, :, :], ALU.mult, ALU.add))
                    q.wait()
                    stats(q, 3, gated, u)

                def step(parts, n, m, c, r):
                    qn = Chain(dve, vec_n, n, U * NT)
                    qm = Chain(dve, vec_m, m, 22)
                    qc = Chain(dve, vec_c, c, 8)
                    if "R" in parts:
                        for u in range(U):
                            normalise(3, r, u, gated, normed3)
                        for u in range(U):
                            dve.wait_ge(R["normed3_ready"][u], r * NT + NT)
                            dve.tensor_copy(xa[:, bass.ds((r * U + u) * NT, NT), :], normed3[u][:, :, :])
                    if "M" in parts:
                        for u in range(U):
                            exponents(qm, m, u)
                    if "R" in parts:
                        for u in range(U):
                            dve.wait_ge(R["logits_ready"][u], r + 1)
                            dve.tensor_tensor(logits[:, bass.ds((r * U + u) * NT, NT), :],
                                              bank(u, 2, T, T + NT * E).rearrange("p (j e) -> p j e", e=E),
                                              router_b[:, :].unsqueeze(1).to_broadcast([P, NT, E]),
                                              ALU.add).then_inc(R["logits_saved"][u], 1)
                    if "N" in parts:
                        for u in range(U):
                            dve.wait_ge(R["x_in_loaded"][u], n * 16 + 16)
                            stats(qn, 1, x_in_rows, u)
                        qn.close()
                    if "M" in parts:
                        weighted_values(qm, m, 0)
                    if "M" in parts:
                        weighted_values(qm, m, 1)
                    if "N" in parts:
                        for u in range(U):
                            normalise(1, n, u, x_in_rows, normed1)
                            dve.wait_ge(R["normed1_ready"][u], n * NT + NT)
                            dve.sem_inc(R["x_in_free"][u], 1)
                    if "M" in parts:
                        first_sum(qm, m, 0)
                    if "C" in parts:
                        second_sum(qc, c, 0)
                    if "M" in parts:
                        first_sum(qm, m, 1)
                    if "M" in parts:
                        normalise(2, m, 0, x1, normed2)
                    if "M" in parts:
                        normalise(2, m, 1, x1, normed2)
                        qm.close()
                    if "C" in parts:
                        second_sum(qc, c, 1)
                        qc.close()

                pipeline(dve, step)

        rw.close()
        layer0.close()

        route = ExitStack()

        best = sb("best", [P, TILES], scope=route)
        candidate = sb("candidate", [P, TILES, E], scope=route)
        chosen = sb("chosen", [P, TILES, E], scope=route)
        chosen_bf = sb("chosen_bf", [P, TILES, E], BF16, scope=route)
        upper_bf = sb("upper_bf", [P, P], BF16, scope=route)
        in_tile = sb("in_tile", [P, E, TILES], scope=route)
        so_far = sb("so_far", [P, E, TILES], scope=route)
        more_than = sb("more_than", [P, E, TILES], scope=route)
        tiles_of = sb("tiles_of", [P, E], scope=route)
        tiles_end = sb("tiles_end", [P, E], scope=route)
        first_row = sb("first_row", [P, E], scope=route)
        place = sb("place", [P, TILES, E], scope=route)
        place_sum = sb("place_sum", [P, TILES], scope=route)
        ended = sb("ended", [P, XTILES, E], scope=route)
        expert_f = sb("expert_f", [P, XTILES], scope=route)

        vec_route = sem("vec_route", rwkv_sems)
        chosen_ready = sem("chosen_ready", rwkv_sems)
        counts_ready = sem("counts_ready", rwkv_sems)
        places_ready = sem("places_ready", rwkv_sems)

        rank = banks[:, 0, 0:TILES * E].rearrange("p (t e) -> p t e", e=E)
        count = banks[:, 1, 0:TILES * E].rearrange("p (t e) -> p t e", e=E)
        preference = consts[:, C_FIRST:C_FIRST + E]
        tile_number = consts[:, C_TILE:C_TILE + XTILES]
        full_tiles = consts[:, C_COUNT:C_COUNT + TILES]
        restart = consts[:, C_RESET:C_RESET + E * TILES]

        with nc.Block() as block:

            @block.vector
            def _(dve):
                c = Chain(dve, vec_route)

                def then(ins):
                    c.wait(c.step(ins))

                wide = [P, TILES, E]
                then(dve.tensor_copy(upper_bf[:, :], consts[:, C_UPPER:C_UPPER + P]))
                then(dve.tensor_reduce(best[:, :], logits[:, :, :], AX, ALU.max))
                then(dve.tensor_tensor(candidate[:, :, :], logits[:, :, :],
                                       best[:, :].unsqueeze(2).to_broadcast(wide), ALU.is_ge))
                then(dve.tensor_tensor(candidate[:, :, :], candidate[:, :, :],
                                       preference.unsqueeze(1).to_broadcast(wide), ALU.mult))
                then(dve.tensor_reduce(best[:, :], candidate[:, :, :], AX, ALU.max))
                then(dve.tensor_tensor(chosen[:, :, :], best[:, :].unsqueeze(2).to_broadcast(wide),
                                       preference.unsqueeze(1).to_broadcast(wide), ALU.is_equal))
                dve.tensor_copy(chosen_bf[:, :, :], chosen[:, :, :]).then_inc(chosen_ready, 1)
                dve.wait_ge(counts_ready, 1)
                then(dve.tensor_copy(in_tile[:, :, :], count.rearrange("p t e -> p e t")))
                then(dve.tensor_tensor_scan(so_far[:, :, :].rearrange("p e t -> p (e t)"), restart,
                                            in_tile[:, :, :].rearrange("p e t -> p (e t)"),
                                            0.0, ALU.mult, ALU.add))
                then(dve.tensor_tensor(more_than[:, :, :],
                                       so_far[:, :, TILES - 1:TILES].to_broadcast([P, E, TILES]),
                                       full_tiles.unsqueeze(1).to_broadcast([P, E, TILES]), ALU.is_gt))
                then(dve.tensor_reduce(tiles_of[:, :], more_than[:, :, :], AX, ALU.add))
                then(dve.tensor_tensor_scan(tiles_end[:, :], restart[:, 1:1 + E], tiles_of[:, :],
                                            0.0, ALU.mult, ALU.add))
                then(dve.tensor_tensor(first_row[:, :], tiles_end[:, :], tiles_of[:, :], ALU.subtract))
                then(dve.tensor_scalar(first_row[:, :], first_row[:, :], float(P), None, ALU.mult))
                then(dve.tensor_tensor(so_far[:, :, :], so_far[:, :, :], in_tile[:, :, :], ALU.subtract))
                then(dve.tensor_tensor(place[:, :, :], rank, so_far[:, :, :].rearrange("p e t -> p t e"), ALU.add))
                then(dve.tensor_tensor(place[:, :, :], place[:, :, :],
                                       first_row[:, :].unsqueeze(1).to_broadcast(wide), ALU.add))
                then(dve.tensor_tensor(place[:, :, :], place[:, :, :], chosen[:, :, :], ALU.mult))
                then(dve.tensor_reduce(place_sum[:, :], place[:, :, :], AX, ALU.add))
                dve.tensor_copy(slot_of[:, :], place_sum[:, :]).then_inc(places_ready, 1)
                then(dve.tensor_tensor(ended[:, :, :], tiles_end[:, :].unsqueeze(1).to_broadcast([P, XTILES, E]),
                                       tile_number.unsqueeze(2).to_broadcast([P, XTILES, E]), ALU.is_le))
                then(dve.tensor_reduce(expert_f[:, :], ended[:, :, :], AX, ALU.add))
                then(dve.tensor_scalar(expert_f[:, :], expert_f[:, :], float(E - 1), None, ALU.min))
                then(dve.tensor_copy(tile_expert[:, :], expert_f[:, :]))

            @block.tensor
            def _(pe):
                flat = chosen_bf[:, :, :].rearrange("p t e -> p (t e)")
                pe.wait_ge(chosen_ready, 1)
                pe.matmul(banks[:, 0, 0:TILES * E], upper_bf[:, :], flat, start=True, stop=True)
                pe.matmul(banks[:, 1, 0:TILES * E], ones_bf[:, :], flat, start=True, stop=True
                          ).then_inc(counts_ready, 1)

            @block.gpsimd
            def _(pool):
                pool.wait_ge(places_ready, 1)
                pool.wait_ge(zeroed_sem, 16)
                for t in range(TILES):
                    pool.indirect_dma_start(sorted_x, bass.IndirectOffsetOnAxis(ap=slot_of[:, t:t + 1], axis=0),
                                            xa[:, t, :], None).then_inc(scattered, 16)

        route.close()

        ex = ExitStack()

        def bufs(name, shape, dt=F32, scope=ex):
            return [sb(f"{name}{u}", shape, dt, scope) for u in range(U)]

        xg = bufs("xg", [P, D])
        xg_cols = bufs("xg_cols", [P, P])
        gate = bufs("gate", [P, XH])
        hidden = bufs("hidden", [P, XH])
        hidden_cols = bufs("hidden_cols", [P, XC, P])
        y_rows = bufs("y_rows", [P, D])

        xg_loaded = pair("xg_loaded", expert_sems)
        xg_turned = pair("xg_turned", expert_sems)
        xg_cols_ready = pair("xg_cols_ready", expert_sems)
        lin_ready = pair("lin_ready", expert_sems)
        gate_in_ready = pair("gate_in_ready", expert_sems)
        gate_ready = pair("gate_ready", expert_sems)
        hidden_ready = pair("hidden_ready", expert_sems)
        hidden_turned = pair("hidden_turned", expert_sems)
        hidden_cols_ready = pair("hidden_cols_ready", expert_sems)
        down_ready = pair("down_ready", expert_sems)
        y_rows_ready = pair("y_rows_ready", expert_sems)

        STEPS = XTILES // U

        def expert_pipeline(eng, step):
            def live(s):
                return "".join(part for part, k in (("T", 2), ("F", 1), ("S", 0)) if 0 <= s + k < STEPS)

            for s in (-2, -1):
                step(live(s), s)
            with eng.Fori(0, STEPS - 2) as i:
                step("TFS", i)
            for s in (STEPS - 2, STEPS - 1):
                step(live(s), s)

        with nc.Block() as block:

            @block.gpsimd
            def _(pool):
                for used in used_semaphores:
                    pool.sem_clear(used)

            @block.sync
            def _(sp):
                def step(parts, s):
                    for u in range(U):
                        if "T" in parts:
                            sp.wait_ge(xg_turned[u], s + 3)
                            sp.dma_start(xg[u][:, :], sorted_x[bass.ds(((s + 2) * U + u) * P, P), :]
                                         ).then_inc(xg_loaded[u], 16)
                    for u in range(U):
                        if "S" in parts:
                            sp.wait_ge(y_rows_ready[u], s + 2)
                            sp.dma_start(sorted_y[bass.ds((s * U + u) * P, P), :], y_rows[u][:, :]
                                         ).then_inc(y_stored[u], 16)

                sp.wait_ge(scattered, 16 * TILES)
                expert_pipeline(sp, step)

            @block.tensor
            def _(pe):
                ones = ones_bf[0:3, :]

                def expert_of(turn, u):
                    return pe.value_load(tile_expert[0:1, bass.ds(turn * U + u, 1)], min_val=0, max_val=E - 1)

                def step(parts, s):
                    e1 = {}
                    for u in range(U):
                        if "S" in parts:
                            pe.wait_ge(hidden_ready[u], s + 1)
                            pe.wait_ge(y_rows_ready[u], s + 1)
                            for c in range(XC):
                                last = pe.transpose(bank(u, 3, c * P, (c + 1) * P),
                                                    hidden[u][:, c * P:(c + 1) * P], ident)
                            last.then_inc(hidden_turned[u], 1)
                        if "F" in parts:
                            e1[u] = expert_of(s + 1, u)
                            pe.wait_ge(xg_cols_ready[u], s + 2)
                            for k, lo, done in ((2, XH, gate_in_ready), (1, 0, lin_ready)):
                                pe.matmul(bank(u, k), ones, b1_parts[:, bass.ds(e1[u], 1), lo:lo + XH].squeeze(1),
                                          start=True, stop=False)
                                pe.matmul(bank(u, k), xg_cols[u][:, :],
                                          w1[:, bass.ds(e1[u], 1), lo:lo + XH].squeeze(1),
                                          start=False, stop=True).then_inc(done[u], 1)
                    e2 = [expert_of(s, u) for u in range(U)] if "S" in parts else None
                    for u in range(U):
                        if "S" in parts:
                            pe.wait_ge(hidden_cols_ready[u], s + 1)
                            dst = bank(u, 3, 0, D)
                            pe.matmul(dst, ones, b2_parts[:, bass.ds(e2[u], 1), :].squeeze(1),
                                      start=True, stop=False)
                            for c in range(XC):
                                last = pe.matmul(dst, hidden_cols[u][:, c, :],
                                                 w2[:, bass.ds(e2[u], 1), c, :].squeeze(1),
                                                 start=False, stop=(c == XC - 1))
                            last.then_inc(down_ready[u], 1)
                    for u in range(U):
                        if "T" in parts:
                            pe.wait_ge(xg_loaded[u], s * 16 + 48)
                            pe.transpose(bank(u, 0, 0, P), xg[u][:, :], ident).then_inc(xg_turned[u], 1)

                pe.wait_ge(expert_w_sem, 32)
                pe.wait_ge(biases_sem, 16)
                for u in range(U):
                    pe.sem_inc(xg_turned[u], 1)
                expert_pipeline(pe, step)

            @block.scalar
            def _(act):
                def step(parts, s):
                    for u in range(U):
                        if "S" in parts:
                            act.wait_ge(hidden_turned[u], s + 1)
                            act.activation(hidden_cols[u][:, :, :].rearrange("p c t -> p (c t)"), bank(u, 3), ACT.Copy
                                           ).then_inc(hidden_cols_ready[u], 1)
                        if "F" in parts:
                            act.wait_ge(gate_in_ready[u], s + 2)
                            act.activation(gate[u][:, :], bank(u, 2), ACT.Sigmoid).then_inc(gate_ready[u], 1)
                    for u in range(U):
                        if "T" in parts:
                            act.wait_ge(xg_turned[u], s + 4)
                            act.activation(xg_cols[u][:, :], bank(u, 0, 0, P), ACT.Copy).then_inc(xg_cols_ready[u], 1)

                expert_pipeline(act, step)

            @block.vector
            def _(dve):
                def step(parts, s):
                    for u in range(U):
                        if "F" in parts:
                            dve.wait_ge(gate_ready[u], s + 2)
                            dve.wait_ge(lin_ready[u], s + 2)
                            dve.tensor_tensor(hidden[u][:, :], gate[u][:, :], bank(u, 1), ALU.mult
                                              ).then_inc(hidden_ready[u], 1)
                    for u in range(U):
                        if "S" in parts:
                            dve.wait_ge(down_ready[u], s + 1)
                            dve.wait_ge(y_stored[u], s * 16 + 16)
                            dve.tensor_copy(y_rows[u][:, :], bank(u, 3, 0, D)).then_inc(y_rows_ready[u], 1)

                for u in range(U):
                    dve.sem_inc(y_rows_ready[u], 1)
                    dve.sem_inc(y_stored[u], 16)
                expert_pipeline(dve, step)

        ex.close()
        rwkv_sems.close()

        with nc.Block() as block:

            @block.gpsimd
            def _(pool):
                for used in expert_semaphores[0::2]:
                    pool.sem_clear(used)

            @block.vector
            def _(dve):
                for used in expert_semaphores[1::2]:
                    dve.sem_clear(used)

        expert_sems.close()

        l1 = ExitStack()

        def bufs(name, shape, dt=F32, scope=l1):
            return [sb(f"{name}{u}", shape, dt, scope) for u in range(U)]

        slot_sq = sb("slot_sq", [P, SC, 2], scope=l1)
        slot_cols = sb("slot_cols", [P, SLOTS], scope=l1)
        square_junk = sb("square_junk", [P, D], scope=l1)

        y_idx = bufs("y_idx", [P, NT], I32)
        y_got = bufs("y_got", [P, NT, D])
        summed = bufs("summed", [P, NT, D])
        moments = bufs("moments_a", [P, NT, 6])
        mean_var = bufs("mean_var_a", [P, NT, 2])
        rstd = bufs("rstd_a", [P, NT])
        summed_e = bufs("summed_e", [P, NT, D])
        moments_e = bufs("moments_e", [P, NT, 6])
        mean_var_e = bufs("mean_var_e", [P, NT, 2])
        rstd_e = bufs("rstd_e", [P, NT])
        qk_squares = bufs("qk_squares", [P, NT, 2 * D])
        x_kept = bufs("x_kept", [P, NT, D])
        summed_b = bufs("summed_b", [P, NT, D])
        moments_b = bufs("moments_b", [P, NT, 6])
        mean_var_b = bufs("mean_var_b", [P, NT, 2])
        rstd_b = bufs("rstd_b", [P, NT])
        xb = bufs("xb", [P, NT, D])
        xb_bias = bufs("xb_bias", [P, NT, D])
        cols = bufs("cols", [P, T])
        junk = bufs("junk", [P, D])
        qk_sq = bufs("qk_sq", [P, 2 * NT])
        qk_rms = bufs("qk_rms", [P, 2 * NT])
        q_rows = bufs("q_rows", [P, NT, D])
        q_cols = bufs("q_cols", [P, T])
        k_rows = bufs("k_rows", [P, NT, D])
        v_rows = bufs("v_rows", [P, NT, N129])
        kv_heads = bufs("kv_heads", [P, D + HEADS])
        norm_inv = bufs("norm_inv", [P, NT, HEADS])
        att = bufs("att", [P, NT, D])
        att_cols = bufs("att_cols", [P, T])
        xc = bufs("xc", [P, NT, D])
        xc_sq = bufs("xc_sq", [P, NT])
        xc_rms = bufs("xc_rms", [P, NT])
        xn = bufs("xn", [P, NT, N129])
        xn_cols = bufs("xn_cols", [P, T])
        slot_peak = bufs("slot_peak", [P, SC], BF16)
        token_peak = bufs("token_peak", [P, NT], BF16)
        slot_shift = bufs("slot_shift", [SC, SC, P], BF16)
        token_shift = bufs("token_shift", [NT, NT, P], BF16)
        dispatch = bufs("dispatch", [P, NT, SLOTS])
        combine = bufs("combine", [P, SC, T])
        slot_inv = bufs("slot_inv", [P, SC])
        slots_n = bufs("slots_n", [P, SC, D])
        slots_cols = bufs("slots_cols", [P, SLOTS])
        act_cols = bufs("act_cols", [P, HC, SLOTS])
        processed = bufs("processed", [P, SC, N129])
        out_inv = bufs("out_inv", [P, NT])
        final = bufs("final", [P, NT, D])
        ident_bf = sb("ident_bf", [P, P], BF16, scope=l1)

        slot_sq_ready = sem("slot_sq_ready", l1)
        slot_rms_ready = sem("slot_rms_ready", l1)
        slot_rows_ready = sem("slot_rows_ready", l1)
        slot_turned = sem("slot_turned", l1)
        slot_cols_ready = sem("slot_cols_ready", l1)
        ones_set = sem("ones_set", l1)
        mix_read = sem("mix_read", l1)
        wout_read = sem("wout_read", l1)
        vec_slots = sem("vec_slots", l1)
        pool_slots = sem("pool_slots", l1)
        vec_a, vec_f, vec_b = pair("vec_a", l1), pair("vec_f", l1), pair("vec_b", l1)
        pool_a, pool_b, pool_e = pair("pool_a", l1), pair("pool_b", l1), pair("pool_e", l1)
        vec_e = pair("vec_e", l1)
        names = """idx_ready y_gathered var_a rstd_a var_b rstd_b var_e rstd_e qk_squared kept mix_added xb_ready xb_bias_ready xb_turned xb_cols_ready
            qk_ready qk_sq_ready qk_rms_ready q_rows_ready k_rows_ready v_rows_ready
            q_turned q_cols_ready kv_sum_ready kv_heads_ready att_ready att_rows_ready att_turned
            att_cols_ready wout_ready xc_ready xc_sq_ready xc_rms_ready xn_ready xn_turned
            xn_cols_ready by_slot_ready slot_peak_ready slot_peak_turned slot_shift_ready
            by_token_ready token_peak_ready by_token_shifted dispatch_ready token_peak_turned
            token_shift_ready by_slot_shifted combine_ready slots_ready slots_n_ready slots_turned
            slots_cols_ready hid_ready gelu_ready proc_ready processed_ready mix_ready
            final_ready final_stored""".split()
        S = {n: pair(n, l1) for n in names}

        STEPS_LOOPED = 2 * ((SEQ - 4) // 2)
        last_looped = STEPS_LOOPED

        def pipeline(eng, step):
            def place(turn, k):
                return k % 2, turn + k // 2

            for s in range(-3, 1):
                step(lambda k, s=s: place(0, s + k), live(s))
            with eng.Fori(0, STEPS_LOOPED // 2) as i:
                for s in (1, 2):
                    step(lambda k, s=s: place(i, s + k), "GEAFB")
            for s in range(last_looped + 1, SEQ + 1):
                step(lambda k, s=s: place(0, s + k), live(s))

        def live(s):
            return "".join(part for part, k in (("G", 3), ("E", 2), ("A", 1), ("F", 0), ("B", -1)) if 0 <= s + k < SEQ)

        def tile_of(u, n):
            return bass.ds((n * 2 + u) * NT, NT)

        LT, L = banks[:, 2:4, :], banks[:, 4:6, :]

        def by_slot(s):
            return banks[:, 2 + s // 2, (s % 2) * T:(s % 2 + 1) * T]

        peak_turned = banks[:, 5, 0:P // 2].bitcast(BF16)
        token_turned = banks[:, 4, 0:P // 2].bitcast(BF16)

        with nc.Block() as block:

            @block.sync
            def _(sp):
                def step(at, parts):
                    if "B" in parts:
                        u, n = at(-1)
                        sp.wait_ge(S["final_ready"][u], n * NT + NT)
                        sp.dma_start(out_rows[bass.ds(n * 2 + u, 1)].squeeze(0), final[u][:, :, :]
                                     ).then_inc(S["final_stored"][u], 16)

                pipeline(sp, step)
                for u in range(U):
                    sp.wait_ge(S["final_stored"][u], 16 + 16 * TURNS)

            @block.tensor
            def _(pe):
                def turn(dst, src, u, done):
                    for j in range(NT):
                        last = pe.transpose(dst[:, j * P:(j + 1) * P], src[u][:, j, 0:D], ident)
                    last.then_inc(S[done][u], 1)

                def step(at, parts):
                    a, f, b = "A" in parts, "F" in parts, "B" in parts
                    ua, na = at(1)
                    uf, nf = at(0)
                    ub, nb = at(-1)

                    def hidden_chunks(chunks):
                        for c in chunks:
                            if c >= 2:
                                pe.wait_ge(S["gelu_ready"][ub], nb * HC + c - 1)
                            pe.matmul(banks[:, 6 + c % 2, :], ffn_w1[:, c * P:(c + 1) * P], slots_cols[ub][:, :],
                                      start=True, stop=True).then_inc(S["hid_ready"][ub], 1)

                    def process(slots):
                        for s in slots:
                            for c in range(HC):
                                last = pe.matmul(banks[:, 6, s * D:(s + 1) * D], act_cols[ub][:, c, s * P:(s + 1) * P],
                                                 ffn_w2[:, c, :], start=(c == 0), stop=(c == HC - 1))
                        return last

                    if a:
                        pe.wait_ge(S["xb_cols_ready"][ua], na + 1)
                        pe.wait_ge(wout_read, na * 2 + ua + 1)
                        for j in range(NT):
                            last = pe.matmul(banks[:, j, 0:3 * D], cols[ua][:, j * P:(j + 1) * P], w_qkv[:, :],
                                             start=True, stop=True)
                        last.then_inc(S["qk_ready"][ua], 1)
                    if f:
                        pe.wait_ge(S["xn_ready"][uf], nf * NT + NT)
                        turn(banks[:, 4, :], xn, uf, "xn_turned")
                    if b:
                        pe.wait_ge(S["slots_cols_ready"][ub], nb + 1)
                        pe.wait_ge(mix_read, nb * 2 + ub + 1)
                        hidden_chunks((0, 1))
                    if f:
                        pe.wait_ge(S["xn_cols_ready"][uf], nf + 1)
                        for s in range(SC):
                            last = pe.matmul(by_slot(s), slot_cols[:, s * P:(s + 1) * P], xn_cols[uf][:, :],
                                             start=(s % 2 == 0), stop=False, skip_group_check=True)
                        last.then_inc(S["by_slot_ready"][uf], 1)
                    if b:
                        hidden_chunks((2, 3))
                    if f:
                        pe.wait_ge(S["slot_peak_ready"][uf], nf + 1)
                        pe.transpose(peak_turned[0:SC, :], slot_peak[uf][:, :], ident_bf[:, :]
                                     ).then_inc(S["slot_peak_turned"][uf], 1)
                    if a:
                        pe.wait_ge(S["q_rows_ready"][ua], na * NT + NT)
                        pe.wait_ge(S["k_rows_ready"][ua], na + 1)
                        pe.wait_ge(S["v_rows_ready"][ua], na + 1)
                        turn(banks[:, 0, :], q_rows, ua, "q_turned")
                        for j in range(NT):
                            last = pe.matmul(banks[:, 1, 0:N129], k_rows[ua][:, j, :], v_rows[ua][:, j, :],
                                             start=(j == 0), stop=(j == NT - 1))
                        last.then_inc(S["kv_sum_ready"][ua], 1)
                    if f:
                        pe.wait_ge(S["slot_shift_ready"][uf], nf + 1)
                        for j in range(NT):
                            last = pe.matmul(banks[:, 4 + j, :], xn_cols[uf][:, j * P:(j + 1) * P], slot_cols[:, :],
                                             start=True, stop=False, skip_group_check=True)
                        last.then_inc(S["by_token_ready"][uf], 1)
                    if b:
                        pe.wait_ge(S["gelu_ready"][ub], nb * HC + HC)
                        process((0, 1))
                    if f:
                        pe.wait_ge(S["token_peak_ready"][uf], nf + 1)
                        for j in range(NT):
                            last = pe.matmul(banks[:, 4 + j, :], ones_bf[0:SC, :],
                                             slot_shift[uf][:, :, :].rearrange("c s p -> c (s p)"),
                                             start=False, stop=True, skip_group_check=True)
                        last.then_inc(S["by_token_shifted"][uf], 1)
                    if a:
                        pe.wait_ge(S["q_cols_ready"][ua], na + 1)
                        pe.wait_ge(S["kv_heads_ready"][ua], na * 2 + 2)
                        for j in range(NT):
                            last = pe.matmul(banks[:, 1, j * (D + HEADS):(j + 1) * (D + HEADS)],
                                             q_cols[ua][:, j * P:(j + 1) * P], kv_heads[ua][:, :],
                                             start=True, stop=True)
                        last.then_inc(S["att_ready"][ua], 1)
                    if b:
                        process((2, 3)).then_inc(S["proc_ready"][ub], 1)
                    if f:
                        pe.wait_ge(S["dispatch_ready"][uf], nf * NT + NT)
                        pe.transpose(token_turned[0:NT, :], token_peak[uf][:, :], ident_bf[:, :]
                                     ).then_inc(S["token_peak_turned"][uf], 1)
                    if a:
                        pe.wait_ge(S["att_rows_ready"][ua], na + 1)
                        turn(banks[:, 0, :], att, ua, "att_turned")
                    if a:
                        pe.wait_ge(S["att_cols_ready"][ua], na + 1)
                        for j in range(NT):
                            last = pe.matmul(banks[:, 1, j * D:(j + 1) * D],
                                             att_cols[ua][:, j * P:(j + 1) * P], w_out[:, :],
                                             start=True, stop=True)
                        last.then_inc(S["wout_ready"][ua], 1)
                    if b:
                        pe.wait_ge(S["processed_ready"][ub], nb + 1)
                        for j in range(NT):
                            for s in range(SC):
                                last = pe.matmul(banks[:, 7, j * N129:(j + 1) * N129],
                                                 combine[ub][:, s, j * P:(j + 1) * P], processed[ub][:, s, :],
                                                 start=(s == 0), stop=(s == SC - 1))
                        last.then_inc(S["mix_ready"][ub], 1)
                    if f:
                        pe.wait_ge(S["token_shift_ready"][uf], nf + 1)
                        shift = token_shift[uf][:, :, :].rearrange("c j p -> c (j p)")
                        for s in range(SC):
                            last = pe.matmul(by_slot(s), ones_bf[0:NT, :], shift,
                                             start=False, stop=True, skip_group_check=True)
                        last.then_inc(S["by_slot_shifted"][uf], 1)
                    if f:
                        for s in range(SC):
                            dst = banks[:, 4 + s // 2, P + (s % 2) * N129:P + (s % 2 + 1) * N129]
                            for j in range(NT):
                                last = pe.matmul(dst, dispatch[uf][:, j, s * P:(s + 1) * P], xn[uf][:, j, :],
                                                 start=(j == 0), stop=(j == NT - 1))
                        last.then_inc(S["slots_ready"][uf], 1)
                    ue, ne = at(2)
                    if "E" in parts:
                        pe.wait_ge(S["xb_ready"][ue], ne * NT + NT)
                        turn(banks[:, 0, :], xb, ue, "xb_turned")
                    if f:
                        pe.wait_ge(S["slots_n_ready"][uf], nf + 1)
                        pe.wait_ge(S["combine_ready"][uf], nf + 1)
                        for s in range(SC):
                            last = pe.transpose(banks[:, 2, s * P:(s + 1) * P], slots_n[uf][:, s, :], ident)
                        last.then_inc(S["slots_turned"][uf], 1)


                pe.wait_ge(slot_rows_ready, SC)
                for s in range(SC):
                    last = pe.transpose(banks[:, 0, s * P:(s + 1) * P], slot_rows[:, s, :], ident)
                last.then_inc(slot_turned, 1)
                pe.wait_ge(slot_cols_ready, 1)
                pe.wait_ge(layer1_w_sem, 16 * 5)
                pipeline(pe, step)

            @block.scalar
            def _(act):
                act.wait_ge(layer1_w_sem, 16 * 5)
                for s in range(SC):
                    act.activation(square_junk[:, :], slot_rows[:, s, :], ACT.Square,
                                   accum_out=slot_sq[:, s, 0:1]).then_inc(slot_sq_ready, 1)
                    act.wait_ge(slot_sq_ready, s + 1)
                act.wait_ge(slot_turned, 1)
                act.activation(slot_cols[:, :], banks[:, 0, :], ACT.Copy).then_inc(slot_cols_ready, 1)

                def step(at, parts):
                    a, f, b = "A" in parts, "F" in parts, "B" in parts
                    ua, na = at(1)
                    uf, nf = at(0)
                    ub, nb = at(-1)

                    def gelus(chunks):
                        for c in chunks:
                            act.wait_ge(S["hid_ready"][ub], nb * HC + c + 1)
                            act.activation(act_cols[ub][:, c, :], banks[:, 6 + c % 2, :], ACT.Gelu
                                           ).then_inc(S["gelu_ready"][ub], 1)

                    if a:
                        act.wait_ge(S["qk_ready"][ua], na + 1)
                        act.activation(v_rows[ua][:, :, 0:D], banks[:, 0:2, 2 * D:3 * D], ACT.Copy
                                       ).then_inc(S["v_rows_ready"][ua], 1)
                        act.activation(qk_squares[ua][:, :, :], banks[:, 0:2, 0:2 * D], ACT.Square
                                       ).then_inc(S["qk_squared"][ua], 1)
                    if f:
                        act.wait_ge(S["xn_turned"][uf], nf + 1)
                        act.activation(xn_cols[uf][:, :], banks[:, 4, 0:T], ACT.Copy).then_inc(S["xn_cols_ready"][uf], 1)
                    if b:
                        gelus((0, 1))
                    if b:
                        gelus((2, 3))
                    if a:
                        act.wait_ge(S["q_turned"][ua], na + 1)
                        act.activation(q_cols[ua][:, :], banks[:, 0, 0:T], ACT.Relu, scale=vec(V_QN)
                                       ).then_inc(S["q_cols_ready"][ua], 1)
                    if f:
                        act.wait_ge(S["by_token_shifted"][uf], nf + 1)
                        for j in range(NT):
                            act.activation(dispatch[uf][:, j, :], banks[:, 4 + j, :], ACT.Exp
                                           ).then_inc(S["dispatch_ready"][uf], 1)
                    if a:
                        act.wait_ge(S["att_turned"][ua], na + 1)
                        act.activation(att_cols[ua][:, :], banks[:, 0, 0:T], ACT.Copy).then_inc(S["att_cols_ready"][ua], 1)
                    if f:
                        act.wait_ge(S["by_slot_shifted"][uf], nf + 1)
                        act.activation(combine[uf][:, :, :].rearrange("p (b c) t -> p b (c t)", b=2), LT, ACT.Exp
                                       ).then_inc(S["combine_ready"][uf], 1)
                    if "E" in parts:
                        ue, ne = at(2)
                        act.wait_ge(S["xb_turned"][ue], ne + 1)
                        act.activation(cols[ue][:, :], banks[:, 0, 0:T], ACT.Copy).then_inc(S["xb_cols_ready"][ue], 1)
                    if a:
                        act.wait_ge(S["xc_ready"][ua], na * NT + NT)
                        for j in range(NT):
                            act.activation(junk[ua][:, :], xc[ua][:, j, :], ACT.Square,
                                           accum_out=xc_sq[ua][:, j:j + 1]).then_inc(S["xc_sq_ready"][ua], 1)
                            act.wait_ge(S["xc_sq_ready"][ua], na * NT + j + 1)
                    if f:
                        act.wait_ge(S["slots_turned"][uf], nf + 1)
                        act.activation(slots_cols[uf][:, :], banks[:, 2, :], ACT.Copy
                                       ).then_inc(S["slots_cols_ready"][uf], 1)

                pipeline(act, step)

            @block.gpsimd
            def _(pool):
                for u in range(U):
                    pool.memset(v_rows[u][:, :, D:D + 1], 1.0).then_inc(ones_set, 1)
                    pool.memset(xn[u][:, :, D:D + 1], 1.0).then_inc(ones_set, 1)
                    pool.memset(processed[u][:, :, D:D + 1], 1.0).then_inc(ones_set, 1)

                def slot_rms():
                    c = Chain(pool, pool_slots)
                    pool.wait_ge(slot_sq_ready, SC)
                    c.step(pool.tensor_scalar(slot_sq[:, :, 1], slot_sq[:, :, 0], 1e-24, 1.0 / D, ALU.max, ALU.mult))
                    c.wait()
                    pool.tensor_tensor(slot_sq[:, :, 0], slot_sq[:, :, 1], neg_half[:, 0:SC], ALU.pow
                                       ).then_inc(slot_rms_ready, 1)

                def gather(u, n):
                    settle(pool, S["idx_ready"][u], n + 1, pool_passed)
                    for j in range(NT):
                        pool.indirect_dma_start(y_got[u][:, j, :], None, sorted_y,
                                                bass.IndirectOffsetOnAxis(ap=y_idx[u][:, j:j + 1], axis=0)
                                                ).then_inc(S["y_gathered"][u], 16)

                def step(at, parts):
                    a, b = "A" in parts, "B" in parts
                    ua, na = at(1)

                    def to_rstd(u, var_sem, value, mv, dst, done, c):
                        pool.wait_ge(var_sem, value)
                        c.step(pool.tensor_tensor(dst[u][:, :], mv[u][:, :, 1], eps[:, EPS_LN, :], ALU.add))
                        c.wait()
                        pool.tensor_tensor(dst[u][:, :], dst[u][:, :], neg_half[:, 0:NT], ALU.pow).then_inc(done, 1)

                    if a:
                        c = Chain(pool, pool_a[ua], na, 3)
                        settle(pool, S["qk_sq_ready"][ua], na + 1, pool_passed)
                        c.step(pool.tensor_scalar(qk_rms[ua][:, :], qk_sq[ua][:, :], 1.0 / D, 1e-6,
                                                  ALU.mult, ALU.add))
                        c.wait()
                        pool.tensor_tensor(qk_rms[ua][:, :], qk_rms[ua][:, :], neg_half[:, 0:2 * NT], ALU.pow
                                           ).then_inc(S["qk_rms_ready"][ua], 1)
                    if "G" in parts:
                        gather(*at(3))
                    if parts == "G":
                        slot_rms()
                    if "F" in parts:
                        u, n = at(0)
                        pool.wait_ge(S["xc_ready"][u], n * NT + NT)
                        pool.wait_ge(S["mix_added"][u], n + 1)
                        pool.tensor_tensor(x_kept[u][:, :, :], xc[u][:, :, :], zeros[:, :].unsqueeze(1).to_broadcast([P, NT, D]),
                                           ALU.add).then_inc(S["kept"][u], 1)
                    if a:
                        pool.wait_ge(S["xb_ready"][ua], na * NT + NT)
                        pool.tensor_tensor(xb_bias[ua][:, :, :], xb[ua][:, :, :],
                                           rows[:, R_BOUT, :].unsqueeze(1).to_broadcast([P, NT, D]), ALU.add
                                           ).then_inc(S["xb_bias_ready"][ua], 1)
                    if "E" in parts:
                        u, n = at(2)
                        to_rstd(u, S["var_e"][u], n * NT + NT, mean_var_e, rstd_e, S["rstd_e"][u],
                                Chain(pool, pool_e[u], n, 1))
                    if a:
                        to_rstd(ua, S["var_a"][ua], na * NT + NT, mean_var, rstd, S["rstd_a"][ua], c)
                        settle(pool, S["xc_sq_ready"][ua], na * NT + NT, pool_passed)
                        c.step(pool.tensor_scalar(xc_rms[ua][:, :], xc_sq[ua][:, :], 1e-24, 1.0 / D,
                                                  ALU.max, ALU.mult))
                        c.wait()
                        pool.tensor_tensor(xc_rms[ua][:, :], xc_rms[ua][:, :], neg_half[:, 0:NT], ALU.pow
                                           ).then_inc(S["xc_rms_ready"][ua], 1)
                        c.close()
                    if b:
                        u, n = at(-1)
                        to_rstd(u, S["var_b"][u], n * NT + NT, mean_var_b, rstd_b, S["rstd_b"][u],
                                Chain(pool, pool_b[u], n, 1))

                for u in range(U):
                    pool.wait_ge(y_stored[u], 16 + 16 * (XTILES // U))
                pipeline(pool, step)

            @block.vector
            def _(dve):
                p = Chain(dve, vec_slots)
                p.step(dve.tensor_copy(ident_bf[:, :], ident))
                dve.wait_ge(ones_set, 3 * U)
                p.wait()
                dve.sem_inc(mix_read, 1)
                dve.sem_inc(wout_read, 1)
                for u in range(U):
                    dve.sem_inc(S["final_stored"][u], 16)
                    dve.sem_inc(S["mix_added"][u], 1)

                def stats_of(c, src, moments, mean_var, done):
                    for j in range(NT):
                        c.step(dve.bn_stats(moments[:, j, :], src[:, j, :]))
                    settle(dve, c.sem, c.turn * c.per_turn + c.n, vec_passed)
                    for j in range(NT):
                        dve.bn_aggr(mean_var[:, j, :], moments[:, j, :]).then_inc(done, 1)

                def normalised(dst, src, mean_var, rstd, done):
                    for j in range(NT):
                        dve.tensor_scalar(dst[:, j, :], src[:, j, :], mean_var[:, j, 0:1],
                                          rstd[:, j:j + 1], ALU.subtract, ALU.mult).then_inc(done, 1)

                def indices(u, n):
                    dve.tensor_copy(y_idx[u][:, :], slot_of[:, tile_of(u, n)]).then_inc(S["idx_ready"][u], 1)

                def step(at, parts):
                    a, f, b = "A" in parts, "F" in parts, "B" in parts
                    ua, na = at(1)
                    uf, nf = at(0)
                    ub, nb = at(-1)
                    ca = Chain(dve, vec_a[ua], na, 7)
                    cf = Chain(dve, vec_f[uf], nf, 1)
                    cb = Chain(dve, vec_b[ub], nb, 5)
                    e = "E" in parts
                    ue, ne = at(2)
                    ce = Chain(dve, vec_e[ue], ne, 3)
                    if "G" in parts:
                        indices(*at(3))
                    if parts == "G":
                        dve.wait_ge(slot_rms_ready, 1)
                        for s in range(SC):
                            dve.scalar_tensor_tensor(slot_rows[:, s, :], slot_rows[:, s, :], slot_sq[:, s, 0:1],
                                                     rows[:, R_GS, :], ALU.mult, ALU.mult
                                                     ).then_inc(slot_rows_ready, 1)
                    if a:
                        dve.wait_ge(S["qk_squared"][ua], na + 1)
                        dve.tensor_reduce(qk_sq[ua][:, :].rearrange("p (m j) -> p j m", j=NT),
                                          qk_squares[ua][:, :, :].rearrange("p j (m d) -> p j m d", d=D),
                                          AX, ALU.add).then_inc(S["qk_sq_ready"][ua], 1)
                    if a:
                        dve.wait_ge(S["qk_rms_ready"][ua], na + 1)
                        for j in range(NT):
                            dve.tensor_scalar(q_rows[ua][:, j, :], banks[:, j, 0:D], qk_rms[ua][:, j:j + 1],
                                              None, ALU.mult).then_inc(S["q_rows_ready"][ua], 1)
                        for j in range(NT):
                            ca.step(dve.scalar_tensor_tensor(k_rows[ua][:, j, :], banks[:, j, D:2 * D],
                                                             qk_rms[ua][:, NT + j:NT + j + 1], rows[:, R_KN, :],
                                                             ALU.mult, ALU.mult))
                        ca.wait()
                        dve.tensor_scalar(k_rows[ua][:, :, :], k_rows[ua][:, :, :], 0.0, None, ALU.max
                                          ).then_inc(S["k_rows_ready"][ua], 1)
                    if f:
                        dve.wait_ge(S["by_slot_ready"][uf], nf + 1)
                        dve.tensor_reduce(slot_peak[uf][:, :], LT.rearrange("p b (c t) -> p (b c) t", t=T),
                                          AX, ALU.max, negate=True).then_inc(S["slot_peak_ready"][uf], 1)
                        dve.wait_ge(S["slot_peak_turned"][uf], nf + 1)
                        dve.tensor_tensor(slot_shift[uf][:, :, :],
                                          consts[0:SC, C_DIAG:C_DIAG + SC].unsqueeze(2).to_broadcast([SC, SC, P]),
                                          peak_turned[0:SC, :].unsqueeze(1).to_broadcast([SC, SC, P]),
                                          ALU.mult).then_inc(S["slot_shift_ready"][uf], 1)
                    if e:
                        dve.wait_ge(S["y_gathered"][ue], ne * 16 * NT + 16 * NT)
                        ce.step(dve.tensor_tensor(summed_e[ue][:, :, :], xa[:, tile_of(ue, ne), :],
                                                  y_got[ue][:, :, :], ALU.add))
                        ce.wait()
                        stats_of(ce, summed_e[ue], moments_e[ue], mean_var_e[ue], S["var_e"][ue])
                        ce.close()
                    if f:
                        dve.wait_ge(S["by_token_ready"][uf], nf + 1)
                        dve.tensor_reduce(token_peak[uf][:, :], L, AX, ALU.max, negate=True
                                          ).then_inc(S["token_peak_ready"][uf], 1)
                    if a:
                        dve.wait_ge(S["kv_sum_ready"][ua], na + 1)
                        dve.tensor_tensor(kv_heads[ua][:, 0:D], consts[:, C_BLOCK:C_BLOCK + D], banks[:, 1, 0:D],
                                          ALU.mult).then_inc(S["kv_heads_ready"][ua], 1)
                        dve.tensor_scalar(kv_heads[ua][:, D:D + HEADS], consts[:, C_HEADS:C_HEADS + HEADS],
                                          banks[:, 1, D:D + 1], None, ALU.mult).then_inc(S["kv_heads_ready"][ua], 1)
                        o = banks[:, 1, 0:NT * (D + HEADS)].rearrange("p (j n) -> p j n", j=NT)
                        dve.wait_ge(S["att_ready"][ua], na + 1)
                        ca.step(dve.tensor_scalar(norm_inv[ua][:, :, :], o[:, :, D:D + HEADS], 1e-6, None, ALU.add))
                        ca.wait()
                        ca.step(dve.reciprocal(norm_inv[ua][:, :, :], norm_inv[ua][:, :, :]))
                        ca.wait()
                        dve.tensor_tensor(att[ua][:, :, :].rearrange("p j (h d) -> p j h d", d=DH),
                                          o[:, :, 0:D].rearrange("p j (h d) -> p j h d", d=DH),
                                          norm_inv[ua][:, :, :].unsqueeze(3).to_broadcast([P, NT, HEADS, DH]),
                                          ALU.mult).then_inc(S["att_rows_ready"][ua], 1)
                    if b:
                        dve.wait_ge(S["proc_ready"][ub], nb + 1)
                        dve.tensor_copy(processed[ub][:, :, 0:D], banks[:, 6, :].rearrange("p (s d) -> p s d", d=D)
                                        ).then_inc(S["processed_ready"][ub], 1)
                    if e:
                        dve.wait_ge(S["rstd_e"][ue], ne + 1)
                        normalised(xb[ue], summed_e[ue], mean_var_e[ue], rstd_e[ue], S["xb_ready"][ue])
                    if f:
                        dve.wait_ge(S["token_peak_turned"][uf], nf + 1)
                        dve.tensor_tensor(token_shift[uf][:, :, :],
                                          consts[0:NT, C_DIAG:C_DIAG + NT].unsqueeze(2).to_broadcast([NT, NT, P]),
                                          token_turned[0:NT, :].unsqueeze(1).to_broadcast([NT, NT, P]),
                                          ALU.mult).then_inc(S["token_shift_ready"][uf], 1)
                    if a:
                        dve.wait_ge(S["wout_ready"][ua], na + 1)
                        dve.wait_ge(S["xb_bias_ready"][ua], na + 1)
                        ca.step(dve.tensor_tensor(summed[ua][:, :, :], xb_bias[ua][:, :, :],
                                                  banks[:, 1, 0:T].rearrange("p (j d) -> p j d", d=D), ALU.add))
                        ca.wait()
                        dve.sem_inc(wout_read, 1)
                        stats_of(ca, summed[ua], moments[ua], mean_var[ua], S["var_a"][ua])
                    if b:
                        o = banks[:, 7, 0:NT * N129].rearrange("p (j n) -> p j n", n=N129)
                        dve.wait_ge(S["mix_ready"][ub], nb + 1)
                        dve.wait_ge(S["kept"][ub], nb + 1)
                        cb.step(dve.reciprocal(out_inv[ub][:, :], o[:, :, D]))
                        cb.wait()
                        for j in range(NT):
                            last = dve.scalar_tensor_tensor(summed_b[ub][:, j, :], o[:, j, 0:D], out_inv[ub][:, j:j + 1],
                                                            x_kept[ub][:, j, :], ALU.mult, ALU.add)
                            cb.step(last)
                        cb.wait()
                        dve.sem_inc(mix_read, 1)
                        dve.sem_inc(S["mix_added"][ub], 1)
                    if a:
                        dve.wait_ge(S["rstd_a"][ua], na + 1)
                        normalised(xc[ua], summed[ua], mean_var[ua], rstd[ua], S["xc_ready"][ua])
                    if f:
                        s = banks[:, 4:6, P:P + 2 * N129].rearrange("p b (c n) -> p b c n", n=N129)
                        inv = slot_inv[uf][:, :].rearrange("p (b c) -> p b c", b=2)
                        dve.wait_ge(S["slots_ready"][uf], nf + 1)
                        cf.step(dve.reciprocal(inv, s[:, :, :, D]))
                        cf.wait()
                        dve.tensor_tensor(slots_n[uf][:, :, :].rearrange("p (b c) d -> p b c d", b=2),
                                          s[:, :, :, 0:D], inv.unsqueeze(3).to_broadcast([P, 2, 2, D]), ALU.mult
                                          ).then_inc(S["slots_n_ready"][uf], 1)
                        cf.close()
                    if b:
                        stats_of(cb, summed_b[ub], moments_b[ub], mean_var_b[ub], S["var_b"][ub])
                        cb.close()
                    if a:
                        dve.wait_ge(S["xc_rms_ready"][ua], na + 1)
                        for j in range(NT):
                            dve.scalar_tensor_tensor(xn[ua][:, j, 0:D], xc[ua][:, j, :], xc_rms[ua][:, j:j + 1],
                                                     rows[:, R_GX, :], ALU.mult, ALU.mult
                                                     ).then_inc(S["xn_ready"][ua], 1)
                        ca.close()

                    if b:
                        dve.wait_ge(S["final_stored"][ub], nb * 16 + 16)
                        dve.wait_ge(S["rstd_b"][ub], nb + 1)
                        normalised(final[ub], summed_b[ub], mean_var_b[ub], rstd_b[ub], S["final_ready"][ub])

                pipeline(dve, step)

        l1.close()


_COLUMNS = ["L0_attn_ln1_g", "L0_attn_ln1_b", "L0_attn_ln2_g", "L0_attn_ln2_b", "L0_attn_tm_mix_k",
            "L0_attn_tm_mix_v", "L0_attn_tm_mix_r", "L0_attn_cm_mix_k", "L0_attn_cm_mix_r",
            "L0_attn_time_decay", "L0_attn_time_first", "L1_attn_qn_w"]
_ROWS = ["L1_attn_kn_w", "L1_attn_b_out", "L1_ffn_gamma_x", "L1_ffn_gamma_slot"]
_WEIGHTS = {"tm_Wk": "L0_attn_tm_Wk", "tm_Wv": "L0_attn_tm_Wv", "tm_Wr": "L0_attn_tm_Wr", "Wo": "L0_attn_Wo",
            "cm_Wk": "L0_attn_cm_Wk", "cm_Wv": "L0_attn_cm_Wv", "cm_Wr": "L0_attn_cm_Wr",
            "router_w": "L0_ffn_router_w", "router_b": "L0_ffn_router_b", "w1": "L0_ffn_w1", "b1": "L0_ffn_b1",
            "w2": "L0_ffn_w2", "b2": "L0_ffn_b2", "W_qkv": "L1_attn_W_qkv", "W_out": "L1_attn_W_out",
            "slots": "L1_ffn_slot_embeds", "ffn_w1": "L1_ffn_w1", "ffn_w2": "L1_ffn_w2"}


def _constants(np, heads=16, experts=8, tiles=32):
    c = np.zeros((P, C_END), np.float32)
    p = np.arange(P)
    c[:, C_IDENT:C_IDENT + P] = np.eye(P)
    c[:, C_UPPER:C_UPPER + P] = p[:, None] < p[None, :]
    c[:, C_BLOCK:C_BLOCK + P] = p[:, None] // (P // heads) == p[None, :] // (P // heads)
    c[:, C_HEADS:C_HEADS + heads] = p[:, None] // (P // heads) == np.arange(heads)
    c[:, C_FIRST:C_FIRST + experts] = experts - np.arange(experts)
    c[:, C_TILE:C_TILE + 40] = np.arange(40)
    c[:, C_COUNT:C_COUNT + tiles] = P * np.arange(tiles)
    c[:, C_RESET:C_RESET + experts * tiles] = np.arange(experts * tiles) % tiles != 0
    c[0:16, C_DIAG:C_DIAG + 16] = np.eye(16)
    return c


def kernel(**inputs):
    import numpy as _np
    import concourse.bacc as _bacc
    from concourse import mybir as _mybir
    from concourse.bass_utils import run_bass_kernel_spmd as _run

    nc = _bacc.Bacc("TRN2", target_bir_lowering=False, num_devices=1)
    arrays = {}

    def give(name, a):
        a = _np.ascontiguousarray(a)
        arrays[name] = a
        return nc.dram_tensor(name, a.shape, _mybir.dt.from_np(a.dtype), kind="ExternalInput").ap()

    x = give("x_dram", inputs["L0_attn_inputs"])
    vecs = give("vecs_dram", _np.stack([_np.asarray(inputs[n]) for n in _COLUMNS], axis=1))
    rows = give("rows_dram", _np.stack([_np.asarray(inputs[n]) for n in _ROWS], axis=0))
    consts = give("consts_dram", _constants(_np))
    w = {}
    for short, name in _WEIGHTS.items():
        a = _np.asarray(inputs[name])
        w[short] = give(short + "_dram", a.reshape(-1, a.shape[-1]) if short == "slots" else a)
    out = nc.dram_tensor("out_dram", inputs["L0_attn_inputs"].shape, F32, kind="ExternalOutput").ap()
    two_layer_kernel(nc, x, vecs, rows, consts, w, out)
    r = _run(nc, [arrays], core_ids=[0])
    return r.results[0]["out_dram"]
```
